# Optimizing a Trainium2 kernel written in Bass

```python
import numpy as np
import jax
import jax.numpy as jnp

def _softmax(x, axis=-1):
    return jax.nn.softmax(x, axis=axis)

def _gelu(x):
    return jax.nn.gelu(x, approximate=True)

def _silu(x):
    return jax.nn.silu(x)

def _sigmoid(x):
    return jax.nn.sigmoid(x)

def _layernorm(x, axis=-1, eps=1e-05):
    m = jnp.mean(x, axis=axis, keepdims=True)
    v = jnp.var(x, axis=axis, keepdims=True)
    return (x - m) / jnp.sqrt(v + eps)

def _scatter_add(tgt, idx, src, axis=0):
    return tgt.at[idx].add(src)

def _segment_sum(src, seg, n):
    return jax.ops.segment_sum(src, seg, n)
kernel_name = 'mk_cond_seq_d2_seqx_r8_58cd03'

def setup_inputs(seed: int=0):
    np.random.seed(seed)
    _w = jnp.asarray

    def _rec_inputs():
        import jax
        import jax.numpy as jnp
        _rk = jax.random.key(seed)
        x = -0.0002928 + 1 * jax.random.normal(jax.random.fold_in(_rk, 1), (2, 512, 128), jnp.float32)
        _lenS = 512 - jax.random.randint(jax.random.fold_in(_rk, 7), (2,), 0, max(1, 512 // 4) + 1, jnp.int32)
        _lenS2 = 512 - jax.random.randint(jax.random.fold_in(_rk, 8), (2,), 0, max(1, 512 // 4) + 1, jnp.int32)
        cond_1024 = 0.0061147 + 1.02565 * jax.random.normal(jax.random.fold_in(_rk, 11), (2, 128), jnp.float32)
        return (x, cond_1024)
    x, cond_1024 = _rec_inputs()

    def _L0_cond_setup():
        import jax, jax.numpy as jnp
        import numpy as np
        B, S, D, H, F = (4, 128, 128, 16, 512)
        EPS = 1e-06
        NEG = -1000000000.0

        def _mat(k, m, n):
            return jax.random.normal(k, (m, n), dtype=jnp.float32) / np.sqrt(m)

        def _ln(x, g, b):
            mu = jnp.mean(x, -1, keepdims=True)
            var = jnp.var(x, -1, keepdims=True)
            return (x - mu) * jax.lax.rsqrt(var + EPS) * g + b

        def _mha(x, wq, wk, wv, wo, bias):
            b, s, dm = x.shape
            dh = dm // H
            q = (x @ wq).reshape(b, s, H, dh)
            k = (x @ wk).reshape(b, s, H, dh)
            v = (x @ wv).reshape(b, s, H, dh)
            scores = jnp.einsum('bqhd,bkhd->bhqk', q, k) / np.sqrt(dh) + bias
            a = jax.nn.softmax(scores, axis=-1)
            o = jnp.einsum('bhqk,bkhd->bqhd', a, v).reshape(b, s, dm)
            return o @ wo

        def _biases(s):
            idx = jnp.arange(s)
            dist = jnp.abs(idx[:, None] - idx[None, :]).astype(jnp.float32)
            grid_bias = -dist
            reg_bias = jnp.where(dist <= 1, 0.0, NEG)
            ent_bias = jnp.where(idx[:, None] // 2 == idx[None, :] // 2, 0.0, NEG)
            sem_bias = jnp.zeros((s, s), jnp.float32)
            return (grid_bias, reg_bias, ent_bias, sem_bias)
        key = jax.random.key(seed)
        ks = jax.random.split(key, 32)
        d = {'x': jax.random.normal(ks[0], (B, S, D), dtype=jnp.float32), 't_emb': jax.random.normal(ks[1], (B, D), dtype=jnp.float32), 'ln1_g': jnp.ones((D,), jnp.float32), 'ln1_b': jnp.zeros((D,), jnp.float32), 'ln2_g': jnp.ones((D,), jnp.float32), 'ln2_b': jnp.zeros((D,), jnp.float32), 'ada_w': _mat(ks[2], D, 6 * D), 'ada_b': jnp.zeros((6 * D,), jnp.float32), 'fus_wg': _mat(ks[3], 4 * D, 4), 'fus_bg': jnp.zeros((4,), jnp.float32), 'fus_wo': _mat(ks[4], D, D), 'ffn_w1': _mat(ks[5], D, F), 'ffn_w2': _mat(ks[6], F, D), 'ffn_w3': _mat(ks[7], D, F)}
        i = 8
        for p in ('grid', 'reg', 'ent', 'sem'):
            for w in ('wq', 'wk', 'wv', 'wo'):
                d[f'{p}_{w}'] = _mat(ks[i], D, D)
                i += 1
        return d
    _L0_cond_all = _L0_cond_setup()
    _L0_cond_in = {k: v for k, v in _L0_cond_all.items() if k in ('ln1_g', 'ln1_b', 'ln2_g', 'ln2_b', 'ada_w', 'ada_b', 'grid_wq', 'grid_wk', 'grid_wv', 'grid_wo', 'reg_wq', 'reg_wk', 'reg_wv', 'reg_wo', 'ent_wq', 'ent_wk', 'ent_wv', 'ent_wo', 'sem_wq', 'sem_wk', 'sem_wv', 'sem_wo', 'fus_wg', 'fus_bg', 'fus_wo', 'ffn_w1', 'ffn_w2', 'ffn_w3')}
    del _L0_cond_all

    def _L1_cond_setup():
        import jax, jax.numpy as jnp
        import numpy as np
        H = 16
        EPS = 1e-05

        def layer_norm(x, g, b):
            mu = jnp.mean(x, axis=-1, keepdims=True)
            var = jnp.var(x, axis=-1, keepdims=True)
            return (x - mu) * jax.lax.rsqrt(var + EPS) * g + b
        key = jax.random.key(seed)
        ks = jax.random.split(key, 8)
        B, T, D, TE = (4, 512, 128, 128)
        s = 0.02
        return {'x': jax.random.normal(ks[0], (B, T, D), jnp.float32), 'emb': jax.random.normal(ks[1], (B, 1, TE), jnp.float32), 'gate_msa': jax.random.normal(ks[2], (B, 1, D), jnp.float32), 'norm_g': jnp.ones((D,), jnp.float32), 'norm_b': jnp.zeros((D,), jnp.float32), 'Wq': jax.random.normal(ks[3], (D, D), jnp.float32) * s, 'bq': jnp.zeros((D,), jnp.float32), 'Wk': jax.random.normal(ks[4], (D, D), jnp.float32) * s, 'bk': jnp.zeros((D,), jnp.float32), 'Wv': jax.random.normal(ks[5], (D, D), jnp.float32) * s, 'bv': jnp.zeros((D,), jnp.float32), 'emb_W': jax.random.normal(ks[6], (TE, 2 * D), jnp.float32) * s, 'emb_b': jnp.zeros((2 * D,), jnp.float32), 'sn_g': jnp.ones((D,), jnp.float32), 'sn_b': jnp.zeros((D,), jnp.float32), 'out_W': jax.random.normal(ks[7], (D, D), jnp.float32) * s, 'out_b': jnp.zeros((D,), jnp.float32)}
    _L1_cond_all = _L1_cond_setup()
    _L1_cond_in = {k: v for k, v in _L1_cond_all.items() if k in ('norm_g', 'norm_b', 'Wq', 'bq', 'Wk', 'bk', 'Wv', 'bv', 'emb_W', 'emb_b', 'sn_g', 'sn_b', 'out_W', 'out_b')}
    del _L1_cond_all
    return {'x': x, 'cond_1024': cond_1024, 'L0_cond_ln1_g': _L0_cond_in['ln1_g'], 'L0_cond_ln1_b': _L0_cond_in['ln1_b'], 'L0_cond_ln2_g': _L0_cond_in['ln2_g'], 'L0_cond_ln2_b': _L0_cond_in['ln2_b'], 'L0_cond_ada_w': _L0_cond_in['ada_w'], 'L0_cond_ada_b': _L0_cond_in['ada_b'], 'L0_cond_grid_wq': _L0_cond_in['grid_wq'], 'L0_cond_grid_wk': _L0_cond_in['grid_wk'], 'L0_cond_grid_wv': _L0_cond_in['grid_wv'], 'L0_cond_grid_wo': _L0_cond_in['grid_wo'], 'L0_cond_reg_wq': _L0_cond_in['reg_wq'], 'L0_cond_reg_wk': _L0_cond_in['reg_wk'], 'L0_cond_reg_wv': _L0_cond_in['reg_wv'], 'L0_cond_reg_wo': _L0_cond_in['reg_wo'], 'L0_cond_ent_wq': _L0_cond_in['ent_wq'], 'L0_cond_ent_wk': _L0_cond_in['ent_wk'], 'L0_cond_ent_wv': _L0_cond_in['ent_wv'], 'L0_cond_ent_wo': _L0_cond_in['ent_wo'], 'L0_cond_sem_wq': _L0_cond_in['sem_wq'], 'L0_cond_sem_wk': _L0_cond_in['sem_wk'], 'L0_cond_sem_wv': _L0_cond_in['sem_wv'], 'L0_cond_sem_wo': _L0_cond_in['sem_wo'], 'L0_cond_fus_wg': _L0_cond_in['fus_wg'], 'L0_cond_fus_bg': _L0_cond_in['fus_bg'], 'L0_cond_fus_wo': _L0_cond_in['fus_wo'], 'L0_cond_ffn_w1': _L0_cond_in['ffn_w1'], 'L0_cond_ffn_w2': _L0_cond_in['ffn_w2'], 'L0_cond_ffn_w3': _L0_cond_in['ffn_w3'], 'L1_cond_norm_g': _L1_cond_in['norm_g'], 'L1_cond_norm_b': _L1_cond_in['norm_b'], 'L1_cond_Wq': _L1_cond_in['Wq'], 'L1_cond_bq': _L1_cond_in['bq'], 'L1_cond_Wk': _L1_cond_in['Wk'], 'L1_cond_bk': _L1_cond_in['bk'], 'L1_cond_Wv': _L1_cond_in['Wv'], 'L1_cond_bv': _L1_cond_in['bv'], 'L1_cond_emb_W': _L1_cond_in['emb_W'], 'L1_cond_emb_b': _L1_cond_in['emb_b'], 'L1_cond_sn_g': _L1_cond_in['sn_g'], 'L1_cond_sn_b': _L1_cond_in['sn_b'], 'L1_cond_out_W': _L1_cond_in['out_W'], 'L1_cond_out_b': _L1_cond_in['out_b']}

def reference(x, cond_1024, L0_cond_ln1_g, L0_cond_ln1_b, L0_cond_ln2_g, L0_cond_ln2_b, L0_cond_ada_w, L0_cond_ada_b, L0_cond_grid_wq, L0_cond_grid_wk, L0_cond_grid_wv, L0_cond_grid_wo, L0_cond_reg_wq, L0_cond_reg_wk, L0_cond_reg_wv, L0_cond_reg_wo, L0_cond_ent_wq, L0_cond_ent_wk, L0_cond_ent_wv, L0_cond_ent_wo, L0_cond_sem_wq, L0_cond_sem_wk, L0_cond_sem_wv, L0_cond_sem_wo, L0_cond_fus_wg, L0_cond_fus_bg, L0_cond_fus_wo, L0_cond_ffn_w1, L0_cond_ffn_w2, L0_cond_ffn_w3, L1_cond_norm_g, L1_cond_norm_b, L1_cond_Wq, L1_cond_bq, L1_cond_Wk, L1_cond_bk, L1_cond_Wv, L1_cond_bv, L1_cond_emb_W, L1_cond_emb_b, L1_cond_sn_g, L1_cond_sn_b, L1_cond_out_W, L1_cond_out_b):
    import jax
    import jax.numpy as jnp

    def _L0_cond_ref(x, t_emb, ln1_g, ln1_b, ln2_g, ln2_b, ada_w, ada_b, grid_wq, grid_wk, grid_wv, grid_wo, reg_wq, reg_wk, reg_wv, reg_wo, ent_wq, ent_wk, ent_wv, ent_wo, sem_wq, sem_wk, sem_wv, sem_wo, fus_wg, fus_bg, fus_wo, ffn_w1, ffn_w2, ffn_w3):
        import jax, jax.numpy as jnp
        import numpy as np
        B, S, D, H, F = (4, 128, 128, 16, 512)
        EPS = 1e-06
        NEG = -1000000000.0

        def _mat(k, m, n):
            return jax.random.normal(k, (m, n), dtype=jnp.float32) / np.sqrt(m)

        def _ln(x, g, b):
            mu = jnp.mean(x, -1, keepdims=True)
            var = jnp.var(x, -1, keepdims=True)
            return (x - mu) * jax.lax.rsqrt(var + EPS) * g + b

        def _mha(x, wq, wk, wv, wo, bias):
            b, s, dm = x.shape
            dh = dm // H
            q = (x @ wq).reshape(b, s, H, dh)
            k = (x @ wk).reshape(b, s, H, dh)
            v = (x @ wv).reshape(b, s, H, dh)
            scores = jnp.einsum('bqhd,bkhd->bhqk', q, k) / np.sqrt(dh) + bias
            a = jax.nn.softmax(scores, axis=-1)
            o = jnp.einsum('bhqk,bkhd->bqhd', a, v).reshape(b, s, dm)
            return o @ wo

        def _biases(s):
            idx = jnp.arange(s)
            dist = jnp.abs(idx[:, None] - idx[None, :]).astype(jnp.float32)
            grid_bias = -dist
            reg_bias = jnp.where(dist <= 1, 0.0, NEG)
            ent_bias = jnp.where(idx[:, None] // 2 == idx[None, :] // 2, 0.0, NEG)
            sem_bias = jnp.zeros((s, s), jnp.float32)
            return (grid_bias, reg_bias, ent_bias, sem_bias)
        s = x.shape[1]
        gb, rb, eb, sb = _biases(s)
        ada = jax.nn.silu(t_emb) @ ada_w + ada_b
        sh_m, sc_m, g_m, sh_f, sc_f, g_f = jnp.split(ada, 6, axis=1)
        nx = _ln(x, ln1_g, ln1_b) * (1 + sc_m[:, None, :]) + sh_m[:, None, :]
        o1 = _mha(nx, grid_wq, grid_wk, grid_wv, grid_wo, gb)
        o2 = _mha(nx, reg_wq, reg_wk, reg_wv, reg_wo, rb)
        o3 = _mha(nx, ent_wq, ent_wk, ent_wv, ent_wo, eb)
        o4 = _mha(nx, sem_wq, sem_wk, sem_wv, sem_wo, sb)
        gate = jax.nn.softmax(jnp.concatenate([o1, o2, o3, o4], axis=-1) @ fus_wg + fus_bg, axis=-1)
        fused = (gate[..., 0:1] * o1 + gate[..., 1:2] * o2 + gate[..., 2:3] * o3 + gate[..., 3:4] * o4) @ fus_wo
        x = x + g_m[:, None, :] * fused
        nx2 = _ln(x, ln2_g, ln2_b) * (1 + sc_f[:, None, :]) + sh_f[:, None, :]
        ffn = jax.nn.silu(nx2 @ ffn_w1) * (nx2 @ ffn_w3) @ ffn_w2
        return x + g_f[:, None, :] * ffn

    def _L1_cond_ref(x, emb, gate_msa, norm_g, norm_b, Wq, bq, Wk, bk, Wv, bv, emb_W, emb_b, sn_g, sn_b, out_W, out_b):
        import jax, jax.numpy as jnp
        import numpy as np
        H = 16
        EPS = 1e-05

        def layer_norm(x, g, b):
            mu = jnp.mean(x, axis=-1, keepdims=True)
            var = jnp.var(x, axis=-1, keepdims=True)
            return (x - mu) * jax.lax.rsqrt(var + EPS) * g + b
        B, T, D = x.shape
        dh = D // H
        xn = layer_norm(x, norm_g, norm_b)
        q = (xn @ Wq + bq).reshape(B, T, H, dh)
        k = (xn @ Wk + bk).reshape(B, T, H, dh)
        v = (xn @ Wv + bv).reshape(B, T, H, dh)
        q = jax.nn.softmax(q, axis=-1)
        k = jax.nn.softmax(k, axis=1)
        ctx = jnp.einsum('bnhd,bnhl->bhdl', k, v)
        y = jnp.einsum('bnhd,bhdl->bnhl', q, ctx).reshape(B, T, D)
        emb_out = jax.nn.silu(emb) @ emb_W + emb_b
        scale, shift = jnp.split(emb_out, 2, axis=-1)
        h = layer_norm(y, sn_g, sn_b) * (1.0 + scale) + shift
        h = jax.nn.silu(h) @ out_W + out_b
        return x + gate_msa * h
    x = _L0_cond_ref(x, cond_1024, L0_cond_ln1_g, L0_cond_ln1_b, L0_cond_ln2_g, L0_cond_ln2_b, L0_cond_ada_w, L0_cond_ada_b, L0_cond_grid_wq, L0_cond_grid_wk, L0_cond_grid_wv, L0_cond_grid_wo, L0_cond_reg_wq, L0_cond_reg_wk, L0_cond_reg_wv, L0_cond_reg_wo, L0_cond_ent_wq, L0_cond_ent_wk, L0_cond_ent_wv, L0_cond_ent_wo, L0_cond_sem_wq, L0_cond_sem_wk, L0_cond_sem_wv, L0_cond_sem_wo, L0_cond_fus_wg, L0_cond_fus_bg, L0_cond_fus_wo, L0_cond_ffn_w1, L0_cond_ffn_w2, L0_cond_ffn_w3)
    x = _L1_cond_ref(x, cond_1024[:, None, :], cond_1024[:, None, :], L1_cond_norm_g, L1_cond_norm_b, L1_cond_Wq, L1_cond_bq, L1_cond_Wk, L1_cond_bk, L1_cond_Wv, L1_cond_bv, L1_cond_emb_W, L1_cond_emb_b, L1_cond_sn_g, L1_cond_sn_b, L1_cond_out_W, L1_cond_out_b)
    return x

_drawn_inputs = setup_inputs


def setup_inputs(seed=0):
    import zlib

    import numpy as np

    out = dict(_drawn_inputs(seed))
    spreads = {'L0_cond_ln1_g': (1.0, 0.2),
     'L0_cond_ln1_b': (0.0, 0.1),
     'L0_cond_ln2_g': (1.0, 0.2),
     'L0_cond_ln2_b': (0.0, 0.1),
     'L0_cond_ada_b': (0.0, 0.1),
     'L0_cond_fus_bg': (0.0, 0.272),
     'L1_cond_norm_g': (1.0, 0.6),
     'L1_cond_norm_b': (0.0, 0.275),
     'L1_cond_bq': (0.0, 0.8),
     'L1_cond_bk': (0.0, 0.8),
     'L1_cond_bv': (0.0, 0.1),
     'L1_cond_emb_b': (0.0, 0.424),
     'L1_cond_sn_g': (1.0, 0.6),
     'L1_cond_sn_b': (0.0, 0.783),
     'L1_cond_out_b': (0.0, 0.1)}
    factors = {'L1_cond_Wq': 8.0, 'L1_cond_Wk': 8.0, 'L1_cond_emb_W': 2.728}
    for name, (base, spread) in spreads.items():
        noise = np.random.default_rng([zlib.crc32(name.encode()), seed]).standard_normal(out[name].shape)
        drawn = base * np.exp(spread * noise) if base else spread * noise
        out[name] = jnp.asarray(drawn.astype(out[name].dtype))
    for name, factor in factors.items():
        out[name] = (out[name] * factor).astype(out[name].dtype)
    return out
```

```python
from contextlib import ExitStack

import concourse.bass as bass
from concourse import mybir

F32 = mybir.dt.float32
BF16 = mybir.dt.bfloat16
ALU = mybir.AluOpType
ACT = mybir.ActivationFunctionType
AX = mybir.AxisListType

P = 128
B, S, D = 2, 512, 128
T = B * S
NT = T // P
QT = S // P
H, DH = 16, 8
G = 4
NG = H // G
F = 512
FT = F // P
SCALE = 1.0 / DH ** 0.5
TERMS = 6
DATA = TERMS * DH
MROW = 64
ROWS = MROW + 3 * G
STEPS = 2 * B * NG
VW = 32
LOOPED = STEPS // 4 - 1

C_GAIN, C_BIAS, C_NG, C_NB, C_BK, C_COND, C_ADA, C_END = 0, 3, 6, 7, 8, 9, 11, 17
A_W, A_GW, A_ID, A_HM, A_LM, A_END = 17, 17 + 768, 17 + 1024, 17 + 1152, 17 + 1280, 17 + 1304
R_G, R_BQ, R_BV, R_OB, R_COND, R_FB, R_END = 0, 256, 384, 512, 640, 896, 900
W_WO, W_FWO, W_FWG, W_W1, W_W3, W_W2, W_QV, W_K, W_OUT, W_END = (
    0, 512, 640, 656, 1168, 1680, 2192, 2448, 2576, 2704)


def program(nc, x, pk_a, pk_b, pk_c, rows, cst_bf, stk_c, stk_o, out):
    ctx = ExitStack()
    with ctx:
        def sb(name, shape, dt=F32):
            return ctx.enter_context(nc.sbuf_tensor(name, shape, dt))

        def sem(name):
            return ctx.enter_context(nc.semaphore(name))

        qk_dram = [[nc.dram_tensor(f"qk_{t}{s}", [B * NG, G, DH, TERMS, S], BF16).ap() for s in "kq"] for t in "gs"]
        v_dram = [nc.dram_tensor(f"v_{t}", [B * NG, P, QT * G * VW], F32).ap() for t in "gs"]

        x_sb = sb("x_sb", [P, NT, D])
        pa = sb("pa", [P, A_END])
        wb = sb("wb", [P, 1536])
        wc = sb("wc", [P, W_END])
        rw = sb("rw", [P, R_END])
        cb = sb("cb", [P, 2 * P], BF16)
        stk = sb("stk", [ROWS, 4, 2, G, S], BF16)
        nxp = sb("nxp", [P, B, S + 2])
        nxs = sb("nxs", [P, B, S])
        v32 = sb("v32", [P, 2, B, NG, QT, G * VW])
        vb = sb("vb", [P, 4, QT, G * VW])
        parts_mem = sb("parts", [P, 4, 3, B, S], BF16)
        kv = sb("kv", [P, 5, 2, NT, D])
        ql = sb("ql", [P, 2, NT, D])
        o_sb = sb("o_sb", [P, 2, QT, B * NG + 1, G * DH])
        oev = sb("oev", [P, S])
        mneg = sb("mneg", [P, 2, G * QT])
        mres = sb("mres", [P, 2, G * QT])
        mprt = sb("mprt", [P, 2, QT, 3, G], BF16)
        mrow = sb("mrow", [G * 3, 2, S], BF16)
        orec = sb("orec", [P, QT * G])
        mv = sb("mv", [P, 4, NT, 2])
        bst = sb("bst", [P, NT, 6])
        rstd = sb("rstd", [P, 4, NT])
        mhalf = sb("mhalf", [P, NT])
        sil = sb("sil", [P, 4, B])
        silb = sb("silb", [P, B, P])
        ada = sb("ada", [P, 6, B])
        ga = sb("ga", [P, 3, B])
        ba = sb("ba", [P, 3, B])
        gr = sb("gr", [P, B, 2 * D])
        ls = sb("ls", [P, 5 * NT * H])
        lsm = sb("lsm", [P, 2, NT * H])
        tiny = sb("tiny", [P, 64])

        a_buf = parts_mem[:, :, :, :, :].rearrange("p a b c d -> p (a b c d)")[:, 0:8192].bitcast(F32) \
            .rearrange("p (n g s) -> p n g s", n=2, g=G)
        kvf = kv[:, :, :, :, :].rearrange("p a b c d -> p (a b c d)")
        resid = [kvf[:, 0:1024], kvf[:, 1024:2048]]
        xh1 = kvf[:, 2048:3072].rearrange("p (t d) -> p t d", t=NT)
        v32f = v32[:, :, :, :, :, :].rearrange("p a b c d e -> p (a b c d e)")
        prod = v32f[:, 0:5120]
        o_loc = v32f[:, 5120:7168].rearrange("p (a t d) -> p a t d", a=2, t=NT)
        ident = pa[:, A_ID:A_ID + P]
        hmask = pa[:, A_HM:A_HM + P]
        lmask = pa[:, A_LM:A_LM + 3 * NT]
        ident_b, diag_b = cb[:, 0:P], cb[:, P:2 * P]

        ps = ctx.enter_context(nc.psum_tensor("ps", [P, 8, 512], F32))

        def bank(i):
            return ps[:, i, :]

        names = """x_in pa_in wb_in wc_in rw_in cst_in grid0_out sem0_out grid1_out sem1_out v_out out_done
          dve_chain act_chain gp_chain tanh_c siluT silb_ready ada_mm gr_mm ga_ready gr_ready var1 rstd1 xh1_ready xT1
          nx_ready nxs_ready pads qk_mm part1 resid1 part2 part3 tok_mm tok_act tok_dve ones_set
          primed s_ready s_max split_step m_split mt_ready mt_evac st_ready st_bank_free a_free o_evac ot_ready o_norm o_rec
          loc_scores loc_soft loc_exp loc_sum loc_norm loc_out
          woT woT_sb fold_mm fold_sb oT oT_sb p_mm logits gate_exp x1_done
          var2 rstd2 xh2_ready xT2 nx2 h_mm h_tanh h_v u_ready y_mm x2_done
          var3 rstd3 xh3_ready xT3 nx3 qv_mm k_mm q_max qv_ready q_exp q_ready k_max k_exp kt_mm kt_sb ctx_mm ctx_sb qT qT_sb
          yl_mm var4 rstd4 xh4_ready xT4 h4 h4_tanh u4 z_mm o_ready gb_ready""".split()
        sm = {n: sem(n) for n in names}
        load_done = [sem(f"load_done{u}") for u in range(4)]
        m_done = [sem(f"m_done{u}") for u in range(4)]

        def chainer(eng, s):
            count = [0]

            def link(ins):
                count[0] += 1
                ins.then_inc(s, 1)
                eng.wait_ge(s, count[0])
            return link

        block = ctx.enter_context(nc.Block())
        nxb = nxp[:, :, 1:S + 1]
        qk_out = [[sm["grid0_out"], sm["grid1_out"]], [sm["sem0_out"], sm["sem1_out"]]]

        @block.sync
        def _(sp):
            sp.dma_start(x_sb[:, :, :], x.rearrange("b (t p) d -> p (b t) d", p=P)).then_inc(sm["x_in"], 16)
            sp.dma_start(pa[:, :], pk_a).then_inc(sm["pa_in"], 16)
            sp.dma_start(wb[:, :], pk_b).then_inc(sm["wb_in"], 16)
            stk_r = stk[:, :, :, :, :].rearrange("r a b c d -> r (a b c d)")
            sp.dma_start(stk_r[DATA:MROW, :], stk_c).then_inc(sm["cst_in"], 16)
            sp.dma_start(stk_r[MROW:ROWS, :], stk_o).then_inc(sm["cst_in"], 16)
            sp.dma_start(cb[:, :], cst_bf).then_inc(sm["cst_in"], 16)
            sp.dma_start(rw[:, :], rows).then_inc(sm["rw_in"], 16)

            order = [[0, 0, 0, 1, 1, 2], [0, 1, 2, 0, 1, 0]]
            for b in range(B):
                for ty in range(2):
                    for side in range(2):
                        sp.wait_ge(sm["part3"], 2 * ty + side + 1)
                        dst = qk_dram[ty][side].rearrange("(b g) h d j q -> b (g h d) j q", b=B)
                        for j in range(TERMS):
                            sp.dma_start(dst[b, :, j, :], parts_mem[:, 2 * ty + side, order[side][j], b, :]) \
                                .then_inc(qk_out[ty][b], 16)
                if b == 0:
                    sp.wait_ge(sm["tok_act"], 3 * NT)
                    sp.wait_ge(sm["ones_set"], 1)
                    for ty in range(2):
                        for bb in range(B):
                            dst = v_dram[ty].rearrange("(b g) p c -> b p g c", b=B)[bb]
                            src = v32[:, ty, bb].rearrange("p g k c -> p g (k c)")
                            sp.dma_start(dst, src).then_inc(sm["v_out"], 16)

            def load(u, bg):
                for side in range(2):
                    src = qk_dram[u % 2][side].rearrange("n h d j q -> n (d j) h q")
                    sp.dma_start(stk[0:DATA, u, side, :, :], src[bass.ds(bg, 1)].rearrange("o r h q -> (o r) h q")) \
                        .then_inc(load_done[u], 16)
                sp.dma_start(vb[:, u, :, :].rearrange("p k c -> p (k c)"),
                             v_dram[u % 2][bass.ds(bg, 1)].rearrange("o p c -> (o p) c")).then_inc(load_done[u], 16)
                sp.dma_start(stk[MROW:ROWS, u, 1, :, :].rearrange("r h q -> r (h q)"), stk_o[:, G * S:2 * G * S]) \
                    .then_inc(load_done[u], 16)

            def max_rows(step, u):
                sp.wait_ge(sm["mt_evac"], step + 1)
                sp.dma_start(stk[MROW:ROWS, u, 1, :, :],
                             mrow[:, u % 2, :].unsqueeze(1).broadcast_to([3 * G, G, S])).then_inc(m_done[u], 16)

            sp.wait_ge(sm["v_out"], 16 * 2 * B)
            sp.wait_ge(sm["cst_in"], 48)
            for u in range(4):
                sp.wait_ge(qk_out[u % 2][0], 16 * 2 * TERMS)
                load(u, u // 2)
            max_rows(0, 0)
            for b in range(2):
                sp.wait_ge(qk_out[b][1], 16 * 2 * TERMS)
            sp.dma_start(wc[:, :], pk_c).then_inc(sm["wc_in"], 16)

            def steps(it, last):
                for u in range(4):
                    n = 4 * it + u
                    if not (last and u == 3):
                        max_rows(n + 1, (u + 1) % 4)
                    if not last:
                        sp.wait_ge(sm["a_free"], 2 + 4 * (n + 1))
                        load(u, 2 * (it + 1) + u // 2)

            with sp.Fori(0, LOOPED) as it:
                steps(it, False)
            steps(LOOPED, True)

            for b in range(B):
                sp.wait_ge(sm["o_ready"], b + 1)
                sp.dma_start(out[b].rearrange("(t p) d -> p t d", p=P), x_sb[:, QT * b:QT * (b + 1), :]) \
                    .then_inc(sm["out_done"], 16)
            sp.wait_ge(sm["out_done"], 32)

        @block.gpsimd
        def _(gp):
            link = chainer(gp, sm["gp_chain"])
            link(gp.memset(mhalf[:, :], -0.5))
            gp.memset(nxp[:, :, 0:1], 0.0)
            gp.memset(nxp[:, :, S + 1:S + 2], 0.0).then_inc(sm["pads"], 1)
            gp.memset(v32f, 1.0).then_inc(sm["ones_set"], 1)

            def inv_std(k, eps, t0, t1, var, ready):
                gp.wait_ge(*var)
                link(gp.tensor_scalar(rstd[:, k, t0:t1], mv[:, k, t0:t1, 1], eps, None, ALU.add))
                gp.tensor_tensor(rstd[:, k, t0:t1], rstd[:, k, t0:t1], mhalf[:, t0:t1], ALU.pow).then_inc(ready, 1)

            inv_std(0, 1e-6, 0, NT, (sm["var1"], 1), sm["rstd1"])

            gp.wait_ge(sm["nx_ready"], 2)
            for par in range(2):
                gp.tensor_copy(nxs[:, :, par::2], nxb[:, :, 1 - par::2]).then_inc(sm["nxs_ready"], 1)

            gp.wait_ge(sm["tok_act"], 4 * NT)
            gp.wait_ge(sm["tok_dve"], 2 * NT)
            gp.wait_ge(sm["v_out"], 16 * 2 * B)
            pv = prod.rearrange("p (n t d) -> p n t d", n=5, t=NT)
            for n in range(5):
                ins = gp.tensor_tensor(pv[:, n], kv[:, n, 0], ql[:, 0 if n < 3 else 1], ALU.mult)
            link(ins)
            pg = prod.rearrange("p (g d) -> p g d", d=DH)
            link(gp.tensor_tensor(pg[:, :, 0:4], pg[:, :, 0:4], pg[:, :, 4:8], ALU.add))
            link(gp.tensor_tensor(pg[:, :, 0:2], pg[:, :, 0:2], pg[:, :, 2:4], ALU.add))
            gp.tensor_tensor(ls[:, :].unsqueeze(2), pg[:, :, 0:1], pg[:, :, 1:2], ALU.add).then_inc(sm["loc_scores"], 1)
            gp.wait_ge(sm["loc_norm"], 1)
            for n in range(5):
                w = ls[:, n * NT * H:(n + 1) * NT * H].unsqueeze(2).broadcast_to([P, NT * H, DH])
                ins = gp.tensor_tensor(pv[:, n].rearrange("p t (h d) -> p (t h) d", d=DH),
                                       kv[:, n, 1].rearrange("p t (h d) -> p (t h) d", d=DH), w, ALU.mult)
            link(ins)
            link(gp.tensor_tensor(pv[:, 0], pv[:, 0], pv[:, 1], ALU.add))
            gp.tensor_tensor(o_loc[:, 0], pv[:, 0], pv[:, 2], ALU.add)
            gp.tensor_tensor(o_loc[:, 1], pv[:, 3], pv[:, 4], ALU.add).then_inc(sm["loc_out"], 1)

            inv_std(1, 1e-6, 0, NT, (sm["var2"], 1), sm["rstd2"])
            for b in range(B):
                inv_std(2, 1e-5, QT * b, QT * (b + 1), (sm["var3"], b + 1), sm["rstd3"])
            for b in range(B):
                inv_std(3, 1e-5, QT * b, QT * (b + 1), (sm["var4"], b + 1), sm["rstd4"])

        wop = kvf[:, 0:1056].rearrange("p (b i c) -> p b i c", b=B, i=4)
        woT_sb = kvf[:, 1056:1568].rearrange("p (i c) -> p i c", i=4)
        oT_sb = kvf[:, 1568:2592].rearrange("p (n i c) -> p n i c", n=2, i=4)
        xh = kvf[:, 2592:3616].rearrange("p (t d) -> p t d", t=NT)
        nT = kvf[:, 3616:4640].rearrange("p (b s) -> p b s", b=B)
        th = kvf[:, 4640:5664].rearrange("p (n s) -> p n s", n=2)
        hv = kvf[:, 5664:6688].rearrange("p (n s) -> p n s", n=2)
        q_sb = kvf[:, 6688:7712].rearrange("p (t d) -> p t d", t=NT)
        v_sb = kvf[:, 7712:8736].rearrange("p (t d) -> p t d", t=NT)
        ctx_sb = kvf[:, 8736:8992].rearrange("p (b d) -> p b d", b=B)
        kx = kvf[:, 8992:10016].rearrange("p (b s) -> p b s", b=B)
        u_sb = a_buf.rearrange("p n g s -> p (n g s)").rearrange("p (f b s) -> p f b s", f=FT, b=B)
        kt_sb = v32f[:, 0:1024].rearrange("p (t d) -> p t d", t=NT)
        qT_sb = v32f[:, 1024:2048].rearrange("p (b s) -> p b s", b=B)
        hT = v32f[:, 2048:3072].rearrange("p (b s) -> p b s", b=B)
        t4 = v32f[:, 3072:4096].rearrange("p (b s) -> p b s", b=B)
        xgb = v32f[:, 4096:5120].rearrange("p (t d) -> p t d", t=NT)
        rowmx = ql[:, 0].rearrange("p t d -> p (t d)")
        gate = rowmx[:, 0:96].rearrange("p (t c) -> p t c", t=NT)
        qmx = rowmx[:, 96:224].rearrange("p (b c) -> p b c", b=B)
        qsm = rowmx[:, 224:352].rearrange("p (b c) -> p b c", b=B)
        ksm = rowmx[:, 352:368].rearrange("p (b c) -> p b c", b=B)
        cgb = rowmx[:, 368:624].rearrange("p (b d) -> p b d", b=B)
        cgh = rowmx[:, 624:880].rearrange("p (b d) -> p b d", b=B)
        gbs = ql[:, 1].rearrange("p t d -> p (t d)")

        def gate_exp(act, t):
            act.wait_ge(sm["logits"], t + 1)
            act.activation(gate[:, t, 4:8], gate[:, t, 0:4], ACT.Exp, bias=gate[:, t, 8:9],
                           accum_out=gate[:, t, 9:10]).then_inc(sm["gate_exp"], 1)

        @block.scalar
        def _(act):
            link = chainer(act, sm["act_chain"])
            act.sem_inc(sm["st_bank_free"], 2)
            act.wait_ge(sm["pa_in"], 16)
            act.activation(sil[:, 0, :], pa[:, C_COND:C_COND + B], ACT.Tanh, scale=0.5).then_inc(sm["tanh_c"], 1)
            act.wait_ge(sm["ga_ready"], 1)
            act.wait_ge(sm["pads"], 1)
            for b in range(B):
                act.wait_ge(sm["xT1"], b + 1)
                act.activation(nxb[:, b, :], bank(b), ACT.Identity, scale=ga[:, 0, b:b + 1],
                               bias=ba[:, 0, b:b + 1]).then_inc(sm["nx_ready"], 1)
            for n in range(4):
                act.wait_ge(sm["qk_mm"], n + 1)
                src = ps[:, 4 + 2 * (n % 2):6 + 2 * (n % 2), :]
                act.activation(parts_mem[:, n, 0], src, ACT.Copy, scale=SCALE if n % 2 else 1.0).then_inc(sm["part1"], 1)
                act.wait_ge(sm["resid1"], n + 1)
                act.activation(parts_mem[:, n, 1], resid[n % 2].rearrange("p (b s) -> p b s", b=B), ACT.Copy) \
                    .then_inc(sm["part2"], 1)
            act.wait_ge(sm["ones_set"], 1)
            for t in range(NT):
                act.wait_ge(sm["tok_mm"], t + 1)
                bk = bank(4 + t % 4)
                act.activation(ql[:, :, t, :], bk[:, 0:256].rearrange("p (a d) -> p a d", a=2), ACT.Copy, scale=SCALE) \
                    .then_inc(sm["tok_act"], 1)
                for ty in range(2):
                    dst = v32[:, ty, t // QT, :, t % QT, :].rearrange("p g (h c) -> p g h c", h=G)[:, :, :, 0:DH]
                    src = bk[:, 256 + P * ty:384 + P * ty].rearrange("p (g h c) -> p g h c", g=NG, h=G)
                    act.activation(dst, src, ACT.Copy).then_inc(sm["tok_act"], 1)
            for t in range(NT):
                act.wait_ge(sm["tok_mm"], NT + 3 * t + 3)
                act.activation(kv[:, 4, :, t, :], bank(4 + t % 4)[:, 0:256].rearrange("p (a d) -> p a d", a=2), ACT.Copy) \
                    .then_inc(sm["tok_act"], 1)

            def max_evac(step, par):
                act.wait_ge(sm["mt_ready"], step + 1)
                act.activation(mrow[:, par, :], bank(7)[0:3 * G, 0:S // 2].bitcast(BF16), ACT.Copy).then_inc(sm["mt_evac"], 1)

            def o_evac(n):
                act.wait_ge(sm["a_free"], 4 * n + 2)
                act.wait_ge(sm["ot_ready"], n + 1)
                act.activation(oev[:, :], bank(6), ACT.Copy).then_inc(sm["o_evac"], 1)

            max_evac(0, 0)

            def steps(it, last):
                for u in range(4):
                    n = 4 * it + u
                    for kt in range(QT):
                        act.wait_ge(sm["a_free"], 4 * n + kt + 1)
                        for h in range(G):
                            act.wait_ge(sm["st_ready"], 16 * n + 4 * kt + h + 1)
                            act.activation(a_buf[:, kt % 2, h, :], bank(4 + h % 2), ACT.Exp) \
                                .then_inc(sm["st_bank_free"], 1)
                        if last and u == 0 and kt == 0:
                            act.wait_ge(sm["loc_soft"], 1)
                            act.activation(ls[:, :], ls[:, :], ACT.Exp).then_inc(sm["loc_exp"], 1)
                        if kt == 0:
                            o_evac(n)
                        if kt == 2 and not (last and u == 3):
                            max_evac(n + 1, (u + 1) % 2)

            act.wait_ge(sm["grid1_out"], 16 * 2 * TERMS)
            act.wait_ge(sm["sem1_out"], 16 * 2 * TERMS)
            act.wait_ge(sm["primed"], 1)
            with act.Fori(0, LOOPED) as it:
                steps(it, False)
            steps(LOOPED, True)
            o_evac(STEPS)

            act.wait_ge(sm["woT"], 1)
            act.wait_ge(sm["loc_out"], 1)
            act.activation(woT_sb, bank(0).rearrange("p (i c) -> p i c", i=4), ACT.Copy).then_inc(sm["woT_sb"], 1)
            for t in range(NT):
                act.wait_ge(sm["oT"], t + 1)
                act.activation(oT_sb[:, t % 2], bank(6 + t % 2).rearrange("p (i c) -> p i c", i=4), ACT.Copy) \
                    .then_inc(sm["oT_sb"], 1)
                if t >= 1:
                    gate_exp(act, t - 1)
            gate_exp(act, NT - 1)
            for b in range(B):
                act.wait_ge(sm["xT2"], b + 1)
                act.activation(nT[:, b, :], bank(b), ACT.Identity, scale=ga[:, 1, b:b + 1],
                               bias=ba[:, 1, b:b + 1]).then_inc(sm["nx2"], 1)
            for n in range(B * FT):
                act.wait_ge(sm["h_mm"], n + 1)
                if n >= 2:
                    act.wait_ge(sm["h_v"], n - 1)
                act.activation(th[:, n % 2], bank(2 * (n % 3)), ACT.Tanh, scale=0.5).then_inc(sm["h_tanh"], 1)
            for b in range(B):
                act.wait_ge(sm["xT3"], b + 1)
                act.activation(nT[:, b, :], bank(b), ACT.Identity, scale=pa[:, C_NG:C_NG + 1],
                               bias=pa[:, C_NB:C_NB + 1]).then_inc(sm["nx3"], 1)
            for b in range(B):
                act.wait_ge(sm["k_max"], b + 1)
                act.activation(kx[:, b, :], bank(6 + b), ACT.Exp, bias=ksm[:, b, 2:3],
                               accum_out=ksm[:, b, 3:4]).then_inc(sm["k_exp"], 1)
                act.wait_ge(sm["q_max"], b + 1)
                qb = q_sb[:, QT * b:QT * (b + 1), :]
                act.activation(qb, qb, ACT.Exp).then_inc(sm["q_exp"], 1)
            for b in range(B):
                act.wait_ge(sm["kt_mm"], b + 1)
                act.activation(kt_sb[:, QT * b:QT * (b + 1), :], bank(b).rearrange("p (t d) -> p t d", t=QT), ACT.Copy) \
                    .then_inc(sm["kt_sb"], 1)
            for b in range(B):
                act.wait_ge(sm["qT"], b + 1)
                act.activation(qT_sb[:, b, :], bank(2 + b), ACT.Copy).then_inc(sm["qT_sb"], 1)
            for b in range(B):
                act.wait_ge(sm["xT4"], b + 1)
                act.activation(hT[:, b, :], bank(b), ACT.Identity, scale=ga[:, 2, b:b + 1],
                               bias=ba[:, 2, b:b + 1]).then_inc(sm["h4"], 1)
                act.wait_ge(sm["h4"], b + 1)
                act.activation(t4[:, b, :], hT[:, b, :], ACT.Tanh, scale=0.5).then_inc(sm["h4_tanh"], 1)

        @block.vector
        def _(dve):
            link = chainer(dve, sm["dve_chain"])

            def stats(k, t, src):
                link(dve.bn_stats(bst[:, t, :], src))
                return dve.bn_aggr(mv[:, k, t, :], bst[:, t, :])

            def normalise(k, t, dst, src):
                return dve.tensor_scalar(dst, src, mv[:, k, t, 0:1], rstd[:, k, t:t + 1], ALU.subtract, ALU.mult)

            dve.wait_ge(sm["x_in"], 16)
            for t in range(NT):
                ins = dve.bn_stats(bst[:, t, :], x_sb[:, t, :])
            link(ins)
            for t in range(NT):
                ins = dve.bn_aggr(mv[:, 0, t, :], bst[:, t, :])
            ins.then_inc(sm["var1"], 1)
            dve.wait_ge(sm["tanh_c"], 1)
            link(dve.scalar_tensor_tensor(sil[:, 1, :], sil[:, 0, :], 1.0, pa[:, C_COND:C_COND + B], ALU.add, ALU.mult))
            dve.tensor_scalar(sil[:, 2, :], sil[:, 1, :], 0.5, None, ALU.mult).then_inc(sm["siluT"], 1)
            dve.wait_ge(sm["siluT"], 1)
            dve.tensor_copy(silb[:, :, :], sil[:, 2, :].unsqueeze(2).broadcast_to([P, B, P])).then_inc(sm["silb_ready"], 1)
            dve.wait_ge(sm["var1"], 1)
            dve.wait_ge(sm["rstd1"], 1)
            for t in range(NT):
                normalise(0, t, xh1[:, t, :], x_sb[:, t, :]).then_inc(sm["xh1_ready"], 1)
            dve.wait_ge(sm["ada_mm"], 1)
            link(dve.tensor_tensor(ada[:, :, :], bank(2)[:, 0:12].rearrange("p (j b) -> p j b", b=B),
                                   pa[:, C_ADA:C_ADA + 6].unsqueeze(2).broadcast_to([P, 6, B]), ALU.add))
            sc = ada[:, 0:3, :]
            dve.scalar_tensor_tensor(ga[:, :, :], sc, 1.0,
                                     pa[:, C_GAIN:C_GAIN + 3].unsqueeze(2).broadcast_to([P, 3, B]), ALU.add, ALU.mult)
            link(dve.scalar_tensor_tensor(ba[:, :, :], sc, 1.0,
                                          pa[:, C_BIAS:C_BIAS + 3].unsqueeze(2).broadcast_to([P, 3, B]), ALU.add, ALU.mult))
            dve.tensor_tensor(ba[:, :, :], ba[:, :, :], ada[:, 3:6, :], ALU.add).then_inc(sm["ga_ready"], 1)
            for n in range(4):
                src = ps[:, 4 + 2 * (n % 2):6 + 2 * (n % 2), :]
                r = resid[n % 2].rearrange("p (b s) -> p b s", b=B)
                dve.wait_ge(sm["part1"], n + 1)
                dve.scalar_tensor_tensor(r, src, SCALE if n % 2 else 1.0, parts_mem[:, n, 0], ALU.mult, ALU.subtract) \
                    .then_inc(sm["resid1"], 1)
                dve.wait_ge(sm["resid1"], n + 1)
                dve.wait_ge(sm["part2"], n + 1)
                dve.tensor_tensor(parts_mem[:, n, 2], r, parts_mem[:, n, 1], ALU.subtract).then_inc(sm["part3"], 1)
            dve.wait_ge(sm["gr_mm"], 1)
            dve.wait_ge(sm["rw_in"], 16)
            link(dve.tensor_tensor(gr[:, :, :], bank(3).rearrange("p (b c) -> p b c", b=B),
                                   rw[:, R_G:R_G + 256].unsqueeze(1).broadcast_to([P, B, 256]), ALU.add))
            dve.tensor_scalar(gr[:, :, D:2 * D], gr[:, :, D:2 * D], 0.5, None, ALU.mult).then_inc(sm["gr_ready"], 1)
            for t in range(NT):
                dve.wait_ge(sm["tok_mm"], NT + 3 * t + 1)
                dve.tensor_copy(kv[:, 1:4:2, :, t, :], bank(t % 2).rearrange("p (n a d) -> p n a d", n=2, a=2)) \
                    .then_inc(sm["tok_dve"], 1)
                dve.wait_ge(sm["tok_mm"], NT + 3 * t + 2)
                dve.tensor_copy(kv[:, 0:3:2, :, t, :], bank(2 + t % 2).rearrange("p (n a d) -> p n a d", n=2, a=2)) \
                    .then_inc(sm["tok_dve"], 1)

            def row_max(step, r, par):
                dve.wait_ge(sm["s_ready"], 8 * step + r + 1)
                dve.tensor_reduce(mneg[:, par, 2 * r:2 * r + 2], ps[:, 2 * (r % 2):2 * (r % 2) + 2, :], AX.X, ALU.max,
                                  negate=True).then_inc(sm["s_max"], 1)

            def split(step, par, again):
                m = mneg[:, par, :].rearrange("p (h q) -> p q h", h=G)
                r = mres[:, par, :].rearrange("p (h q) -> p q h", h=G)
                dve.wait_ge(sm["s_max"], 8 * (step + 1))
                if again:
                    dve.wait_ge(sm["mt_ready"], step - 1)
                dve.tensor_copy(mprt[:, par, :, 0, :], m).then_inc(sm["split_step"], 1)
                dve.wait_ge(sm["split_step"], 4 * step + 1)
                dve.tensor_tensor(r, m, mprt[:, par, :, 0, :], ALU.subtract).then_inc(sm["split_step"], 1)
                dve.wait_ge(sm["split_step"], 4 * step + 2)
                dve.tensor_copy(mprt[:, par, :, 1, :], r).then_inc(sm["split_step"], 1)
                dve.wait_ge(sm["split_step"], 4 * step + 3)
                dve.tensor_tensor(r, r, mprt[:, par, :, 1, :], ALU.subtract).then_inc(sm["split_step"], 1)
                dve.wait_ge(sm["split_step"], 4 * step + 4)
                dve.tensor_copy(mprt[:, par, :, 2, :], r).then_inc(sm["m_split"], 1)

            def o_norm(n, ty, slot):
                t7 = bank(7).rearrange("p (n c) -> p n c", c=VW)
                t4d = bank(7).rearrange("p (q h c) -> p q h c", q=QT, c=VW)
                dve.wait_ge(sm["ot_ready"], n + 2)
                dve.reciprocal(orec[:, :].unsqueeze(2), t7[:, :, DH:DH + 1]).then_inc(sm["o_rec"], 1)
                dve.wait_ge(sm["o_rec"], n + 1)
                dst = o_sb[:, ty, :, bass.ds(slot, 1), :].rearrange("p q o (h d) -> p q (o h) d", d=DH)
                inv = orec[:, :].rearrange("p (q h) -> p q h", q=QT).unsqueeze(3).broadcast_to([P, QT, G, DH])
                dve.tensor_tensor(dst, t4d[:, :, :, 0:DH], inv, ALU.mult).then_inc(sm["o_norm"], 1)

            dve.wait_ge(sm["tok_act"], 4 * NT)
            dve.memset(bank(6), 1.0).then_inc(sm["primed"], 1)
            for step in range(2):
                for r in range(8):
                    row_max(step, r, step)
                split(step, step, False)

            def steps(it, last):
                for u in range(4):
                    n = 4 * it + u
                    ahead = not (last and u >= 2)
                    for kt in range(QT):
                        if ahead:
                            for r in (2 * kt, 2 * kt + 1):
                                row_max(n + 2, r, u % 2)
                        if kt == 0:
                            o_norm(n, (u + 1) % 2, 2 * it + (u + 1) // 2)
                    if ahead:
                        split(n + 2, u % 2, True)

            with dve.Fori(0, LOOPED) as it:
                steps(it, False)
            dve.wait_ge(sm["loc_scores"], 1)
            lr = ls[:, 0:3 * NT * H].rearrange("p (n h) -> p n h", h=H)
            link(dve.tensor_tensor(lr, lr, lmask.unsqueeze(2).broadcast_to([P, 3 * NT, H]), ALU.add))
            l5 = ls[:, :].rearrange("p (n c) -> p n c", n=5)
            link(dve.tensor_tensor(lsm[:, :, :], l5[:, 0:4:3, :], l5[:, 1:5:3, :], ALU.max))
            link(dve.tensor_tensor(lsm[:, 0, :], lsm[:, 0, :], l5[:, 2, :], ALU.max))
            dve.tensor_tensor(l5[:, 0:3, :], l5[:, 0:3, :], lsm[:, 0:1, :].broadcast_to([P, 3, NT * H]), ALU.subtract)
            dve.tensor_tensor(l5[:, 3:5, :], l5[:, 3:5, :], lsm[:, 1:2, :].broadcast_to([P, 2, NT * H]), ALU.subtract) \
                .then_inc(sm["loc_soft"], 1)
            dve.wait_ge(sm["loc_exp"], 1)
            link(dve.tensor_tensor(lsm[:, :, :], l5[:, 0:4:3, :], l5[:, 1:5:3, :], ALU.add))
            link(dve.tensor_tensor(lsm[:, 0, :], lsm[:, 0, :], l5[:, 2, :], ALU.add))
            link(dve.reciprocal(lsm[:, :, :], lsm[:, :, :]))
            dve.tensor_tensor(l5[:, 0:3, :], l5[:, 0:3, :], lsm[:, 0:1, :].broadcast_to([P, 3, NT * H]), ALU.mult)
            dve.tensor_tensor(l5[:, 3:5, :], l5[:, 3:5, :], lsm[:, 1:2, :].broadcast_to([P, 2, NT * H]), ALU.mult) \
                .then_inc(sm["loc_norm"], 1)
            steps(LOOPED, True)
            o_norm(STEPS, 1, B * NG)

            dve.wait_ge(sm["fold_mm"], 1)
            for b in range(B):
                for i in range(4):
                    src = bank(1 + i)[:, 0:132]
                    dve.tensor_tensor(wop[:, b, i, 0:D], src[:, 0:D], gr[:, b, 0:D], ALU.mult)
                    ins = dve.tensor_copy(wop[:, b, i, D:132], src[:, D:132])
            ins.then_inc(sm["fold_sb"], 1)

            def p_out(t):
                a = 2 * (t % 3)
                return ps[:, a:a + 2, :].rearrange("p n (i c) -> p (n i) c", i=2)

            for t in range(NT + 1):
                if t < NT:
                    g = gate[:, t, :]
                    dve.wait_ge(sm["p_mm"], t + 1)
                    link(dve.tensor_reduce(g[:, 0:4], p_out(t)[:, :, D:132].rearrange("p i c -> p c i"), AX.X, ALU.add))
                    link(dve.tensor_tensor(g[:, 0:4], g[:, 0:4], rw[:, R_FB:R_FB + 4], ALU.add))
                    dve.tensor_reduce(g[:, 8:9], g[:, 0:4], AX.X, ALU.max, negate=True).then_inc(sm["logits"], 1)
                if t >= 1:
                    k = t - 1
                    g = gate[:, k, :]
                    dve.wait_ge(sm["gate_exp"], k + 1)
                    link(dve.reciprocal(g[:, 10:11], g[:, 9:10]))
                    link(dve.tensor_scalar(g[:, 0:4], g[:, 4:8], g[:, 10:11], None, ALU.mult))
                    for i in range(4):
                        ins = dve.scalar_tensor_tensor(x_sb[:, k, :], p_out(k)[:, i, 0:D], g[:, i:i + 1], x_sb[:, k, :],
                                                       ALU.mult, ALU.add)
                        if i < 3:
                            link(ins)
                    ins.then_inc(sm["x1_done"], 1)
                    dve.wait_ge(sm["x1_done"], k + 1)
                    ins = stats(1, k, x_sb[:, k, :])
            ins.then_inc(sm["var2"], 1)
            dve.wait_ge(sm["rstd2"], 1)
            dve.wait_ge(sm["var2"], 1)
            for t in range(NT):
                normalise(1, t, xh[:, t, :], x_sb[:, t, :]).then_inc(sm["xh2_ready"], 1)
            for b in range(B):
                for f in range(FT):
                    n = FT * b + f
                    dve.wait_ge(sm["h_tanh"], n + 1)
                    dve.scalar_tensor_tensor(hv[:, n % 2], th[:, n % 2], 1.0, bank(2 * (n % 3)), ALU.add, ALU.mult) \
                        .then_inc(sm["h_v"], 1)
                    dve.wait_ge(sm["h_v"], n + 1)
                    dve.tensor_tensor(u_sb[:, f, b, :], hv[:, n % 2], bank(2 * (n % 3) + 1), ALU.mult) \
                        .then_inc(sm["u_ready"], 1)
            for b in range(B):
                xb = x_sb[:, QT * b:QT * (b + 1), :]
                dve.wait_ge(sm["y_mm"], b + 1)
                yb = bank(6 + b).rearrange("p (t d) -> p t d", t=QT)
                hb = xh[:, QT * b:QT * (b + 1), :]
                link(dve.tensor_tensor(hb, yb, gr[:, b:b + 1, D:2 * D].broadcast_to([P, QT, D]), ALU.mult))
                dve.tensor_tensor(xb, xb, hb, ALU.add).then_inc(sm["x2_done"], 1)
                dve.wait_ge(sm["x2_done"], b + 1)
                for t in range(QT * b, QT * (b + 1)):
                    ins = dve.bn_stats(bst[:, t, :], x_sb[:, t, :])
                link(ins)
                for t in range(QT * b, QT * (b + 1)):
                    ins = dve.bn_aggr(mv[:, 2, t, :], bst[:, t, :])
                ins.then_inc(sm["var3"], 1)
            dve.tensor_scalar(cgh, rw[:, R_COND:R_COND + 256].rearrange("p (b d) -> p b d", b=B), 0.5, None, ALU.mult)
            link(dve.tensor_tensor(cgb, rw[:, R_COND:R_COND + 256].rearrange("p (b d) -> p b d", b=B),
                                   rw[:, R_OB:R_OB + P].unsqueeze(1).broadcast_to([P, B, D]), ALU.mult))
            for b in range(B):
                dve.wait_ge(sm["rstd3"], b + 1)
                dve.wait_ge(sm["var3"], b + 1)
                for t in range(QT * b, QT * (b + 1)):
                    normalise(2, t, xh[:, t, :], x_sb[:, t, :]).then_inc(sm["xh3_ready"], 1)
            for b in range(B):
                ins = dve.tensor_tensor(xgb[:, QT * b:QT * (b + 1), :], x_sb[:, QT * b:QT * (b + 1), :],
                                        cgb[:, b:b + 1, :].broadcast_to([P, QT, D]), ALU.add)
            ins.then_inc(sm["gb_ready"], 1)
            for b in range(B):
                k = ksm[:, b, :]
                dve.wait_ge(sm["k_mm"], b + 1)
                link(dve.tensor_reduce(k[:, 0:1], bank(6 + b), AX.X, ALU.max))
                link(dve.tensor_tensor(k[:, 1:2], k[:, 0:1], pa[:, C_BK:C_BK + 1], ALU.add))
                dve.tensor_tensor(k[:, 2:3], pa[:, C_BK:C_BK + 1], k[:, 1:2], ALU.subtract).then_inc(sm["k_max"], 1)
                dve.wait_ge(sm["qv_mm"], b + 1)
                qv = ps[:, 2 + 2 * b:4 + 2 * b, :].rearrange("p n (t c) -> p (n t) c", t=2)
                qb = q_sb[:, QT * b:QT * (b + 1), :]
                q8 = qb.rearrange("p t (h d) -> p (t h) d", d=DH)
                link(dve.tensor_tensor(qb, qv[:, :, 0:D], rw[:, R_BQ:R_BQ + P].unsqueeze(1).broadcast_to([P, QT, D]), ALU.add))
                dve.tensor_tensor(v_sb[:, QT * b:QT * (b + 1), :], qv[:, :, D:2 * D],
                                  rw[:, R_BV:R_BV + P].unsqueeze(1).broadcast_to([P, QT, D]), ALU.add) \
                    .then_inc(sm["qv_ready"], 1)
                link(dve.tensor_reduce(qmx[:, b, :], q8, AX.X, ALU.max))
                dve.tensor_tensor(q8, q8, qmx[:, b, :].unsqueeze(2).broadcast_to([P, QT * H, DH]), ALU.subtract) \
                    .then_inc(sm["q_max"], 1)
            for b in range(B):
                q8 = q_sb[:, QT * b:QT * (b + 1), :].rearrange("p t (h d) -> p (t h) d", d=DH)
                dve.wait_ge(sm["q_exp"], b + 1)
                link(dve.tensor_reduce(qsm[:, b, :], q8, AX.X, ALU.add))
                link(dve.reciprocal(qsm[:, b, :], qsm[:, b, :]))
                dve.tensor_tensor(q8, q8, qsm[:, b, :].unsqueeze(2).broadcast_to([P, QT * H, DH]), ALU.mult) \
                    .then_inc(sm["q_ready"], 1)
            for b in range(B):
                dve.wait_ge(sm["k_exp"], b + 1)
                link(dve.reciprocal(ksm[:, b, 4:5], ksm[:, b, 3:4]))
                dve.wait_ge(sm["ctx_mm"], b + 1)
                dve.scalar_tensor_tensor(ctx_sb[:, b, :], bank(4 + b)[:, 0:D], ksm[:, b, 4:5], hmask, ALU.mult, ALU.mult) \
                    .then_inc(sm["ctx_sb"], 1)
            for b in range(B):
                dve.wait_ge(sm["yl_mm"], b + 1)
                yb = bank(6 + b).rearrange("p (t d) -> p t d", t=QT)
                for t in range(QT):
                    ins = dve.bn_stats(bst[:, QT * b + t, :], yb[:, t, :])
                link(ins)
                for t in range(QT):
                    ins = dve.bn_aggr(mv[:, 3, QT * b + t, :], bst[:, QT * b + t, :])
                ins.then_inc(sm["var4"], 1)
            for b in range(B):
                yb = bank(6 + b).rearrange("p (t d) -> p t d", t=QT)
                dve.wait_ge(sm["rstd4"], b + 1)
                dve.wait_ge(sm["var4"], b + 1)
                for t in range(QT):
                    normalise(3, QT * b + t, xh[:, QT * b + t, :], yb[:, t, :]).then_inc(sm["xh4_ready"], 1)
            for b in range(B):
                dve.wait_ge(sm["h4_tanh"], b + 1)
                dve.scalar_tensor_tensor(t4[:, b, :], t4[:, b, :], 1.0, hT[:, b, :], ALU.add, ALU.mult) \
                    .then_inc(sm["u4"], 1)
            for b in range(B):
                dve.wait_ge(sm["z_mm"], b + 1)
                zb = bank(2 + b).rearrange("p (t d) -> p t d", t=QT)
                hb = xh[:, QT * b:QT * (b + 1), :]
                dve.wait_ge(sm["gb_ready"], 1)
                link(dve.tensor_tensor(hb, zb, cgh[:, b:b + 1, :].broadcast_to([P, QT, D]), ALU.mult))
                dve.tensor_tensor(x_sb[:, QT * b:QT * (b + 1), :], hb, xgb[:, QT * b:QT * (b + 1), :], ALU.add) \
                    .then_inc(sm["o_ready"], 1)

        def ffn_out(pe, b):
            pe.wait_ge(sm["u_ready"], FT * (b + 1))
            for t in range(QT):
                for f in range(FT):
                    ins = pe.matmul(bank(6 + b)[:, P * t:P * (t + 1)], u_sb[:, f, b, P * t:P * (t + 1)],
                                    wc[:, W_W2 + P * f:W_W2 + P * (f + 1)], start=f == 0, stop=f == FT - 1)
            ins.then_inc(sm["y_mm"], 1)

        @block.tensor
        def _(pe):
            pe.sem_inc(sm["ot_ready"], 1)
            pe.sem_inc(sm["a_free"], 2)
            pe.wait_ge(sm["pa_in"], 16)
            pe.wait_ge(sm["silb_ready"], 1)
            for j in range(6):
                ins = pe.matmul(bank(2)[:, 2 * j:2 * j + 2], pa[:, A_W + P * j:A_W + P * (j + 1)], sil[:, 2, :],
                                start=True, stop=True)
            ins.then_inc(sm["ada_mm"], 1)
            for b in range(B):
                ins = pe.matmul(bank(3)[:, 256 * b:256 * (b + 1)], silb[:, b, :], pa[:, A_GW:A_GW + 256],
                                start=True, stop=True)
            ins.then_inc(sm["gr_mm"], 1)

            def transposes(bk, src, dst, ready, base):
                for t in range(QT):
                    pe.wait_ge(ready, base + t + 1)
                    ins = pe.transpose(bank(bk)[:, P * t:P * (t + 1)], src[:, base + t, :], ident)
                ins.then_inc(dst, 1)

            for b in range(B):
                transposes(b, xh1, sm["xT1"], sm["xh1_ready"], QT * b)
            pe.wait_ge(sm["wb_in"], 16)
            pe.wait_ge(sm["nx_ready"], 2)
            for n in range(4):
                if n >= 2:
                    pe.wait_ge(sm["resid1"], n - 1)
                for b in range(B):
                    ins = pe.matmul(bank(4 + 2 * (n % 2) + b), wb[:, P * n:P * (n + 1)], nxb[:, b, :],
                                    start=True, stop=True)
                ins.then_inc(sm["qk_mm"], 1)

            def tokens(t, shift):
                b, q = t // QT, t % QT
                return nxp[:, b, 1 + shift + P * q:1 + shift + P * (q + 1)]

            for t in range(NT):
                if t < 4:
                    pe.wait_ge(sm["resid1"], 3 + t // 2)
                else:
                    pe.wait_ge(sm["tok_act"], 3 * (t - 3))
                pe.matmul(bank(4 + t % 4), tokens(t, 0), wb[:, 512:1024], start=True, stop=True).then_inc(sm["tok_mm"], 1)
            pe.wait_ge(sm["nxs_ready"], 2)
            pe.wait_ge(sm["gr_ready"], 1)
            for t in range(NT):
                b, q = t // QT, t % QT
                if t >= 2:
                    pe.wait_ge(sm["tok_dve"], 2 * (t - 1) - 1)
                pe.matmul(bank(t % 2), tokens(t, 0), wb[:, 1024:1536], start=True, stop=True).then_inc(sm["tok_mm"], 1)
                if t >= 2:
                    pe.wait_ge(sm["tok_dve"], 2 * (t - 1))
                pe.matmul(bank(2 + t % 2)[:, 0:256], tokens(t, -1), wb[:, 1024:1280], start=True, stop=True)
                pe.matmul(bank(2 + t % 2)[:, 256:512], tokens(t, 1), wb[:, 1024:1280], start=True, stop=True) \
                    .then_inc(sm["tok_mm"], 1)
                pe.wait_ge(sm["tok_act"], 3 * (t + 5) if t < 4 else 3 * NT + t - 3)
                pe.matmul(bank(4 + t % 4)[:, 0:256], nxs[:, b, P * q:P * (q + 1)], wb[:, 1280:1536],
                          start=True, stop=True).then_inc(sm["tok_mm"], 1)

            def score(u, r, step, j):
                h, q = r // 2, 2 * (r % 2) + j
                dst = ps[:, 2 * (r % 2) + j, :]
                if j == 0 and step is not None:
                    pe.wait_ge(sm["s_max"], 8 * step + r - 1)
                ins = pe.matmul(dst, stk[:, u, 1, h, P * q:P * (q + 1)], stk[:, u, 0, h, :], start=True, stop=u % 2 == 1)
                if u % 2 == 0:
                    ins = pe.matmul(dst[:, P * q:P * (q + 1)], ident_b, diag_b, start=False, stop=True)
                if j == 1:
                    ins.then_inc(sm["s_ready"], 1)

            def score_t(u, kt, h, step):
                pe.wait_ge(sm["st_bank_free"], 16 * step + 4 * kt + h + 1)
                dst = bank(4 + h % 2)
                ins = pe.matmul(dst, stk[:, u, 0, h, P * kt:P * (kt + 1)], stk[:, u, 1, h, :], start=True, stop=u % 2 == 1)
                if u % 2 == 0:
                    ins = pe.matmul(dst[:, P * kt:P * (kt + 1)], ident_b, diag_b, start=False, stop=True)
                ins.then_inc(sm["st_ready"], 1)

            def weighted(u, kt, step):
                pe.wait_ge(sm["st_bank_free"], 2 + 16 * step + 4 * kt + 4)
                if kt == 0:
                    pe.wait_ge(sm["o_evac"], step + 1)
                for h in range(G):
                    ins = pe.matmul(bank(6)[VW * h:VW * (h + 1), :], vb[:, u, kt, VW * h:VW * (h + 1)],
                                    a_buf[:, kt % 2, h, :], start=kt == 0, stop=kt == QT - 1)
                ins.then_inc(sm["a_free"], 1)

            def o_back(n):
                pe.wait_ge(sm["mt_evac"], n + 1)
                pe.wait_ge(sm["o_evac"], n + 1)
                for q in range(QT):
                    ins = pe.transpose(bank(7)[:, P * q:P * (q + 1)], oev[:, P * q:P * (q + 1)], ident)
                ins.then_inc(sm["ot_ready"], 1)

            def max_t(step, par, normed):
                pe.wait_ge(sm["m_split"], step + 1)
                if normed is not None:
                    pe.wait_ge(sm["o_norm"], normed)
                for q in range(QT):
                    ins = pe.transpose(bank(7)[0:3 * G, P // 2 * q:P // 2 * (q + 1)].bitcast(BF16),
                                       mprt[:, par, q].rearrange("p c h -> p (c h)"), ident_b)
                ins.then_inc(sm["mt_ready"], 1)

            pe.wait_ge(sm["cst_in"], 48)
            pe.wait_ge(sm["tok_dve"], 2 * NT)
            pe.wait_ge(sm["tok_act"], 4 * NT)
            for step in range(2):
                pe.wait_ge(load_done[step], 64)
                for r in range(8):
                    for j in range(2):
                        score(step, r, step if 8 * step + r >= 2 else None, j)
                if step == 0:
                    max_t(0, 0, None)
            pe.wait_ge(m_done[0], 16)
            for h in range(G):
                score_t(0, 0, h, 0)

            def steps(it, last):
                for u in range(4):
                    n = 4 * it + u
                    ahead = not (last and u >= 2)
                    w = (u + 2) % 4
                    for kt in range(QT):
                        if kt == 0 and ahead:
                            pe.wait_ge(load_done[w], 64 * (it + 1 + (u >= 2)))
                        more = not (last and u == 3 and kt == 3)
                        if kt == 3 and more:
                            pe.wait_ge(m_done[(u + 1) % 4], 16 * (it + 1 + (u == 3)))
                        for h in range(G):
                            if more:
                                if kt < 3:
                                    score_t(u, kt + 1, h, n)
                                else:
                                    score_t((u + 1) % 4, 0, h, n + 1)
                            if ahead:
                                score(w, 2 * kt + h // 2, n + 2, h % 2)
                        weighted(u, kt, n)
                        if kt == 0:
                            o_back(n)
                        if kt == 1 and not (last and u == 3):
                            max_t(n + 1, (u + 1) % 2, n + 1)

            with pe.Fori(0, LOOPED) as it:
                steps(it, False)
            steps(LOOPED, True)
            pe.wait_ge(sm["o_norm"], STEPS)
            pe.wait_ge(sm["o_evac"], STEPS + 1)
            for q in range(QT):
                ins = pe.transpose(bank(7)[:, P * q:P * (q + 1)], oev[:, P * q:P * (q + 1)], ident)
            ins.then_inc(sm["ot_ready"], 1)

            pe.wait_ge(sm["wc_in"], 16)
            for i in range(4):
                ins = pe.transpose(bank(0)[:, P * i:P * (i + 1)], wc[:, W_WO + P * i:W_WO + P * (i + 1)], ident)
            ins.then_inc(sm["woT"], 1)
            pe.wait_ge(sm["woT_sb"], 1)
            for i in range(4):
                pe.matmul(bank(1 + i)[:, 0:D], woT_sb[:, i, :], wc[:, W_FWO:W_FWO + D], start=True, stop=True)
                ins = pe.matmul(bank(1 + i)[:, D:132], woT_sb[:, i, :], wc[:, W_FWG + 4 * i:W_FWG + 4 * (i + 1)],
                                start=True, stop=True)
            ins.then_inc(sm["fold_mm"], 1)

            def out_t(t):
                b, q = t // QT, t % QT
                if t == 1:
                    pe.wait_ge(sm["o_norm"], STEPS + 1)
                if t >= 2:
                    pe.wait_ge(sm["oT_sb"], t - 1)

                def tile(ty):
                    first = b * NG + 1
                    return o_sb[:, ty, q, first:first + NG, :].rearrange("p g c -> p (g c)")
                srcs = [tile(0), o_loc[:, 0, t, :], o_loc[:, 1, t, :], tile(1)]
                for i, src in enumerate(srcs):
                    ins = pe.transpose(bank(6 + t % 2)[:, P * i:P * (i + 1)], src, ident)
                ins.then_inc(sm["oT"], 1)

            pe.wait_ge(sm["o_norm"], STEPS + 1)
            pe.wait_ge(sm["loc_out"], 1)
            out_t(0)
            pe.wait_ge(sm["fold_sb"], 1)
            for t in range(NT):
                if t + 1 < NT:
                    out_t(t + 1)
                pe.wait_ge(sm["oT_sb"], t + 1)
                if t >= 3:
                    pe.wait_ge(sm["x1_done"], t - 2)
                a = 2 * (t % 3)
                for i in range(4):
                    ins = pe.matmul(ps[:, a + i // 2, 256 * (i % 2):256 * (i % 2) + 132], oT_sb[:, t % 2, i, :],
                                    wop[:, t // QT, i, :], start=True, stop=True)
                ins.then_inc(sm["p_mm"], 1)

            pe.wait_ge(sm["x1_done"], NT)
            for b in range(B):
                transposes(b, xh, sm["xT2"], sm["xh2_ready"], QT * b)
            for b in range(B):
                pe.wait_ge(sm["nx2"], B)
                for f in range(FT):
                    n = FT * b + f
                    if n >= 3:
                        pe.wait_ge(sm["u_ready"], n - 2)
                    pe.matmul(bank(2 * (n % 3)), wc[:, W_W1 + P * f:W_W1 + P * (f + 1)], nT[:, b, :], start=True, stop=True)
                    pe.matmul(bank(2 * (n % 3) + 1), wc[:, W_W3 + P * f:W_W3 + P * (f + 1)], nT[:, b, :],
                              start=True, stop=True).then_inc(sm["h_mm"], 1)
                    if b == 1 and f == 2:
                        ffn_out(pe, 0)
            ffn_out(pe, 1)

            pe.wait_ge(sm["u_ready"], B * FT)
            for b in range(B):
                transposes(b, xh, sm["xT3"], sm["xh3_ready"], QT * b)
            for b in range(B):
                pe.wait_ge(sm["nx3"], b + 1)
                pe.matmul(bank(6 + b), wc[:, W_K:W_K + D], nT[:, b, :], start=True, stop=True).then_inc(sm["k_mm"], 1)
                for t in range(QT):
                    ins = pe.matmul(ps[:, 2 + 2 * b + t // 2, 256 * (t % 2):256 * (t % 2 + 1)], nT[:, b, P * t:P * (t + 1)],
                                    wc[:, W_QV:W_QV + 256], start=True, stop=True)
                ins.then_inc(sm["qv_mm"], 1)
            for b in range(B):
                pe.wait_ge(sm["k_exp"], b + 1)
                for t in range(QT):
                    ins = pe.transpose(bank(b)[:, P * t:P * (t + 1)], kx[:, b, P * t:P * (t + 1)], ident)
                ins.then_inc(sm["kt_mm"], 1)
            for b in range(B):
                pe.wait_ge(sm["q_ready"], b + 1)
                pe.wait_ge(sm["qv_ready"], b + 1)
                for t in range(QT):
                    ins = pe.transpose(bank(2 + b)[:, P * t:P * (t + 1)], q_sb[:, QT * b + t, :], ident)
                ins.then_inc(sm["qT"], 1)
            for b in range(B):
                pe.wait_ge(sm["kt_sb"], b + 1)
                pe.wait_ge(sm["qv_ready"], B)
                for t in range(QT):
                    ins = pe.matmul(bank(4 + b)[:, 0:D], kt_sb[:, QT * b + t, :], v_sb[:, QT * b + t, :],
                                    start=t == 0, stop=t == QT - 1)
                ins.then_inc(sm["ctx_mm"], 1)
            for b in range(B):
                pe.wait_ge(sm["ctx_sb"], b + 1)
                pe.wait_ge(sm["qT_sb"], b + 1)
                for t in range(QT):
                    ins = pe.matmul(bank(6 + b)[:, P * t:P * (t + 1)], qT_sb[:, b, P * t:P * (t + 1)], ctx_sb[:, b, :],
                                    start=True, stop=True)
                ins.then_inc(sm["yl_mm"], 1)
            for b in range(B):
                transposes(b, xh, sm["xT4"], sm["xh4_ready"], QT * b)
            for b in range(B):
                pe.wait_ge(sm["u4"], b + 1)
                for t in range(QT):
                    ins = pe.matmul(bank(2 + b)[:, P * t:P * (t + 1)], t4[:, b, P * t:P * (t + 1)], wc[:, W_OUT:W_OUT + D],
                                    start=True, stop=True)
                ins.then_inc(sm["z_mm"], 1)


def _constants():
    import numpy as np
    bf = mybir.dt.np(BF16)
    tok = np.arange(S)
    tile, at = tok // P, tok % P
    kside = np.zeros((MROW - DATA, S), np.float32)
    qside = np.zeros((MROW - DATA, S), np.float32)
    for t in range(QT):
        s = np.sign(tile - t).astype(np.float32)
        kside[3 * t] = -s * P * (tile - t)
        kside[3 * t + 1] = -s * at
        kside[3 * t + 2] = s
        qside[3 * t] = tile == t
        qside[3 * t + 1] = tile == t
        qside[3 * t + 2] = (tile == t) * at
    stk_c = np.zeros((MROW - DATA, 4, 2, G, S), np.float32)
    for u in (0, 2):
        stk_c[:, u, 0] = kside[:, None, :]
        stk_c[:, u, 1] = qside[:, None, :]
    stk_o = np.zeros((3, G, 4, 2, G, S), np.float32)
    for h in range(G):
        stk_o[:, h, :, 0, h] = 1.0
    i = np.arange(P)
    diag = -np.abs(i[:, None] - i[None, :]).astype(np.float32)
    cst_bf = np.concatenate([np.eye(P, dtype=np.float32), diag], 1)
    hmask = (i[:, None] // DH == i[None, :] // DH).astype(np.float32)
    lmask = np.zeros((P, 3, NT), np.float32)
    for t in range(NT):
        if t % QT == 0:
            lmask[0, 0, t] = -1e9
        if t % QT == QT - 1:
            lmask[P - 1, 2, t] = -1e9
    return (np.eye(P, dtype=np.float32), hmask, lmask.reshape(P, 3 * NT), cst_bf.astype(bf),
            stk_c.reshape(MROW - DATA, -1).astype(bf), stk_o.reshape(3 * G, -1).astype(bf))


def kernel(**inputs):
    import numpy as np
    import concourse.bacc as bacc
    from concourse.bass_utils import run_bass_kernel_spmd as run

    a = {k: np.asarray(v) for k, v in inputs.items()}
    l0 = {k[8:]: v for k, v in a.items() if k.startswith("L0_cond_")}
    l1 = {k[8:]: v for k, v in a.items() if k.startswith("L1_cond_")}
    eye, hmask, lmask, cst_bf, stk_c, stk_o = _constants()

    def block(w, j):
        return w[..., P * j:P * (j + 1)]

    aw, ab, ew, eb = l0["ada_w"], l0["ada_b"], l1["emb_W"], l1["emb_b"]
    cond = a["cond_1024"]
    cols = np.stack([l0["ln1_g"], l0["ln2_g"], l1["sn_g"], l0["ln1_b"], l0["ln2_b"], l1["sn_b"], l1["norm_g"], l1["norm_b"],
                     l1["bk"], cond[0], cond[1], block(ab, 1), block(ab, 4), block(eb, 0), block(ab, 0), block(ab, 3),
                     block(eb, 1)], 1)
    pk_a = np.concatenate([cols, block(aw, 1), block(aw, 4), block(ew, 0), block(aw, 0), block(aw, 3), block(ew, 1),
                           block(aw, 2), block(aw, 5), eye, hmask, lmask], 1)
    pk_b = np.concatenate([l0["grid_wk"], l0["grid_wq"], l0["sem_wk"], l0["sem_wq"],
                           l0["reg_wq"], l0["ent_wq"], l0["grid_wv"], l0["sem_wv"],
                           l0["reg_wk"], l0["reg_wv"], l0["ent_wk"], l0["ent_wv"]], 1)
    fwg = l0["fus_wg"].reshape(4, P, 4).transpose(1, 0, 2).reshape(P, 16)
    w2 = l0["ffn_w2"].reshape(FT, P, D).transpose(1, 0, 2).reshape(P, FT * D)
    pk_c = np.concatenate([l0["grid_wo"], l0["reg_wo"], l0["ent_wo"], l0["sem_wo"], l0["fus_wo"], fwg,
                           l0["ffn_w1"], l0["ffn_w3"], w2, l1["Wq"], l1["Wv"], l1["Wk"], l1["out_W"]], 1)
    row = np.concatenate([block(ab, 2), block(ab, 5), l1["bq"], l1["bv"], l1["out_b"], cond[0], cond[1], l0["fus_bg"]])
    arrays = {"x": a["x"], "pk_a": pk_a, "pk_b": pk_b, "pk_c": pk_c, "rows": np.broadcast_to(row, (P, R_END)),
              "cst_bf": cst_bf, "stk_c": stk_c, "stk_o": stk_o}
    arrays = {k: np.ascontiguousarray(v) for k, v in arrays.items()}
    nc = bacc.Bacc("TRN2", target_bir_lowering=False, num_devices=1)
    args = [nc.dram_tensor(k, v.shape, mybir.dt.from_np(v.dtype), kind="ExternalInput").ap() for k, v in arrays.items()]
    args.append(nc.dram_tensor("out", (B, S, D), F32, kind="ExternalOutput").ap())
    program(nc, *args)
    r = run(nc, [arrays], core_ids=[0])
    return r.results[0]["out"]
```

```python
from contextlib import ExitStack

import concourse.bass as bass
from concourse import mybir

F32 = mybir.dt.float32
BF16 = mybir.dt.bfloat16
ALU = mybir.AluOpType
ACT = mybir.ActivationFunctionType
AX = mybir.AxisListType

P = 128
B, S, D = 2, 512, 128
T = B * S
NT = T // P
QT = S // P
H, DH = 16, 8
G = 4
NG = H // G
F = 512
FT = F // P
SCALE = 1.0 / DH ** 0.5
TERMS = 6
DATA = TERMS * DH
MROW = 64
OUTS = 16 * 2 * 3
ROWS = MROW + 3 * G
STEPS = 2 * B * NG
VW = 32
LOOPED = STEPS // 4 - 1

C_GAIN, C_BIAS, C_NG, C_NB, C_BK, C_COND, C_ADA, C_END = 0, 3, 6, 7, 8, 9, 11, 17
A_W, A_GW, A_ID, A_HM, A_LM, A_END = 17, 17 + 768, 17 + 1024, 17 + 1152, 17 + 1280, 17 + 1304
R_G, R_BQ, R_BV, R_OB, R_COND, R_FB, R_END = 0, 256, 384, 512, 640, 896, 900
W_WO, W_FWO, W_FWG, W_W1, W_W3, W_W2, W_QV, W_K, W_OUT, W_END = (
    0, 512, 640, 656, 1168, 1680, 2192, 2448, 2576, 2704)


def program(nc, x, pk_a, pk_b, pk_c, rows, cst_bf, stk_c, stk_o, out):
    ctx = ExitStack()
    with ctx:
        def sb(name, shape, dt=F32):
            return ctx.enter_context(nc.sbuf_tensor(name, shape, dt))

        def sem(name):
            return ctx.enter_context(nc.semaphore(name))

        qk_dram = [[nc.dram_tensor(f"qk_{t}{s}", [B * NG, G, DH, TERMS, S], BF16).ap() for s in "kq"] for t in "gs"]
        v_dram = [nc.dram_tensor(f"v_{t}", [B * NG, P, QT * G * VW], F32).ap() for t in "gs"]

        x_sb = sb("x_sb", [P, NT, D])
        pa = sb("pa", [P, A_END])
        wb = sb("wb", [P, 1536])
        wc = sb("wc", [P, W_END])
        rw = sb("rw", [P, R_END])
        cb = sb("cb", [P, 2 * P], BF16)
        stk = sb("stk", [ROWS, 4, 2, G, S], BF16)
        nxp = sb("nxp", [P, B, S + 2])
        nxs = sb("nxs", [P, B, S])
        v32 = sb("v32", [P, 2, B, NG, QT, G * VW])
        vb = sb("vb", [P, 4, QT, G * VW])
        parts_mem = sb("parts", [P, 4, 3, B, S], BF16)
        kv = sb("kv", [P, 5, 2, NT, D])
        ql = sb("ql", [P, 2, NT, D])
        o_sb = sb("o_sb", [P, 2, QT, B * NG + 1, G * DH])
        oev = sb("oev", [P, S])
        mneg = sb("mneg", [P, 2, G * QT])
        mres = sb("mres", [P, 2, G * QT])
        mprt = sb("mprt", [P, 2, QT, 3, G], BF16)
        mrow = sb("mrow", [G * 3, 2, S], BF16)
        orec = sb("orec", [P, QT * G])
        mv = sb("mv", [P, 4, NT, 2])
        bst = sb("bst", [P, NT, 6])
        rstd = sb("rstd", [P, 4, NT])
        mhalf = sb("mhalf", [P, NT])
        sil = sb("sil", [P, 4, B])
        silb = sb("silb", [P, B, P])
        ada = sb("ada", [P, 6, B])
        ga = sb("ga", [P, 3, B])
        ba = sb("ba", [P, 3, B])
        gr = sb("gr", [P, B, 2 * D])
        ls = sb("ls", [P, 5 * NT * H])
        lsm = sb("lsm", [P, 2, NT * H])
        wop = sb("wop", [P, B, 4, D + 4])

        a_buf = parts_mem[:, :, :, :, :].rearrange("p a b c d -> p (a b c d)")[:, 0:8192].bitcast(F32) \
            .rearrange("p (n g s) -> p n g s", n=2, g=G)
        kvf = kv[:, :, :, :, :].rearrange("p a b c d -> p (a b c d)")
        resid = [kvf[:, 0:1024], kvf[:, 1024:2048]]
        xh1 = kvf[:, 2048:3072].rearrange("p (t d) -> p t d", t=NT)
        v32f = v32[:, :, :, :, :, :].rearrange("p a b c d e -> p (a b c d e)")
        prod = v32f[:, 0:5120]
        o_loc = v32f[:, 5120:7168].rearrange("p (a t d) -> p a t d", a=2, t=NT)
        woT_sb = oev[:, :].rearrange("p (i c) -> p i c", i=4)
        ident = pa[:, A_ID:A_ID + P]
        hmask = pa[:, A_HM:A_HM + P]
        lmask = pa[:, A_LM:A_LM + 3 * NT]
        ident_b, diag_b = cb[:, 0:P], cb[:, P:2 * P]

        ps = ctx.enter_context(nc.psum_tensor("ps", [P, 8, 512], F32))


        def bank(i):
            return ps[:, i, :]

        names = """x_in pa_in wb_in wo_in wc_in rw_in cst_in grid0_out sem0_out grid1_out sem1_out v_out out_done
          dve_chain act_chain gp_chain tanh_c siluT silb_ready ada_mm gr_mm ga_ready gr_ready var1 rstd1 xh1_ready xT1
          nx_ready nxs_ready pads qk_mm part1 resid1 part2 part3 tok_mm tok_act ones_set
          primed s_ready s_max split_step m_split mt_ready mt_evac st_ready st_free a_free o_evac ot_ready o_norm o_rec
          loc_scores loc_max loc_soft loc_exp loc_sum loc_inv loc_out
          woT woT_sb fold_mm fold_sb oT oT_sb p_mm logits gate_exp x1_done
          var2 rstd2 xh2_ready xT2 nx2 h_mm h_tanh h_v u_ready y_mm x2_done
          var3 rstd3 xh3_ready xT3 nx3 qv_mm k_mm q_max qv_ready q_exp q_ready k_max k_exp kt_mm kt_sb ctx_mm ctx_sb qT qT_sb
          yl_mm var4 rstd4 xh4_ready xT4 h4 h4_tanh u4 z_mm o_ready gb_ready""".split()
        sm = {n: sem(n) for n in names}
        load_done = [sem(f"load_done{u}") for u in range(4)]
        v_done = [sem(f"v_done{u}") for u in range(4)]
        m_done = [sem(f"m_done{u}") for u in range(4)]

        def chainer(eng, s):
            count = [0]

            def link(ins):
                count[0] += 1
                ins.then_inc(s, 1)
                eng.wait_ge(s, count[0])
            return link

        block = ctx.enter_context(nc.Block())
        nxb = nxp[:, :, 1:S + 1]
        qk_out = [[sm["grid0_out"], sm["grid1_out"]], [sm["sem0_out"], sm["sem1_out"]]]

        @block.sync
        def _(sp):
            sp.dma_start(x_sb[:, :, :], x.rearrange("b (t p) d -> p (b t) d", p=P)).then_inc(sm["x_in"], 16)
            sp.dma_start(pa[:, :], pk_a).then_inc(sm["pa_in"], 16)
            sp.dma_start(wb[:, :], pk_b).then_inc(sm["wb_in"], 16)
            stk_r = stk[:, :, :, :, :].rearrange("r a b c d -> r (a b c d)")
            sp.dma_start(stk_r[DATA:MROW, :], stk_c).then_inc(sm["cst_in"], 16)
            sp.dma_start(stk_r[MROW:ROWS, :], stk_o).then_inc(sm["cst_in"], 16)
            sp.dma_start(cb[:, :], cst_bf).then_inc(sm["cst_in"], 16)
            sp.dma_start(rw[:, :], rows).then_inc(sm["rw_in"], 16)

            def parts_out(ty, b):
                for side in range(2):
                    sp.wait_ge(sm["part3"], 2 * ty + side + 1)
                    dst = qk_dram[ty][side].rearrange("(b g) h d j q -> b (g h d) j q", b=B)[b]
                    for j0, n, first in ((0, 3, 0), (3, 2, 1 - side), (5, 1, 2 - 2 * side)):
                        own = n if side else 1
                        src = parts_mem[:, 2 * ty + side, first:first + own, b, :]
                        sp.dma_start(dst[:, j0:j0 + n, :], src if side else src.broadcast_to([P, n, S])) \
                            .then_inc(qk_out[ty][b], 16)

            def v_to_dram():
                sp.wait_ge(sm["tok_act"], 3 * NT)
                sp.wait_ge(sm["ones_set"], 1)
                for ty in range(2):
                    for bb in range(B):
                        dst = v_dram[ty].rearrange("(b g) p c -> b p g c", b=B)[bb]
                        src = v32[:, ty, bb].rearrange("p g k c -> p g (k c)")
                        sp.dma_start(dst, src).then_inc(sm["v_out"], 16)

            def load_v(u, bg):
                sp.dma_start(vb[:, u, :, :].rearrange("p k c -> p (k c)"),
                             v_dram[u % 2][bass.ds(bg, 1)].rearrange("o p c -> (o p) c")).then_inc(v_done[u], 16)

            def load(u, bg):
                for side in range(2):
                    src = qk_dram[u % 2][side].rearrange("n h d j q -> n (d j) h q")
                    sp.dma_start(stk[0:DATA, u, side, :, :], src[bass.ds(bg, 1)].rearrange("o r h q -> (o r) h q")) \
                        .then_inc(load_done[u], 16)
                sp.dma_start(stk[MROW:ROWS, u, 1, :, :].rearrange("r h q -> r (h q)"), stk_o[:, G * S:2 * G * S]) \
                    .then_inc(load_done[u], 16)

            def max_rows(step, u):
                sp.wait_ge(sm["mt_evac"], step + 1)
                sp.dma_start(stk[MROW:ROWS, u, 1, :, :],
                             mrow[:, u % 2, :].unsqueeze(1).broadcast_to([3 * G, G, S])).then_inc(m_done[u], 16)

            for ty in range(2):
                parts_out(ty, 0)
            for u in range(2):
                sp.wait_ge(qk_out[u][0], OUTS)
                load(u, 0)
            v_to_dram()
            sp.dma_start(wc[:, 0:W_W1], pk_c[:, 0:W_W1]).then_inc(sm["wo_in"], 16)
            for u in range(2, 4):
                load(u, 1)
            for ty in range(2):
                parts_out(ty, 1)
            sp.wait_ge(sm["v_out"], 16 * 2 * B)
            for u in range(4):
                load_v(u, u // 2)
            max_rows(0, 0)
            for b in range(2):
                sp.wait_ge(qk_out[b][1], OUTS)
            sp.dma_start(wc[:, W_W1:W_END], pk_c[:, W_W1:W_END]).then_inc(sm["wc_in"], 16)

            def steps(it, last):
                for u in range(4):
                    n = 4 * it + u
                    if not (last and u == 3):
                        max_rows(n + 1, (u + 1) % 4)
                    if not last:
                        sp.wait_ge(sm["a_free"], 2 + 4 * (n + 1))
                        load(u, 2 * (it + 1) + u // 2)
                        load_v(u, 2 * (it + 1) + u // 2)

            with sp.Fori(0, LOOPED) as it:
                steps(it, False)
            steps(LOOPED, True)

            for b in range(B):
                sp.wait_ge(sm["o_ready"], b + 1)
                sp.dma_start(out[b].rearrange("(t p) d -> p t d", p=P), x_sb[:, QT * b:QT * (b + 1), :]) \
                    .then_inc(sm["out_done"], 16)
            sp.wait_ge(sm["out_done"], 32)

        @block.gpsimd
        def _(gp):
            link = chainer(gp, sm["gp_chain"])
            link(gp.memset(mhalf[:, :], -0.5))
            gp.memset(nxp[:, :, 0:1], 0.0)
            gp.memset(nxp[:, :, S + 1:S + 2], 0.0).then_inc(sm["pads"], 1)
            gp.memset(v32f, 1.0).then_inc(sm["ones_set"], 1)

            def inv_std(k, eps, t0, t1, var, ready):
                gp.wait_ge(*var)
                link(gp.tensor_scalar(rstd[:, k, t0:t1], mv[:, k, t0:t1, 1], eps, None, ALU.add))
                gp.tensor_tensor(rstd[:, k, t0:t1], rstd[:, k, t0:t1], mhalf[:, t0:t1], ALU.pow).then_inc(ready, 1)

            inv_std(0, 1e-6, 0, NT, (sm["var1"], 1), sm["rstd1"])

            gp.wait_ge(sm["nx_ready"], 2)
            for par in range(2):
                gp.tensor_copy(nxs[:, :, par::2], nxb[:, :, 1 - par::2]).then_inc(sm["nxs_ready"], 1)

            l5 = ls[:, :].rearrange("p (n c) -> p n c", n=5)
            gp.wait_ge(sm["tok_act"], 6 * NT)
            gp.wait_ge(sm["v_out"], 16 * 2 * B)
            pv = prod.rearrange("p (n t d) -> p n t d", n=5, t=NT)
            for n in range(5):
                ins = gp.tensor_tensor(pv[:, n], kv[:, n, 0], ql[:, 0 if n < 3 else 1], ALU.mult)
            link(ins)
            pg = prod.rearrange("p (g d) -> p g d", d=DH)
            link(gp.tensor_tensor(pg[:, :, 0:4], pg[:, :, 0:4], pg[:, :, 4:8], ALU.add))
            link(gp.tensor_tensor(pg[:, :, 0:2], pg[:, :, 0:2], pg[:, :, 2:4], ALU.add))
            link(gp.tensor_tensor(ls[:, :].unsqueeze(2), pg[:, :, 0:1], pg[:, :, 1:2], ALU.add))
            lr = ls[:, 0:3 * NT * H].rearrange("p (n h) -> p n h", h=H)
            gp.tensor_tensor(lr, lr, lmask.unsqueeze(2).broadcast_to([P, 3 * NT, H]), ALU.add).then_inc(sm["loc_scores"], 1)
            gp.wait_ge(sm["loc_max"], 1)
            gp.tensor_tensor(l5[:, 0:3, :], l5[:, 0:3, :], lsm[:, 0:1, :].broadcast_to([P, 3, NT * H]), ALU.subtract)
            gp.tensor_tensor(l5[:, 3:5, :], l5[:, 3:5, :], lsm[:, 1:2, :].broadcast_to([P, 2, NT * H]), ALU.subtract) \
                .then_inc(sm["loc_soft"], 1)
            gp.wait_ge(sm["loc_exp"], 1)
            link(gp.tensor_tensor(lsm[:, :, :], l5[:, 0:4:3, :], l5[:, 1:5:3, :], ALU.add))
            gp.tensor_tensor(lsm[:, 0, :], lsm[:, 0, :], l5[:, 2, :], ALU.add).then_inc(sm["loc_sum"], 1)
            gp.wait_ge(sm["loc_inv"], 4)
            gp.tensor_tensor(l5[:, 0:3, :], l5[:, 0:3, :], lsm[:, 0:1, :].broadcast_to([P, 3, NT * H]), ALU.mult)
            link(gp.tensor_tensor(l5[:, 3:5, :], l5[:, 3:5, :], lsm[:, 1:2, :].broadcast_to([P, 2, NT * H]), ALU.mult))
            for n in range(5):
                w = ls[:, n * NT * H:(n + 1) * NT * H].unsqueeze(2).broadcast_to([P, NT * H, DH])
                ins = gp.tensor_tensor(pv[:, n].rearrange("p t (h d) -> p (t h) d", d=DH),
                                       kv[:, n, 1].rearrange("p t (h d) -> p (t h) d", d=DH), w, ALU.mult)
            link(ins)
            link(gp.tensor_tensor(pv[:, 0], pv[:, 0], pv[:, 1], ALU.add))
            gp.tensor_tensor(o_loc[:, 0], pv[:, 0], pv[:, 2], ALU.add)
            gp.tensor_tensor(o_loc[:, 1], pv[:, 3], pv[:, 4], ALU.add).then_inc(sm["loc_out"], 1)

            inv_std(1, 1e-6, 0, NT, (sm["var2"], 1), sm["rstd2"])
            for b in range(B):
                inv_std(2, 1e-5, QT * b, QT * (b + 1), (sm["var3"], b + 1), sm["rstd3"])
            for b in range(B):
                inv_std(3, 1e-5, QT * b, QT * (b + 1), (sm["var4"], b + 1), sm["rstd4"])

        oT_sb = kvf[:, 1568:2592].rearrange("p (n i c) -> p n i c", n=2, i=4)
        xh = kvf[:, 2592:3616].rearrange("p (t d) -> p t d", t=NT)
        nT = kvf[:, 3616:4640].rearrange("p (b s) -> p b s", b=B)
        th = kvf[:, 4640:5664].rearrange("p (n s) -> p n s", n=2)
        hv = kvf[:, 5664:6688].rearrange("p (n s) -> p n s", n=2)
        q_sb = kvf[:, 6688:7712].rearrange("p (t d) -> p t d", t=NT)
        v_sb = kvf[:, 7712:8736].rearrange("p (t d) -> p t d", t=NT)
        ctx_sb = kvf[:, 8736:8992].rearrange("p (b d) -> p b d", b=B)
        kx = kvf[:, 8992:10016].rearrange("p (b s) -> p b s", b=B)
        u_sb = a_buf.rearrange("p n g s -> p (n g s)").rearrange("p (f b s) -> p f b s", f=FT, b=B)
        kt_sb = v32f[:, 0:1024].rearrange("p (t d) -> p t d", t=NT)
        qT_sb = v32f[:, 1024:2048].rearrange("p (b s) -> p b s", b=B)
        hT = v32f[:, 2048:3072].rearrange("p (b s) -> p b s", b=B)
        t4 = v32f[:, 3072:4096].rearrange("p (b s) -> p b s", b=B)
        xgb = v32f[:, 4096:5120].rearrange("p (t d) -> p t d", t=NT)
        rowmx = ql[:, 0].rearrange("p t d -> p (t d)")
        gate = rowmx[:, 0:96].rearrange("p (t c) -> p t c", t=NT)
        qmx = rowmx[:, 96:224].rearrange("p (b c) -> p b c", b=B)
        qsm = rowmx[:, 224:352].rearrange("p (b c) -> p b c", b=B)
        ksm = rowmx[:, 352:368].rearrange("p (b c) -> p b c", b=B)
        cgb = rowmx[:, 368:624].rearrange("p (b d) -> p b d", b=B)
        cgh = rowmx[:, 624:880].rearrange("p (b d) -> p b d", b=B)
        gbs = ql[:, 1].rearrange("p t d -> p (t d)")

        def max_evac(act, step, par):
            act.wait_ge(sm["mt_ready"], step + 1)
            act.activation(mrow[:, par, :], bank(7)[0:3 * G, 0:S // 2].bitcast(BF16), ACT.Copy).then_inc(sm["mt_evac"], 1)

        def gate_exp(act, t):
            act.wait_ge(sm["logits"], t + 1)
            act.activation(gate[:, t, 4:8], gate[:, t, 0:4], ACT.Exp, bias=gate[:, t, 8:9],
                           accum_out=gate[:, t, 9:10]).then_inc(sm["gate_exp"], 1)

        @block.scalar
        def _(act):
            link = chainer(act, sm["act_chain"])
            act.sem_inc(sm["st_free"], 2)
            act.wait_ge(sm["pa_in"], 16)
            act.activation(sil[:, 0, :], pa[:, C_COND:C_COND + B], ACT.Tanh, scale=0.5).then_inc(sm["tanh_c"], 1)
            act.wait_ge(sm["ga_ready"], 1)
            act.wait_ge(sm["pads"], 1)
            for b in range(B):
                act.wait_ge(sm["xT1"], b + 1)
                act.activation(nxb[:, b, :], bank(b), ACT.Identity, scale=ga[:, 0, b:b + 1],
                               bias=ba[:, 0, b:b + 1]).then_inc(sm["nx_ready"], 1)
            for n in range(4):
                act.wait_ge(sm["qk_mm"], n + 1)
                src = ps[:, 4 + 2 * (n % 2):6 + 2 * (n % 2), :]
                act.activation(parts_mem[:, n, 0], src, ACT.Copy, scale=SCALE if n % 2 else 1.0).then_inc(sm["part1"], 1)
                act.wait_ge(sm["resid1"], n + 1)
                act.activation(parts_mem[:, n, 1], resid[n % 2].rearrange("p (b s) -> p b s", b=B), ACT.Copy) \
                    .then_inc(sm["part2"], 1)
            act.wait_ge(sm["ones_set"], 1)
            for t in range(NT):
                act.wait_ge(sm["tok_mm"], t + 1)
                bk = bank(4 + t % 4)
                act.activation(ql[:, :, t, :], bk[:, 0:256].rearrange("p (a d) -> p a d", a=2), ACT.Copy, scale=SCALE) \
                    .then_inc(sm["tok_act"], 1)
                for ty in range(2):
                    dst = v32[:, ty, t // QT, :, t % QT, :].rearrange("p g (h c) -> p g h c", h=G)[:, :, :, 0:DH]
                    src = bk[:, 256 + P * ty:384 + P * ty].rearrange("p (g h c) -> p g h c", g=NG, h=G)
                    act.activation(dst, src, ACT.Copy).then_inc(sm["tok_act"], 1)
            act.wait_ge(sm["part3"], 4)
            for j in range(3 * NT):
                act.wait_ge(sm["tok_mm"], NT + j + 1)
                src = bank(2 + j % 4)
                if j % 3 < 2:
                    dst = kv[:, 1 - j % 3:4 - j % 3:2, :, j // 3, :]
                    act.activation(dst, src.rearrange("p (n a d) -> p n a d", n=2, a=2), ACT.Copy).then_inc(sm["tok_act"], 1)
                else:
                    act.activation(kv[:, 4, :, j // 3, :], src[:, 0:256].rearrange("p (a d) -> p a d", a=2), ACT.Copy) \
                        .then_inc(sm["tok_act"], 1)
                if j == 14:
                    act.wait_ge(sm["woT"], 1)
                    act.activation(woT_sb, bank(7).rearrange("p (i c) -> p i c", i=4), ACT.Copy).then_inc(sm["woT_sb"], 1)
                if j == 17:
                    max_evac(act, 0, 0)

            def o_evac(n):
                act.wait_ge(sm["a_free"], 4 * n + 2)
                act.wait_ge(sm["ot_ready"], n + 1)
                act.activation(oev[:, :], bank(6), ACT.Copy).then_inc(sm["o_evac"], 1)

            def steps(it, last):
                for u in range(4):
                    n = 4 * it + u
                    for kt in range(QT):
                        act.wait_ge(sm["a_free"], 4 * n + kt + 1)
                        for p in range(2):
                            act.wait_ge(sm["st_ready"], 8 * n + 2 * kt + p + 1)
                            act.activation(a_buf[:, kt % 2, 2 * p:2 * p + 2, :], ps[:, 2 + 2 * p:4 + 2 * p, :], ACT.Exp) \
                                .then_inc(sm["st_free"], 1)
                            if kt == 0 and p == 1:
                                o_evac(n)
                            if kt == 2 and p == 0 and not (last and u == 3):
                                max_evac(act, n + 1, (u + 1) % 2)
                        if last and u == 0 and kt == 1:
                            act.wait_ge(sm["loc_soft"], 1)
                            act.activation(ls[:, :], ls[:, :], ACT.Exp).then_inc(sm["loc_exp"], 1)

            act.wait_ge(sm["grid1_out"], OUTS)
            act.wait_ge(sm["sem1_out"], OUTS)
            act.wait_ge(sm["primed"], 1)
            with act.Fori(0, LOOPED) as it:
                steps(it, False)
            steps(LOOPED, True)
            o_evac(STEPS)

            act.wait_ge(sm["loc_out"], 1)
            for t in range(NT):
                act.wait_ge(sm["oT"], t + 1)
                act.activation(oT_sb[:, t % 2], bank(6 + t % 2).rearrange("p (i c) -> p i c", i=4), ACT.Copy) \
                    .then_inc(sm["oT_sb"], 1)
                if t >= 1:
                    gate_exp(act, t - 1)
            gate_exp(act, NT - 1)
            for b in range(B):
                act.wait_ge(sm["xT2"], b + 1)
                act.activation(nT[:, b, :], bank(b), ACT.Identity, scale=ga[:, 1, b:b + 1],
                               bias=ba[:, 1, b:b + 1]).then_inc(sm["nx2"], 1)
            for n in range(B * FT):
                act.wait_ge(sm["h_mm"], n + 1)
                if n >= 2:
                    act.wait_ge(sm["h_v"], n - 1)
                act.activation(th[:, n % 2], bank(2 * (n % 3)), ACT.Tanh, scale=0.5).then_inc(sm["h_tanh"], 1)
            for b in range(B):
                act.wait_ge(sm["xT3"], b + 1)
                act.activation(nT[:, b, :], bank(b), ACT.Identity, scale=pa[:, C_NG:C_NG + 1],
                               bias=pa[:, C_NB:C_NB + 1]).then_inc(sm["nx3"], 1)
            for b in range(B):
                act.wait_ge(sm["k_max"], b + 1)
                act.activation(kx[:, b, :], bank(6 + b), ACT.Exp, bias=ksm[:, b, 2:3],
                               accum_out=ksm[:, b, 3:4]).then_inc(sm["k_exp"], 1)
                act.wait_ge(sm["q_max"], b + 1)
                qb = q_sb[:, QT * b:QT * (b + 1), :]
                act.activation(qb, qb, ACT.Exp).then_inc(sm["q_exp"], 1)
            for b in range(B):
                act.wait_ge(sm["kt_mm"], b + 1)
                act.activation(kt_sb[:, QT * b:QT * (b + 1), :], bank(b).rearrange("p (t d) -> p t d", t=QT), ACT.Copy) \
                    .then_inc(sm["kt_sb"], 1)
            for b in range(B):
                act.wait_ge(sm["qT"], b + 1)
                act.activation(qT_sb[:, b, :], bank(2 + b), ACT.Copy).then_inc(sm["qT_sb"], 1)
            for b in range(B):
                act.wait_ge(sm["xT4"], b + 1)
                act.activation(hT[:, b, :], bank(b), ACT.Identity, scale=ga[:, 2, b:b + 1],
                               bias=ba[:, 2, b:b + 1]).then_inc(sm["h4"], 1)
                act.wait_ge(sm["h4"], b + 1)
                act.activation(t4[:, b, :], hT[:, b, :], ACT.Tanh, scale=0.5).then_inc(sm["h4_tanh"], 1)

        @block.vector
        def _(dve):
            link = chainer(dve, sm["dve_chain"])

            def stats(k, t, src):
                link(dve.bn_stats(bst[:, t, :], src))
                return dve.bn_aggr(mv[:, k, t, :], bst[:, t, :])

            def normalise(k, t, dst, src):
                return dve.tensor_scalar(dst, src, mv[:, k, t, 0:1], rstd[:, k, t:t + 1], ALU.subtract, ALU.mult)

            dve.wait_ge(sm["x_in"], 16)
            for t in range(NT):
                ins = dve.bn_stats(bst[:, t, :], x_sb[:, t, :])
            link(ins)
            for t in range(NT):
                ins = dve.bn_aggr(mv[:, 0, t, :], bst[:, t, :])
            ins.then_inc(sm["var1"], 1)
            dve.wait_ge(sm["tanh_c"], 1)
            link(dve.scalar_tensor_tensor(sil[:, 1, :], sil[:, 0, :], 1.0, pa[:, C_COND:C_COND + B], ALU.add, ALU.mult))
            dve.tensor_scalar(sil[:, 2, :], sil[:, 1, :], 0.5, None, ALU.mult).then_inc(sm["siluT"], 1)
            dve.wait_ge(sm["siluT"], 1)
            dve.tensor_copy(silb[:, :, :], sil[:, 2, :].unsqueeze(2).broadcast_to([P, B, P])).then_inc(sm["silb_ready"], 1)
            dve.wait_ge(sm["var1"], 1)
            dve.wait_ge(sm["rstd1"], 1)
            for t in range(NT):
                normalise(0, t, xh1[:, t, :], x_sb[:, t, :]).then_inc(sm["xh1_ready"], 1)
            dve.wait_ge(sm["ada_mm"], 1)
            link(dve.tensor_tensor(ada[:, :, :], bank(2)[:, 0:12].rearrange("p (j b) -> p j b", b=B),
                                   pa[:, C_ADA:C_ADA + 6].unsqueeze(2).broadcast_to([P, 6, B]), ALU.add))
            sc = ada[:, 0:3, :]
            dve.scalar_tensor_tensor(ga[:, :, :], sc, 1.0,
                                     pa[:, C_GAIN:C_GAIN + 3].unsqueeze(2).broadcast_to([P, 3, B]), ALU.add, ALU.mult)
            link(dve.scalar_tensor_tensor(ba[:, :, :], sc, 1.0,
                                          pa[:, C_BIAS:C_BIAS + 3].unsqueeze(2).broadcast_to([P, 3, B]), ALU.add, ALU.mult))
            dve.tensor_tensor(ba[:, :, :], ba[:, :, :], ada[:, 3:6, :], ALU.add).then_inc(sm["ga_ready"], 1)
            for n in range(4):
                src = ps[:, 4 + 2 * (n % 2):6 + 2 * (n % 2), :]
                r = resid[n % 2].rearrange("p (b s) -> p b s", b=B)
                dve.wait_ge(sm["part1"], n + 1)
                dve.scalar_tensor_tensor(r, src, SCALE if n % 2 else 1.0, parts_mem[:, n, 0], ALU.mult, ALU.subtract) \
                    .then_inc(sm["resid1"], 1)
                dve.wait_ge(sm["resid1"], n + 1)
                dve.wait_ge(sm["part2"], n + 1)
                dve.tensor_tensor(parts_mem[:, n, 2], r, parts_mem[:, n, 1], ALU.subtract).then_inc(sm["part3"], 1)
            dve.wait_ge(sm["gr_mm"], 1)
            dve.wait_ge(sm["rw_in"], 16)
            link(dve.tensor_tensor(gr[:, :, :], bank(3).rearrange("p (b c) -> p b c", b=B),
                                   rw[:, R_G:R_G + 256].unsqueeze(1).broadcast_to([P, B, 256]), ALU.add))
            dve.tensor_scalar(gr[:, :, D:2 * D], gr[:, :, D:2 * D], 0.5, None, ALU.mult).then_inc(sm["gr_ready"], 1)
            def row_max(step, r, par):
                dve.wait_ge(sm["s_ready"], 16 * step + r + 1)
                dve.tensor_reduce(mneg[:, par, r:r + 1], bank(r % 2), AX.X, ALU.max, negate=True) \
                    .then_inc(sm["s_max"], 1)

            def split(step, par, k):
                m = mneg[:, par, :].rearrange("p (h q) -> p q h", h=G)
                r = mres[:, par, :].rearrange("p (h q) -> p q h", h=G)
                if k == 0:
                    dve.wait_ge(sm["s_max"], 16 * (step + 1))
                else:
                    dve.wait_ge(sm["split_step"], 4 * step + k)
                if k == 0:
                    dve.tensor_copy(mprt[:, par, :, 0, :], m).then_inc(sm["split_step"], 1)
                elif k == 1:
                    dve.tensor_tensor(r, m, mprt[:, par, :, 0, :], ALU.subtract).then_inc(sm["split_step"], 1)
                elif k == 2:
                    dve.tensor_copy(mprt[:, par, :, 1, :], r).then_inc(sm["split_step"], 1)
                elif k == 3:
                    dve.tensor_tensor(r, r, mprt[:, par, :, 1, :], ALU.subtract).then_inc(sm["split_step"], 1)
                else:
                    dve.tensor_copy(mprt[:, par, :, 2, :], r).then_inc(sm["m_split"], 1)

            def o_inv(n):
                t7 = bank(7).rearrange("p (n c) -> p n c", c=VW)
                dve.wait_ge(sm["ot_ready"], n + 2)
                dve.reciprocal(orec[:, :].unsqueeze(2), t7[:, :, DH:DH + 1]).then_inc(sm["o_rec"], 1)

            def o_norm(n, ty, slot):
                t4d = bank(7).rearrange("p (q h c) -> p q h c", q=QT, c=VW)
                dve.wait_ge(sm["o_rec"], n + 1)
                dst = o_sb[:, ty, :, bass.ds(slot, 1), :].rearrange("p q o (h d) -> p q (o h) d", d=DH)
                inv = orec[:, :].rearrange("p (q h) -> p q h", q=QT).unsqueeze(3).broadcast_to([P, QT, G, DH])
                dve.tensor_tensor(dst, t4d[:, :, :, 0:DH], inv, ALU.mult).then_inc(sm["o_norm"], 1)

            def fold():
                dve.wait_ge(sm["fold_mm"], 1)
                for i, n, bk in ((0, 3, 6), (3, 1, 7)):
                    src = bank(bk)[:, 0:n * (D + 4)].rearrange("p (i c) -> p i c", i=n)
                    for b in range(B):
                        dve.tensor_tensor(wop[:, b, i:i + n, 0:D], src[:, :, 0:D],
                                          gr[:, b:b + 1, 0:D].broadcast_to([P, n, D]), ALU.mult)
                    ins = dve.tensor_copy(wop[:, :, i:i + n, D:D + 4],
                                          src[:, :, D:D + 4].unsqueeze(1).broadcast_to([P, B, n, 4]))
                ins.then_inc(sm["fold_sb"], 1)
                dve.wait_ge(sm["fold_sb"], 1)
                dve.memset(bank(6), 1.0).then_inc(sm["primed"], 1)

            for step in range(2):
                for r in range(4 * G):
                    row_max(step, r, step)
                    if step == 1 and r < 5:
                        split(0, 0, r)
                    if step == 1 and r == 7:
                        fold()

            def steps(it, last):
                for u in range(4):
                    n = 4 * it + u
                    ahead = not (last and u >= 2)
                    for kt in range(QT):
                        for r in range(4 * kt, 4 * kt + 4):
                            if ahead:
                                row_max(n + 2, r, u % 2)
                            if r < 5 and not (last and u == 3):
                                split(n + 1, (u + 1) % 2, r)
                            if r == 4:
                                o_inv(n)
                            if r == 5:
                                o_norm(n, (u + 1) % 2, 2 * it + (u + 1) // 2)
                            if last and u == 1 and r % 4 == 3:
                                dve.wait_ge(sm["loc_sum"], 1)
                                c = slice(NT * H // 4 * kt, NT * H // 4 * (kt + 1))
                                dve.reciprocal(lsm[:, :, c], lsm[:, :, c]).then_inc(sm["loc_inv"], 1)

            with dve.Fori(0, LOOPED) as it:
                steps(it, False)
            l5 = ls[:, :].rearrange("p (n c) -> p n c", n=5)
            dve.wait_ge(sm["loc_scores"], 1)
            link(dve.tensor_tensor(lsm[:, :, :], l5[:, 0:4:3, :], l5[:, 1:5:3, :], ALU.max))
            dve.tensor_tensor(lsm[:, 0, :], lsm[:, 0, :], l5[:, 2, :], ALU.max).then_inc(sm["loc_max"], 1)
            steps(LOOPED, True)
            o_inv(STEPS)
            o_norm(STEPS, 1, B * NG)

            def p_out(t):
                a = 2 * (t % 3)
                return ps[:, a:a + 2, :].rearrange("p n (i c) -> p (n i) c", i=2)

            for t in range(NT + 1):
                if t < NT:
                    g = gate[:, t, :]
                    dve.wait_ge(sm["p_mm"], t + 1)
                    link(dve.tensor_reduce(g[:, 0:4], p_out(t)[:, :, D:132].rearrange("p i c -> p c i"), AX.X, ALU.add))
                    link(dve.tensor_tensor(g[:, 0:4], g[:, 0:4], rw[:, R_FB:R_FB + 4], ALU.add))
                    dve.tensor_reduce(g[:, 8:9], g[:, 0:4], AX.X, ALU.max, negate=True).then_inc(sm["logits"], 1)
                if t >= 1:
                    k = t - 1
                    g = gate[:, k, :]
                    dve.wait_ge(sm["gate_exp"], k + 1)
                    link(dve.reciprocal(g[:, 10:11], g[:, 9:10]))
                    link(dve.tensor_scalar(g[:, 0:4], g[:, 4:8], g[:, 10:11], None, ALU.mult))
                    for i in range(4):
                        ins = dve.scalar_tensor_tensor(x_sb[:, k, :], p_out(k)[:, i, 0:D], g[:, i:i + 1], x_sb[:, k, :],
                                                       ALU.mult, ALU.add)
                        if i < 3:
                            link(ins)
                    ins.then_inc(sm["x1_done"], 1)
                    dve.wait_ge(sm["x1_done"], k + 1)
                    ins = stats(1, k, x_sb[:, k, :])
            ins.then_inc(sm["var2"], 1)
            dve.wait_ge(sm["rstd2"], 1)
            dve.wait_ge(sm["var2"], 1)
            for t in range(NT):
                normalise(1, t, xh[:, t, :], x_sb[:, t, :]).then_inc(sm["xh2_ready"], 1)
            for b in range(B):
                for f in range(FT):
                    n = FT * b + f
                    dve.wait_ge(sm["h_tanh"], n + 1)
                    dve.scalar_tensor_tensor(hv[:, n % 2], th[:, n % 2], 1.0, bank(2 * (n % 3)), ALU.add, ALU.mult) \
                        .then_inc(sm["h_v"], 1)
                    dve.wait_ge(sm["h_v"], n + 1)
                    dve.tensor_tensor(u_sb[:, f, b, :], hv[:, n % 2], bank(2 * (n % 3) + 1), ALU.mult) \
                        .then_inc(sm["u_ready"], 1)
            for b in range(B):
                xb = x_sb[:, QT * b:QT * (b + 1), :]
                dve.wait_ge(sm["y_mm"], b + 1)
                yb = bank(6 + b).rearrange("p (t d) -> p t d", t=QT)
                hb = xh[:, QT * b:QT * (b + 1), :]
                link(dve.tensor_tensor(hb, yb, gr[:, b:b + 1, D:2 * D].broadcast_to([P, QT, D]), ALU.mult))
                dve.tensor_tensor(xb, xb, hb, ALU.add).then_inc(sm["x2_done"], 1)
                dve.wait_ge(sm["x2_done"], b + 1)
                for t in range(QT * b, QT * (b + 1)):
                    ins = dve.bn_stats(bst[:, t, :], x_sb[:, t, :])
                link(ins)
                for t in range(QT * b, QT * (b + 1)):
                    ins = dve.bn_aggr(mv[:, 2, t, :], bst[:, t, :])
                ins.then_inc(sm["var3"], 1)
            dve.tensor_scalar(cgh, rw[:, R_COND:R_COND + 256].rearrange("p (b d) -> p b d", b=B), 0.5, None, ALU.mult)
            link(dve.tensor_tensor(cgb, rw[:, R_COND:R_COND + 256].rearrange("p (b d) -> p b d", b=B),
                                   rw[:, R_OB:R_OB + P].unsqueeze(1).broadcast_to([P, B, D]), ALU.mult))
            for b in range(B):
                dve.wait_ge(sm["rstd3"], b + 1)
                dve.wait_ge(sm["var3"], b + 1)
                for t in range(QT * b, QT * (b + 1)):
                    normalise(2, t, xh[:, t, :], x_sb[:, t, :]).then_inc(sm["xh3_ready"], 1)
            for b in range(B):
                ins = dve.tensor_tensor(xgb[:, QT * b:QT * (b + 1), :], x_sb[:, QT * b:QT * (b + 1), :],
                                        cgb[:, b:b + 1, :].broadcast_to([P, QT, D]), ALU.add)
            ins.then_inc(sm["gb_ready"], 1)
            for b in range(B):
                k = ksm[:, b, :]
                dve.wait_ge(sm["k_mm"], b + 1)
                link(dve.tensor_reduce(k[:, 0:1], bank(6 + b), AX.X, ALU.max))
                link(dve.tensor_tensor(k[:, 1:2], k[:, 0:1], pa[:, C_BK:C_BK + 1], ALU.add))
                dve.tensor_tensor(k[:, 2:3], pa[:, C_BK:C_BK + 1], k[:, 1:2], ALU.subtract).then_inc(sm["k_max"], 1)
                dve.wait_ge(sm["qv_mm"], b + 1)
                qv = ps[:, 2 + 2 * b:4 + 2 * b, :].rearrange("p n (t c) -> p (n t) c", t=2)
                qb = q_sb[:, QT * b:QT * (b + 1), :]
                q8 = qb.rearrange("p t (h d) -> p (t h) d", d=DH)
                link(dve.tensor_tensor(qb, qv[:, :, 0:D], rw[:, R_BQ:R_BQ + P].unsqueeze(1).broadcast_to([P, QT, D]), ALU.add))
                dve.tensor_tensor(v_sb[:, QT * b:QT * (b + 1), :], qv[:, :, D:2 * D],
                                  rw[:, R_BV:R_BV + P].unsqueeze(1).broadcast_to([P, QT, D]), ALU.add) \
                    .then_inc(sm["qv_ready"], 1)
                link(dve.tensor_reduce(qmx[:, b, :], q8, AX.X, ALU.max))
                dve.tensor_tensor(q8, q8, qmx[:, b, :].unsqueeze(2).broadcast_to([P, QT * H, DH]), ALU.subtract) \
                    .then_inc(sm["q_max"], 1)
            for b in range(B):
                q8 = q_sb[:, QT * b:QT * (b + 1), :].rearrange("p t (h d) -> p (t h) d", d=DH)
                dve.wait_ge(sm["q_exp"], b + 1)
                link(dve.tensor_reduce(qsm[:, b, :], q8, AX.X, ALU.add))
                link(dve.reciprocal(qsm[:, b, :], qsm[:, b, :]))
                dve.tensor_tensor(q8, q8, qsm[:, b, :].unsqueeze(2).broadcast_to([P, QT * H, DH]), ALU.mult) \
                    .then_inc(sm["q_ready"], 1)
            for b in range(B):
                dve.wait_ge(sm["k_exp"], b + 1)
                link(dve.reciprocal(ksm[:, b, 4:5], ksm[:, b, 3:4]))
                dve.wait_ge(sm["ctx_mm"], b + 1)
                dve.scalar_tensor_tensor(ctx_sb[:, b, :], bank(4 + b)[:, 0:D], ksm[:, b, 4:5], hmask, ALU.mult, ALU.mult) \
                    .then_inc(sm["ctx_sb"], 1)
            for b in range(B):
                dve.wait_ge(sm["yl_mm"], b + 1)
                yb = bank(6 + b).rearrange("p (t d) -> p t d", t=QT)
                for t in range(QT):
                    ins = dve.bn_stats(bst[:, QT * b + t, :], yb[:, t, :])
                link(ins)
                for t in range(QT):
                    ins = dve.bn_aggr(mv[:, 3, QT * b + t, :], bst[:, QT * b + t, :])
                ins.then_inc(sm["var4"], 1)
            for b in range(B):
                yb = bank(6 + b).rearrange("p (t d) -> p t d", t=QT)
                dve.wait_ge(sm["rstd4"], b + 1)
                dve.wait_ge(sm["var4"], b + 1)
                for t in range(QT):
                    normalise(3, QT * b + t, xh[:, QT * b + t, :], yb[:, t, :]).then_inc(sm["xh4_ready"], 1)
            for b in range(B):
                dve.wait_ge(sm["h4_tanh"], b + 1)
                dve.scalar_tensor_tensor(t4[:, b, :], t4[:, b, :], 1.0, hT[:, b, :], ALU.add, ALU.mult) \
                    .then_inc(sm["u4"], 1)
            for b in range(B):
                dve.wait_ge(sm["z_mm"], b + 1)
                zb = bank(2 + b).rearrange("p (t d) -> p t d", t=QT)
                hb = xh[:, QT * b:QT * (b + 1), :]
                dve.wait_ge(sm["gb_ready"], 1)
                link(dve.tensor_tensor(hb, zb, cgh[:, b:b + 1, :].broadcast_to([P, QT, D]), ALU.mult))
                dve.tensor_tensor(x_sb[:, QT * b:QT * (b + 1), :], hb, xgb[:, QT * b:QT * (b + 1), :], ALU.add) \
                    .then_inc(sm["o_ready"], 1)

        def ffn_out(pe, b):
            pe.wait_ge(sm["u_ready"], FT * (b + 1))
            for t in range(QT):
                for f in range(FT):
                    ins = pe.matmul(bank(6 + b)[:, P * t:P * (t + 1)], u_sb[:, f, b, P * t:P * (t + 1)],
                                    wc[:, W_W2 + P * f:W_W2 + P * (f + 1)], start=f == 0, stop=f == FT - 1)
            ins.then_inc(sm["y_mm"], 1)

        @block.tensor
        def _(pe):
            pe.sem_inc(sm["ot_ready"], 1)
            pe.sem_inc(sm["a_free"], 2)
            pe.wait_ge(sm["pa_in"], 16)
            pe.wait_ge(sm["silb_ready"], 1)
            for j in range(6):
                ins = pe.matmul(bank(2)[:, 2 * j:2 * j + 2], pa[:, A_W + P * j:A_W + P * (j + 1)], sil[:, 2, :],
                                start=True, stop=True)
            ins.then_inc(sm["ada_mm"], 1)
            for b in range(B):
                ins = pe.matmul(bank(3)[:, 256 * b:256 * (b + 1)], silb[:, b, :], pa[:, A_GW:A_GW + 256],
                                start=True, stop=True)
            ins.then_inc(sm["gr_mm"], 1)

            def transposes(bk, src, dst, ready, base):
                for t in range(QT):
                    pe.wait_ge(ready, base + t + 1)
                    ins = pe.transpose(bank(bk)[:, P * t:P * (t + 1)], src[:, base + t, :], ident)
                ins.then_inc(dst, 1)

            for b in range(B):
                transposes(b, xh1, sm["xT1"], sm["xh1_ready"], QT * b)
            pe.wait_ge(sm["wb_in"], 16)
            pe.wait_ge(sm["nx_ready"], 2)
            for n in range(4):
                if n >= 2:
                    pe.wait_ge(sm["resid1"], n - 1)
                for b in range(B):
                    ins = pe.matmul(bank(4 + 2 * (n % 2) + b), wb[:, P * n:P * (n + 1)], nxb[:, b, :],
                                    start=True, stop=True)
                ins.then_inc(sm["qk_mm"], 1)

            def tokens(t, shift):
                b, q = t // QT, t % QT
                return nxp[:, b, 1 + shift + P * q:1 + shift + P * (q + 1)]

            for t in range(NT):
                if t < 4:
                    pe.wait_ge(sm["resid1"], 3 + t // 2)
                else:
                    pe.wait_ge(sm["tok_act"], 3 * (t - 3))
                pe.matmul(bank(4 + t % 4), tokens(t, 0), wb[:, 512:1024], start=True, stop=True).then_inc(sm["tok_mm"], 1)

            def local_product(j):
                t, k = j // 3, j % 3
                b, q = t // QT, t % QT
                pe.wait_ge(sm["tok_act"], 3 * NT + max(j - 3, 0))
                dst = bank(2 + j % 4)
                if k == 0:
                    ins = pe.matmul(dst, tokens(t, 0), wb[:, 1024:1536], start=True, stop=True)
                elif k == 1:
                    pe.matmul(dst[:, 0:256], tokens(t, -1), wb[:, 1024:1280], start=True, stop=True)
                    ins = pe.matmul(dst[:, 256:512], tokens(t, 1), wb[:, 1024:1280], start=True, stop=True)
                else:
                    ins = pe.matmul(dst[:, 0:256], nxs[:, b, P * q:P * (q + 1)], wb[:, 1280:1536], start=True, stop=True)
                ins.then_inc(sm["tok_mm"], 1)

            def wo_transposes():
                pe.wait_ge(sm["wo_in"], 16)
                for i in range(4):
                    ins = pe.transpose(bank(7)[:, P * i:P * (i + 1)], wc[:, W_WO + P * i:W_WO + P * (i + 1)], ident)
                ins.then_inc(sm["woT"], 1)

            def fold():
                pe.wait_ge(sm["woT_sb"], 1)
                for i in range(4):
                    dst = bank(6 + i // 3)[:, (D + 4) * (i % 3):(D + 4) * (i % 3 + 1)]
                    pe.matmul(dst[:, 0:D], woT_sb[:, i, :], wc[:, W_FWO:W_FWO + D], start=True, stop=True)
                    ins = pe.matmul(dst[:, D:D + 4], woT_sb[:, i, :], wc[:, W_FWG + 4 * i:W_FWG + 4 * (i + 1)],
                                    start=True, stop=True)
                ins.then_inc(sm["fold_mm"], 1)

            def score(u, r, step):
                h, q = r // QT, r % QT
                dst = bank(r % 2)
                if step is not None:
                    pe.wait_ge(sm["s_max"], 16 * step + r - 1)
                ins = pe.matmul(dst, stk[:, u, 1, h, P * q:P * (q + 1)], stk[:, u, 0, h, :], start=True, stop=u % 2 == 1)
                if u % 2 == 0:
                    ins = pe.matmul(dst[:, P * q:P * (q + 1)], ident_b, diag_b, start=False, stop=True)
                ins.then_inc(sm["s_ready"], 1)

            def score_t(u, kt, h, step):
                if h % 2 == 0:
                    pe.wait_ge(sm["st_free"], 8 * step + 2 * kt + h // 2 + 1)
                dst = bank(2 + h)
                ins = pe.matmul(dst, stk[:, u, 0, h, P * kt:P * (kt + 1)], stk[:, u, 1, h, :], start=True, stop=u % 2 == 1)
                if u % 2 == 0:
                    ins = pe.matmul(dst[:, P * kt:P * (kt + 1)], ident_b, diag_b, start=False, stop=True)
                if h % 2 == 1:
                    ins.then_inc(sm["st_ready"], 1)

            def weighted(u, kt, step, half):
                if half == 0:
                    pe.wait_ge(sm["st_free"], 2 + 8 * step + 2 * kt + 2)
                    if kt == 0:
                        pe.wait_ge(sm["o_evac"], step + 1)
                q = slice(S // 2 * half, S // 2 * (half + 1))
                for h in range(G):
                    ins = pe.matmul(bank(6)[VW * h:VW * (h + 1), q], vb[:, u, kt, VW * h:VW * (h + 1)],
                                    a_buf[:, kt % 2, h, q], start=kt == 0 and half == 0, stop=kt == QT - 1 and half == 1)
                if half == 1:
                    ins.then_inc(sm["a_free"], 1)

            def o_back(n):
                pe.wait_ge(sm["mt_evac"], n + 1)
                pe.wait_ge(sm["o_evac"], n + 1)
                for q in range(QT):
                    ins = pe.transpose(bank(7)[:, P * q:P * (q + 1)], oev[:, P * q:P * (q + 1)], ident)
                ins.then_inc(sm["ot_ready"], 1)

            def max_t(step, par, normed):
                pe.wait_ge(sm["m_split"], step + 1)
                if normed is not None:
                    pe.wait_ge(sm["o_norm"], normed)
                for q in range(QT):
                    ins = pe.transpose(bank(7)[0:3 * G, P // 2 * q:P // 2 * (q + 1)].bitcast(BF16),
                                       mprt[:, par, q].rearrange("p c h -> p (c h)"), ident_b)
                ins.then_inc(sm["mt_ready"], 1)

            pe.wait_ge(sm["cst_in"], 48)
            pe.wait_ge(sm["nxs_ready"], 2)
            pe.wait_ge(sm["gr_ready"], 1)
            for step in range(2):
                pe.wait_ge(load_done[step], 48)
                for r in range(4 * G):
                    score(step, r, step if 16 * step + r >= 2 else None)
                    if r % 4 < 3:
                        local_product(12 * step + 3 * (r // 4) + r % 4)
                    if step == 1 and r == 2:
                        wo_transposes()
                    if step == 1 and r == 5:
                        fold()
                    if step == 1 and r == 8:
                        pe.wait_ge(sm["fold_sb"], 1)
                        max_t(0, 0, None)
            pe.wait_ge(m_done[0], 16)
            pe.wait_ge(sm["tok_act"], 6 * NT)
            for h in range(G):
                score_t(0, 0, h, 0)

            def steps(it, last):
                for u in range(4):
                    n = 4 * it + u
                    ahead = not (last and u >= 2)
                    w = (u + 2) % 4
                    for kt in range(QT):
                        if kt == 0 and ahead:
                            pe.wait_ge(load_done[w], 48 * (it + 1 + (u >= 2)))
                        more = not (last and u == 3 and kt == 3)
                        if kt == 3 and more:
                            pe.wait_ge(m_done[(u + 1) % 4], 16 * (it + 1 + (u == 3)))

                        def st(h):
                            if more and kt < 3:
                                score_t(u, kt + 1, h, n)
                            elif more:
                                score_t((u + 1) % 4, 0, h, n + 1)

                        def s(i):
                            if ahead:
                                score(w, 4 * kt + i, n + 2)

                        s(0)
                        st(0)
                        st(1)
                        s(1)
                        if kt == 0:
                            pe.wait_ge(v_done[u], 16 * (it + 1))
                        weighted(u, kt, n, 0)
                        if kt == 1 and not (last and u == 3):
                            max_t(n + 1, (u + 1) % 2, n + 1)
                        s(2)
                        st(2)
                        st(3)
                        s(3)
                        weighted(u, kt, n, 1)
                        if kt == 0:
                            o_back(n)

            with pe.Fori(0, LOOPED) as it:
                steps(it, False)
            steps(LOOPED, True)
            pe.wait_ge(sm["o_norm"], STEPS)
            pe.wait_ge(sm["o_evac"], STEPS + 1)
            for q in range(QT):
                ins = pe.transpose(bank(7)[:, P * q:P * (q + 1)], oev[:, P * q:P * (q + 1)], ident)
            ins.then_inc(sm["ot_ready"], 1)

            def out_t(t):
                b, q = t // QT, t % QT
                if t == 1:
                    pe.wait_ge(sm["o_norm"], STEPS + 1)
                if t >= 2:
                    pe.wait_ge(sm["oT_sb"], t - 1)

                def tile(ty):
                    first = b * NG + 1
                    return o_sb[:, ty, q, first:first + NG, :].rearrange("p g c -> p (g c)")
                srcs = [tile(0), o_loc[:, 0, t, :], o_loc[:, 1, t, :], tile(1)]
                for i, src in enumerate(srcs):
                    ins = pe.transpose(bank(6 + t % 2)[:, P * i:P * (i + 1)], src, ident)
                ins.then_inc(sm["oT"], 1)

            pe.wait_ge(sm["o_norm"], STEPS + 1)
            pe.wait_ge(sm["loc_out"], 1)
            out_t(0)
            pe.wait_ge(sm["fold_sb"], 1)
            for t in range(NT):
                if t + 1 < NT:
                    out_t(t + 1)
                pe.wait_ge(sm["oT_sb"], t + 1)
                if t >= 3:
                    pe.wait_ge(sm["x1_done"], t - 2)
                a = 2 * (t % 3)
                for i in range(4):
                    ins = pe.matmul(ps[:, a + i // 2, 256 * (i % 2):256 * (i % 2) + 132], oT_sb[:, t % 2, i, :],
                                    wop[:, t // QT, i, :], start=True, stop=True)
                ins.then_inc(sm["p_mm"], 1)

            pe.wait_ge(sm["x1_done"], NT)
            for b in range(B):
                transposes(b, xh, sm["xT2"], sm["xh2_ready"], QT * b)
            for b in range(B):
                pe.wait_ge(sm["nx2"], B)
                for f in range(FT):
                    n = FT * b + f
                    if n >= 3:
                        pe.wait_ge(sm["u_ready"], n - 2)
                    pe.matmul(bank(2 * (n % 3)), wc[:, W_W1 + P * f:W_W1 + P * (f + 1)], nT[:, b, :], start=True, stop=True)
                    pe.matmul(bank(2 * (n % 3) + 1), wc[:, W_W3 + P * f:W_W3 + P * (f + 1)], nT[:, b, :],
                              start=True, stop=True).then_inc(sm["h_mm"], 1)
                    if b == 1 and f == 2:
                        ffn_out(pe, 0)
            ffn_out(pe, 1)

            pe.wait_ge(sm["u_ready"], B * FT)
            for b in range(B):
                transposes(b, xh, sm["xT3"], sm["xh3_ready"], QT * b)
            for b in range(B):
                pe.wait_ge(sm["nx3"], b + 1)
                pe.matmul(bank(6 + b), wc[:, W_K:W_K + D], nT[:, b, :], start=True, stop=True).then_inc(sm["k_mm"], 1)
                for t in range(QT):
                    ins = pe.matmul(ps[:, 2 + 2 * b + t // 2, 256 * (t % 2):256 * (t % 2 + 1)], nT[:, b, P * t:P * (t + 1)],
                                    wc[:, W_QV:W_QV + 256], start=True, stop=True)
                ins.then_inc(sm["qv_mm"], 1)
            for b in range(B):
                pe.wait_ge(sm["k_exp"], b + 1)
                for t in range(QT):
                    ins = pe.transpose(bank(b)[:, P * t:P * (t + 1)], kx[:, b, P * t:P * (t + 1)], ident)
                ins.then_inc(sm["kt_mm"], 1)
            for b in range(B):
                pe.wait_ge(sm["q_ready"], b + 1)
                pe.wait_ge(sm["qv_ready"], b + 1)
                for t in range(QT):
                    ins = pe.transpose(bank(2 + b)[:, P * t:P * (t + 1)], q_sb[:, QT * b + t, :], ident)
                ins.then_inc(sm["qT"], 1)
            for b in range(B):
                pe.wait_ge(sm["kt_sb"], b + 1)
                pe.wait_ge(sm["qv_ready"], B)
                for t in range(QT):
                    ins = pe.matmul(bank(4 + b)[:, 0:D], kt_sb[:, QT * b + t, :], v_sb[:, QT * b + t, :],
                                    start=t == 0, stop=t == QT - 1)
                ins.then_inc(sm["ctx_mm"], 1)
            for b in range(B):
                pe.wait_ge(sm["ctx_sb"], b + 1)
                pe.wait_ge(sm["qT_sb"], b + 1)
                for t in range(QT):
                    ins = pe.matmul(bank(6 + b)[:, P * t:P * (t + 1)], qT_sb[:, b, P * t:P * (t + 1)], ctx_sb[:, b, :],
                                    start=True, stop=True)
                ins.then_inc(sm["yl_mm"], 1)
            for b in range(B):
                transposes(b, xh, sm["xT4"], sm["xh4_ready"], QT * b)
            for b in range(B):
                pe.wait_ge(sm["u4"], b + 1)
                for t in range(QT):
                    ins = pe.matmul(bank(2 + b)[:, P * t:P * (t + 1)], t4[:, b, P * t:P * (t + 1)], wc[:, W_OUT:W_OUT + D],
                                    start=True, stop=True)
                ins.then_inc(sm["z_mm"], 1)


def _constants():
    import numpy as np
    bf = mybir.dt.np(BF16)
    tok = np.arange(S)
    tile, at = tok // P, tok % P
    kside = np.zeros((MROW - DATA, S), np.float32)
    qside = np.zeros((MROW - DATA, S), np.float32)
    for t in range(QT):
        s = np.sign(tile - t).astype(np.float32)
        kside[3 * t] = -s * P * (tile - t)
        kside[3 * t + 1] = -s * at
        kside[3 * t + 2] = s
        qside[3 * t] = tile == t
        qside[3 * t + 1] = tile == t
        qside[3 * t + 2] = (tile == t) * at
    stk_c = np.zeros((MROW - DATA, 4, 2, G, S), np.float32)
    for u in (0, 2):
        stk_c[:, u, 0] = kside[:, None, :]
        stk_c[:, u, 1] = qside[:, None, :]
    stk_o = np.zeros((3, G, 4, 2, G, S), np.float32)
    for h in range(G):
        stk_o[:, h, :, 0, h] = 1.0
    i = np.arange(P)
    diag = -np.abs(i[:, None] - i[None, :]).astype(np.float32)
    cst_bf = np.concatenate([np.eye(P, dtype=np.float32), diag], 1)
    hmask = (i[:, None] // DH == i[None, :] // DH).astype(np.float32)
    lmask = np.zeros((P, 3, NT), np.float32)
    for t in range(NT):
        if t % QT == 0:
            lmask[0, 0, t] = -1e9
        if t % QT == QT - 1:
            lmask[P - 1, 2, t] = -1e9
    return (np.eye(P, dtype=np.float32), hmask, lmask.reshape(P, 3 * NT), cst_bf.astype(bf),
            stk_c.reshape(MROW - DATA, -1).astype(bf), stk_o.reshape(3 * G, -1).astype(bf))


def kernel(**inputs):
    import numpy as np
    import concourse.bacc as bacc
    from concourse.bass_utils import run_bass_kernel_spmd as run

    a = {k: np.asarray(v) for k, v in inputs.items()}
    l0 = {k[8:]: v for k, v in a.items() if k.startswith("L0_cond_")}
    l1 = {k[8:]: v for k, v in a.items() if k.startswith("L1_cond_")}
    eye, hmask, lmask, cst_bf, stk_c, stk_o = _constants()

    def block(w, j):
        return w[..., P * j:P * (j + 1)]

    aw, ab, ew, eb = l0["ada_w"], l0["ada_b"], l1["emb_W"], l1["emb_b"]
    cond = a["cond_1024"]
    cols = np.stack([l0["ln1_g"], l0["ln2_g"], l1["sn_g"], l0["ln1_b"], l0["ln2_b"], l1["sn_b"], l1["norm_g"], l1["norm_b"],
                     l1["bk"], cond[0], cond[1], block(ab, 1), block(ab, 4), block(eb, 0), block(ab, 0), block(ab, 3),
                     block(eb, 1)], 1)
    pk_a = np.concatenate([cols, block(aw, 1), block(aw, 4), block(ew, 0), block(aw, 0), block(aw, 3), block(ew, 1),
                           block(aw, 2), block(aw, 5), eye, hmask, lmask], 1)
    pk_b = np.concatenate([l0["grid_wk"], l0["grid_wq"], l0["sem_wk"], l0["sem_wq"],
                           l0["reg_wq"], l0["ent_wq"], l0["grid_wv"], l0["sem_wv"],
                           l0["reg_wk"], l0["reg_wv"], l0["ent_wk"], l0["ent_wv"]], 1)
    fwg = l0["fus_wg"].reshape(4, P, 4).transpose(1, 0, 2).reshape(P, 16)
    w2 = l0["ffn_w2"].reshape(FT, P, D).transpose(1, 0, 2).reshape(P, FT * D)
    pk_c = np.concatenate([l0["grid_wo"], l0["reg_wo"], l0["ent_wo"], l0["sem_wo"], l0["fus_wo"], fwg,
                           l0["ffn_w1"], l0["ffn_w3"], w2, l1["Wq"], l1["Wv"], l1["Wk"], l1["out_W"]], 1)
    row = np.concatenate([block(ab, 2), block(ab, 5), l1["bq"], l1["bv"], l1["out_b"], cond[0], cond[1], l0["fus_bg"]])
    arrays = {"x": a["x"], "pk_a": pk_a, "pk_b": pk_b, "pk_c": pk_c, "rows": np.broadcast_to(row, (P, R_END)),
              "cst_bf": cst_bf, "stk_c": stk_c, "stk_o": stk_o}
    arrays = {k: np.ascontiguousarray(v) for k, v in arrays.items()}
    nc = bacc.Bacc("TRN2", target_bir_lowering=False, num_devices=1)
    args = [nc.dram_tensor(k, v.shape, mybir.dt.from_np(v.dtype), kind="ExternalInput").ap() for k, v in arrays.items()]
    args.append(nc.dram_tensor("out", (B, S, D), F32, kind="ExternalOutput").ap())
    program(nc, *args)
    r = run(nc, [arrays], core_ids=[0])
    return r.results[0]["out"]
```

```python
from contextlib import ExitStack

import concourse.bass as bass
from concourse import mybir

F32 = mybir.dt.float32
BF16 = mybir.dt.bfloat16
ALU = mybir.AluOpType
ACT = mybir.ActivationFunctionType
AX = mybir.AxisListType

P = 128
B, S, D = 2, 512, 128
T = B * S
NT = T // P
QT = S // P
H, DH = 16, 8
G = 4
NG = H // G
F = 512
FT = F // P
SCALE = 1.0 / DH ** 0.5
TERMS = 6
DATA = TERMS * DH
MROW = 64
OUTS = 16 * 2 * 3
LOADS = 16 * (2 + 1)
ROWS = MROW + 3 * G
STEPS = 2 * B * NG
VW = 32
WARM = 20
LOOPED = STEPS // 4 - 1
T_AT = (5, 7, 9, 11)
O_AT = (6, 7)

C_GAIN, C_BIAS, C_NG, C_NB, C_BK, C_COND, C_ADA, C_END = 0, 3, 6, 7, 8, 9, 11, 17
A_W, A_GW, A_ID, A_HM, A_LM, A_END = (C_END + n for n in (0, 768, 1024, 1152, 1280, 1304))
R_G, R_BQ, R_BV, R_OB, R_COND, R_FB, R_END = 0, 256, 384, 512, 640, 896, 900
W_WO, W_FWO, W_FWG, W_W1, W_W3, W_W2, W_QV, W_K, W_OUT, W_END = (
    0, 512, 640, 656, 1168, 1680, 2192, 2448, 2576, 2704)


def program(nc, x, pk_a, pk_b, pk_c, rows, cst_bf, stk_c, stk_o, out):
    ctx = ExitStack()
    with ctx:
        def sb(name, shape, dt=F32):
            return ctx.enter_context(nc.sbuf_tensor(name, shape, dt))

        def sem(name):
            return ctx.enter_context(nc.semaphore(name))

        qk_dram = [[nc.dram_tensor(f"qk_{t}{s}", [B * NG, G, DH, TERMS, S], BF16).ap() for s in "kq"] for t in "gs"]

        x_sb = sb("x_sb", [P, NT, D])
        pa = sb("pa", [P, A_END])
        wb = sb("wb", [P, 1536])
        wc = sb("wc", [P, W_END])
        rw = sb("rw", [P, R_END])
        cb = sb("cb", [P, 2 * P], BF16)
        stk = sb("stk", [ROWS, 4, 2, G, S], BF16)
        nxb = sb("nx", [P, B, S])
        nxs = sb("nxs", [P, B, S])
        vc = sb("vc", [P, 2, B * NG, QT, G * DH])
        vb = sb("vb", [P, 4, QT, G, VW])
        prod = sb("prod", [P, 5 * NT * D])
        parts_mem = sb("parts", [P, 4, 3, B, S], BF16)
        kv = sb("kv", [P, 5, 2, NT, D])
        ql = sb("ql", [P, 2, NT, D])
        o_sb = sb("o_sb", [P, 2, QT, B * NG + 1, G * DH])
        oev = sb("oev", [P, S])
        mneg = sb("mneg", [P, 2, G * QT])
        mres = sb("mres", [P, 2, G * QT])
        mprt = sb("mprt", [P, 2, QT, 3, G], BF16)
        mrow = sb("mrow", [G * 3, 2, S], BF16)
        orec = sb("orec", [P, QT * G])
        mv = sb("mv", [P, 4, NT, 2])
        bst = sb("bst", [P, NT, 6])
        rstd = sb("rstd", [P, 4, NT])
        mhalf = sb("mhalf", [P, NT])
        sil = sb("sil", [P, 4, B])
        silb = sb("silb", [P, B, P])
        ada = sb("ada", [P, 6, B])
        ga = sb("ga", [P, 3, B])
        ba = sb("ba", [P, 3, B])
        gr = sb("gr", [P, B, 2 * D])
        ls = sb("ls", [P, 5 * NT * H])
        lsm = sb("lsm", [P, 2, NT * H])
        wop = sb("wop", [P, B, 4, D + 4])

        a_buf = parts_mem[:, :, :, :, :].rearrange("p a b c d -> p (a b c d)")[:, 0:8192].bitcast(F32) \
            .rearrange("p (n g s) -> p n g s", n=2, g=G)
        kvf = kv[:, :, :, :, :].rearrange("p a b c d -> p (a b c d)")
        resid = [kvf[:, S * k:S * (k + 1)] for k in range(3)]
        xh1 = kvf[:, 2048:3072].rearrange("p (t d) -> p t d", t=NT)
        pv = prod[:, :].rearrange("p (n t d) -> p n t d", n=5, t=NT)
        o_loc = pv[:, 1:4:2]
        woT_sb = oev[:, :].rearrange("p (i c) -> p i c", i=4)
        ident = pa[:, A_ID:A_ID + P]
        hmask = pa[:, A_HM:A_HM + P]
        lmask = pa[:, A_LM:A_LM + 3 * NT]
        ident_b, diag_b = cb[:, 0:P], cb[:, P:2 * P]

        oT_sb = kvf[:, 0:2048].rearrange("p (n i c) -> p n i c", n=QT, i=4)
        xh = kvf[:, 2048:3072].rearrange("p (t d) -> p t d", t=NT)
        nT = kvf[:, 3072:4096].rearrange("p (b s) -> p b s", b=B)
        th = kvf[:, 4096:5120].rearrange("p (n s) -> p n s", n=2)
        hv = kvf[:, 5120:6144].rearrange("p (n s) -> p n s", n=2)
        q_sb = kvf[:, 6144:7168].rearrange("p (t d) -> p t d", t=NT)
        v_sb = kvf[:, 7168:8192].rearrange("p (t d) -> p t d", t=NT)
        ctx_sb = kvf[:, 8192:8448].rearrange("p (b d) -> p b d", b=B)
        kx = kvf[:, 8448:9472].rearrange("p (b s) -> p b s", b=B)
        u_sb = a_buf.rearrange("p n g s -> p (n g s)").rearrange("p (f b s) -> p f b s", f=FT, b=B)
        kt_sb = prod[:, 0:1024].rearrange("p (t d) -> p t d", t=NT)
        qT_sb = prod[:, 1024:2048].rearrange("p (b s) -> p b s", b=B)
        hT = prod[:, 2048:3072].rearrange("p (b s) -> p b s", b=B)
        t4 = prod[:, 3072:4096].rearrange("p (b s) -> p b s", b=B)
        xgb = prod[:, 4096:5120].rearrange("p (t d) -> p t d", t=NT)
        small = ql[:, 0].rearrange("p t d -> p (t d)")
        gate = small[:, 0:32].rearrange("p (k j c) -> p k j c", k=NT // 2, j=2)
        gate_r = small[:, 32:48].rearrange("p (k n j) -> p k n j", k=NT // 2, n=2)
        gate_3 = small[:, 48:80].rearrange("p (k j c) -> p k j c", k=NT // 2, j=2)
        qmx = small[:, 96:224].rearrange("p (b c) -> p b c", b=B)
        qsm = small[:, 224:352].rearrange("p (b c) -> p b c", b=B)
        ksm = small[:, 352:368].rearrange("p (b c) -> p b c", b=B)
        cgb = small[:, 368:624].rearrange("p (b d) -> p b d", b=B)
        cgh = small[:, 624:880].rearrange("p (b d) -> p b d", b=B)
        OUT_BANKS = ((0, 1, 7), (2, 3, 4), (0, 1, 6), (0, 1, 7))
        OW = D + 4

        LAST = ((0, 1, 7), (2, 3, 4))

        ps = ctx.enter_context(nc.psum_tensor("ps", [P, 8, 512], F32))

        def bank(i):
            return ps[:, i, :]

        names = """warm_in warmed x0_in x1_in pa_in wqk_in wb_in wo_in wc_in rw_in cst_in grid0_out sem0_out
          grid1_out sem1_out kv_moved out_done dve_chain act_chain gp_chain tanh_c siluT silb_ready ada_mm gr_mm ga_ready gr_ready var1 rstd1 xh1_ready xT1
          nx_ready nxs_ready qk_mm part1 resid1 part2 part3 tok_mm tok_act ones_set
          primed s_ready s_max split_step m_split mt_ready mt_evac st_ready st_free a_free o_evac ot_ready o_norm o_rec
          loc_scores loc_max loc_soft loc_exp loc_sum loc_inv loc_out
          woT woT_sb fold_mm fold_sb oT oT_sb p_mm logits gate_exp x1_step
          var2 rstd2 xh2_ready xT2 nx2 h_mm h_tanh h_v u_ready y_mm x2_done
          var3 rstd3 xh3_ready xT3 nx3 qv_mm k_mm q_max qv_ready q_exp k_max k_exp kt_mm kt_sb ctx_mm ctx_sb qT qT_sb
          yl_mm var4 rstd4 xh4_ready xT4 h4 h4_tanh u4 z_mm o_ready gb_ready""".split()
        sm = {n: sem(n) for n in names}
        load_done = [sem(f"load_done{u}") for u in range(4)]
        v_done = [sem(f"v_done{u}") for u in range(4)]
        m_done = [sem(f"m_done{u}") for u in range(4)]

        def chainer(eng, s):
            count = [0]

            def link(ins):
                count[0] += 1
                ins.then_inc(s, 1)
                eng.wait_ge(s, count[0])
            return link

        block = ctx.enter_context(nc.Block())
        qk_out = [[sm["grid0_out"], sm["grid1_out"]], [sm["sem0_out"], sm["sem1_out"]]]

        @block.sync
        def _(sp):
            xs = x.rearrange("b (t p) d -> b p t d", p=P)
            sp.dma_start(x_sb[:, 0:QT, :], xs[0]).then_inc(sm["x0_in"], 16)
            sp.dma_start(pa[:, :], pk_a).then_inc(sm["pa_in"], 16)
            sp.dma_start(x_sb[:, QT:NT, :], xs[1]).then_inc(sm["x1_in"], 16)
            sp.dma_start(wb[:, 0:512], pk_b[:, 0:512]).then_inc(sm["wqk_in"], 16)
            sp.dma_start(rw[:, :], rows).then_inc(sm["rw_in"], 16)
            sp.dma_start(wb[:, 512:1536], pk_b[:, 512:1536]).then_inc(sm["wb_in"], 16)
            stk_r = stk[:, :, :, :, :].rearrange("r a b c d -> r (a b c d)")
            sp.dma_start(stk_r[DATA:MROW, :], stk_c).then_inc(sm["cst_in"], 16)
            sp.dma_start(stk_r[MROW:ROWS, :], stk_o).then_inc(sm["cst_in"], 16)
            sp.dma_start(cb[:, :], cst_bf).then_inc(sm["cst_in"], 16)
            sp.dma_start(wc[:, 0:W_W1], pk_c[:, 0:W_W1]).then_inc(sm["wo_in"], 16)
            sp.dma_start(wc[:, W_W1:W_END], pk_c[:, W_W1:W_END]).then_inc(sm["wc_in"], 16)

            def parts_out(i):
                b, n = i // 4, i % 4
                ty, side = n // 2, n % 2
                dst = qk_dram[ty][side].rearrange("(b g) h d j q -> b (g h d) j q", b=B)[b]
                runs = ((5, 1, 0), (3, 2, 0), (0, 3, 0)) if side else ((0, 3, 0), (3, 2, 1), (5, 1, 2))
                for k, (j0, c, first) in enumerate(runs):
                    sp.wait_ge(sm[f"part{k + 1}"], i + 1)
                    src = parts_mem[:, n, first:first + (c if side else 1), b, :]
                    sp.dma_start(dst[:, j0:j0 + c, :], src if side else src.broadcast_to([P, c, S])) \
                        .then_inc(qk_out[ty][b], 16)

            def load(u, bg):
                for side in range(2):
                    src = qk_dram[u % 2][side].rearrange("n h d j q -> n (d j) h q")
                    sp.dma_start(stk[0:DATA, u, side, :, :], src[bass.ds(bg, 1)].rearrange("o r h q -> (o r) h q")) \
                        .then_inc(load_done[u], 16)
                sp.dma_start(stk[MROW:ROWS, u, 1, :, :].rearrange("r h q -> r (h q)"), stk_o[:, G * S:2 * G * S]) \
                    .then_inc(load_done[u], 16)

            def max_rows(step, u):
                sp.wait_ge(sm["mt_evac"], step + 1)
                sp.dma_start(stk[MROW:ROWS, u, 1, :, :],
                             mrow[:, u % 2, :].unsqueeze(1).broadcast_to([3 * G, G, S])).then_inc(m_done[u], 16)

            def neighbours():
                sp.wait_ge(sm["tok_act"], 3 * NT)
                for slot, to, at, edge, tile_to, tile_at in ((0, 1, 0, 0, 1, 0), (2, 0, 1, P - 1, 0, 1)):
                    far = P - 1 - edge
                    end = (NT - 1) * (edge > 0)
                    for dst, src in ((kv[to:to + P - 1, slot], kv[at:at + P - 1, 1]),
                                     (kv[edge:edge + 1, slot, :, tile_to:tile_to + NT - 1],
                                      kv[far:far + 1, 1, :, tile_at:tile_at + NT - 1]),
                                     (kv[edge:edge + 1, slot, :, end], kv[edge:edge + 1, 1, :, end])):
                        sp.dma_start(dst, src).then_inc(sm["kv_moved"], 16)

            for i in range(3):
                parts_out(i)
            sp.wait_ge(sm["cst_in"], 48)
            sp.wait_ge(qk_out[0][0], OUTS)
            load(0, 0)
            parts_out(3)
            sp.wait_ge(qk_out[1][0], OUTS)
            load(1, 0)
            for i in range(4, 8):
                parts_out(i)
            for u in range(2, 4):
                load(u, 1)
            max_rows(0, 0)
            neighbours()
            for ty in range(2):
                sp.wait_ge(qk_out[ty][1], OUTS)

            def steps(it, last):
                for u in range(4):
                    n = 4 * it + u
                    if not (last and u == 3):
                        max_rows(n + 1, (u + 1) % 4)
                    if not last:
                        sp.wait_ge(sm["a_free"], 2 + 4 * (n + 1))
                        load(u, 2 * (it + 1) + u // 2)

            with sp.Fori(0, LOOPED) as it:
                steps(it, False)
            steps(LOOPED, True)

            for pair in range(NT // 2):
                sp.wait_ge(sm["o_ready"], pair + 1)
                dst = out.rearrange("b (n t p) d -> p (b n) t d", n=2, p=P)
                sp.dma_start(dst[:, pair], x_sb[:, 2 * pair:2 * pair + 2, :]).then_inc(sm["out_done"], 16)
            sp.wait_ge(sm["out_done"], 16 * (NT // 2))

        @block.gpsimd
        def _(gp):
            link = chainer(gp, sm["gp_chain"])
            link(gp.memset(mhalf[:, :], -0.5))

            def inv_std(k, eps, t0, t1, var, ready):
                gp.wait_ge(*var)
                link(gp.tensor_scalar(rstd[:, k, t0:t1], mv[:, k, t0:t1, 1], eps, None, ALU.add))
                gp.tensor_tensor(rstd[:, k, t0:t1], rstd[:, k, t0:t1], mhalf[:, t0:t1], ALU.pow).then_inc(ready, 1)

            for b in range(B):
                inv_std(0, 1e-6, QT * b, QT * (b + 1), (sm["var1"], b + 1), sm["rstd1"])
            gp.memset(vb[:, :, :, :, :], 1.0).then_inc(sm["ones_set"], 1)

            gp.wait_ge(sm["nx_ready"], 2)
            for par in range(2):
                gp.tensor_copy(nxs[:, :, par::2], nxb[:, :, 1 - par::2]).then_inc(sm["nxs_ready"], 1)

            l5 = ls[:, :].rearrange("p (n c) -> p n c", n=5)

            def spread_v(u, bg):
                gp.tensor_copy(vb[:, u, :, :, 0:DH].rearrange("p k h (o c) -> p o k h c", o=1),
                               vc[:, u % 2, bass.ds(bg, 1)].rearrange("p o k (h c) -> p o k h c", h=G)) \
                    .then_inc(v_done[u], 1)

            gp.wait_ge(sm["ones_set"], 1)
            gp.wait_ge(sm["tok_act"], 2 * NT)
            for u in range(4):
                spread_v(u, u // 2)

            gp.wait_ge(sm["tok_act"], 4 * NT)
            gp.wait_ge(sm["kv_moved"], 16 * 6)
            for n in range(5):
                ins = gp.tensor_tensor(pv[:, n], kv[:, n, 0], ql[:, 0 if n < 3 else 1], ALU.mult)
            link(ins)
            pg = prod[:, :].rearrange("p (g d) -> p g d", d=DH)
            link(gp.tensor_tensor(pg[:, :, 0:4], pg[:, :, 0:4], pg[:, :, 4:8], ALU.add))
            link(gp.tensor_tensor(pg[:, :, 0:2], pg[:, :, 0:2], pg[:, :, 2:4], ALU.add))
            link(gp.tensor_tensor(ls[:, :].unsqueeze(2), pg[:, :, 0:1], pg[:, :, 1:2], ALU.add))
            lr = ls[:, 0:3 * NT * H].rearrange("p (n h) -> p n h", h=H)
            gp.tensor_tensor(lr, lr, lmask.unsqueeze(2).broadcast_to([P, 3 * NT, H]), ALU.add).then_inc(sm["loc_scores"], 1)
            with gp.Fori(0, LOOPED) as it:
                for u in range(4):
                    gp.wait_ge(sm["a_free"], 2 + 4 * (4 * it + u + 1))
                    spread_v(u, 2 * (it + 1) + u // 2)
            gp.wait_ge(sm["loc_max"], 1)
            gp.tensor_tensor(l5[:, 0:3, :], l5[:, 0:3, :], lsm[:, 0:1, :].broadcast_to([P, 3, NT * H]), ALU.subtract)
            gp.tensor_tensor(l5[:, 3:5, :], l5[:, 3:5, :], lsm[:, 1:2, :].broadcast_to([P, 2, NT * H]), ALU.subtract) \
                .then_inc(sm["loc_soft"], 1)
            gp.wait_ge(sm["loc_exp"], 1)
            link(gp.tensor_tensor(lsm[:, :, :], l5[:, 0:4:3, :], l5[:, 1:5:3, :], ALU.add))
            gp.tensor_tensor(lsm[:, 0, :], lsm[:, 0, :], l5[:, 2, :], ALU.add).then_inc(sm["loc_sum"], 1)
            for n in range(5):
                w = ls[:, n * NT * H:(n + 1) * NT * H].unsqueeze(2).broadcast_to([P, NT * H, DH])
                ins = gp.tensor_tensor(pv[:, n].rearrange("p t (h d) -> p (t h) d", d=DH),
                                       kv[:, n, 1].rearrange("p t (h d) -> p (t h) d", d=DH), w, ALU.mult)
            link(ins)
            link(gp.tensor_tensor(pv[:, 0], pv[:, 0], pv[:, 1], ALU.add))
            gp.tensor_tensor(o_loc[:, 0], pv[:, 0], pv[:, 2], ALU.add)
            link(gp.tensor_tensor(o_loc[:, 1], pv[:, 3], pv[:, 4], ALU.add))
            gp.wait_ge(sm["loc_inv"], 4)
            for a in range(2):
                o8 = o_loc[:, a].rearrange("p t (h d) -> p (t h) d", d=DH)
                ins = gp.tensor_tensor(o8, o8, lsm[:, a, :].unsqueeze(2).broadcast_to([P, NT * H, DH]), ALU.mult)
            ins.then_inc(sm["loc_out"], 1)

            gp.wait_ge(sm["rw_in"], 16)
            cond = rw[:, R_COND:R_COND + 256].rearrange("p (b d) -> p b d", b=B)
            gp.tensor_scalar(cgh, cond, 0.5, None, ALU.mult)
            link(gp.tensor_tensor(cgb, cond, rw[:, R_OB:R_OB + P].unsqueeze(1).broadcast_to([P, B, D]), ALU.mult))
            for b in range(B):
                inv_std(1, 1e-6, QT * b, QT * (b + 1), (sm["var2"], b + 1), sm["rstd2"])
            for b in range(B):
                inv_std(2, 1e-5, QT * b, QT * (b + 1), (sm["var3"], b + 1), sm["rstd3"])
                t = slice(QT * b, QT * (b + 1))
                gp.wait_ge(sm["x2_done"], b + 1)
                gp.tensor_tensor(xgb[:, t, :], x_sb[:, t, :], cgb[:, b:b + 1, :].broadcast_to([P, QT, D]), ALU.add) \
                    .then_inc(sm["gb_ready"], 1)
            for b in range(B):
                inv_std(3, 1e-5, QT * b, QT * (b + 1), (sm["var4"], b + 1), sm["rstd4"])

        def max_evac(act, step, par):
            act.wait_ge(sm["mt_ready"], step + 1)
            act.activation(mrow[:, par, :], bank(7)[0:3 * G, 0:S // 2].bitcast(BF16), ACT.Copy).then_inc(sm["mt_evac"], 1)

        @block.scalar
        def _(act):
            link = chainer(act, sm["act_chain"])
            act.sem_inc(sm["st_free"], 2)
            act.wait_ge(sm["pa_in"], 16)
            act.activation(sil[:, 0, :], pa[:, C_COND:C_COND + B], ACT.Tanh, scale=0.5).then_inc(sm["tanh_c"], 1)
            act.wait_ge(sm["ga_ready"], 1)
            for b in range(B):
                act.wait_ge(sm["xT1"], b + 1)
                act.activation(nxb[:, b, :], bank(b), ACT.Identity, scale=ga[:, 0, b:b + 1],
                               bias=ba[:, 0, b:b + 1]).then_inc(sm["nx_ready"], 1)
            act.wait_ge(sm["warmed"], 1)
            for i in range(9):
                if i < 8:
                    b, n = i // 4, i % 4
                    act.wait_ge(sm["qk_mm"], i + 1)
                    act.activation(parts_mem[:, n, 0, b, :], bank(4 + n), ACT.Copy, scale=SCALE if n % 2 else 1.0) \
                        .then_inc(sm["part1"], 1)
                if i >= 1:
                    b, n = (i - 1) // 4, (i - 1) % 4
                    act.wait_ge(sm["resid1"], i)
                    act.activation(parts_mem[:, n, 1, b, :], resid[(i - 1) % 3], ACT.Copy).then_inc(sm["part2"], 1)
            for t in range(NT):
                act.wait_ge(sm["tok_mm"], t + 1)
                bk = bank(2 + t % 4)
                act.activation(ql[:, :, t, :], bk[:, 0:256].rearrange("p (a d) -> p a d", a=2), ACT.Copy, scale=SCALE) \
                    .then_inc(sm["tok_act"], 1)
                act.activation(vc[:, :, NG * (t // QT):NG * (t // QT + 1), t % QT, :],
                               bk[:, 256:512].rearrange("p (a g c) -> p a g c", a=2, g=NG), ACT.Copy) \
                    .then_inc(sm["tok_act"], 1)
                if t == 5:
                    act.wait_ge(sm["woT"], 1)
                    act.activation(woT_sb, bank(7).rearrange("p (i c) -> p i c", i=4), ACT.Copy).then_inc(sm["woT_sb"], 1)
            act.wait_ge(sm["part3"], 8)
            for j in range(NT, 3 * NT):
                act.wait_ge(sm["tok_mm"], j + 1)
                src = bank(2 + j % 4)
                if j < 2 * NT:
                    dst = kv[:, 1:4:2, :, j - NT, :]
                    act.activation(dst, src.rearrange("p (n a d) -> p n a d", n=2, a=2), ACT.Copy).then_inc(sm["tok_act"], 1)
                else:
                    act.activation(kv[:, 4, :, j - 2 * NT, :], src[:, 0:256].rearrange("p (a d) -> p a d", a=2), ACT.Copy) \
                        .then_inc(sm["tok_act"], 1)
                if j == 15:
                    max_evac(act, 0, 0)

            def o_evac(n):
                act.wait_ge(sm["a_free"], 4 * n + 2)
                act.wait_ge(sm["ot_ready"], n + 1)
                act.activation(oev[:, :], bank(6), ACT.Copy).then_inc(sm["o_evac"], 1)

            def steps(it, last):
                for u in range(4):
                    n = 4 * it + u
                    for kt in range(QT):
                        act.wait_ge(sm["a_free"], 4 * n + kt + 1)
                        for p in range(2):
                            act.wait_ge(sm["st_ready"], 8 * n + 2 * kt + p + 1)
                            act.activation(a_buf[:, kt % 2, 2 * p:2 * p + 2, :], ps[:, 2 + 2 * p:4 + 2 * p, :], ACT.Exp) \
                                .then_inc(sm["st_free"], 1)
                            if kt == 0 and p == 1:
                                o_evac(n)
                            if kt == 2 and p == 1 and not (last and u == 3):
                                max_evac(act, n + 1, (u + 1) % 2)
                        if last and u == 0 and kt == 1:
                            act.wait_ge(sm["loc_soft"], 1)
                            act.activation(ls[:, :], ls[:, :], ACT.Exp).then_inc(sm["loc_exp"], 1)
                        if last and u == 3 and kt == 2:
                            gate_exp(0)

            def gate_exp(k):
                act.wait_ge(sm["logits"], k + 1)
                act.activation(gate[:, k], gate[:, k], ACT.Exp).then_inc(sm["gate_exp"], 1)

            act.wait_ge(sm["grid1_out"], OUTS)
            act.wait_ge(sm["sem1_out"], OUTS)
            act.wait_ge(sm["primed"], 1)
            with act.Fori(0, LOOPED) as it:
                steps(it, False)
            steps(LOOPED, True)
            o_evac(STEPS)

            def nx2(b):
                act.wait_ge(sm["xT2"], b + 1)
                act.activation(nT[:, b, :], bank((5, 0)[b]), ACT.Identity, scale=ga[:, 1, b:b + 1],
                               bias=ba[:, 1, b:b + 1]).then_inc(sm["nx2"], 1)

            def h_tanh(b, f):
                n = FT * b + f
                act.wait_ge(sm["h_mm"], 2 * n + 1)
                if n >= 2:
                    act.wait_ge(sm["h_v"], n - 1)
                act.activation(th[:, n % 2], bank(2 + 2 * (n % 2)), ACT.Tanh, scale=0.5).then_inc(sm["h_tanh"], 1)

            def nx3(b):
                act.wait_ge(sm["xT3"], b + 1)
                act.activation(nT[:, b, :], bank(LAST[b][0]), ACT.Identity, scale=pa[:, C_NG:C_NG + 1],
                               bias=pa[:, C_NB:C_NB + 1]).then_inc(sm["nx3"], 1)

            def k_exp(b):
                act.wait_ge(sm["k_max"], b + 1)
                act.activation(kx[:, b, :], bank(LAST[b][2]), ACT.Exp, bias=ksm[:, b, 2:3],
                               accum_out=ksm[:, b, 3:4]).then_inc(sm["k_exp"], 1)

            def q_exp(b):
                act.wait_ge(sm["q_max"], b + 1)
                qb = q_sb[:, QT * b:QT * (b + 1), :]
                act.activation(qb, qb, ACT.Exp).then_inc(sm["q_exp"], 1)

            def k_copy(b):
                act.wait_ge(sm["kt_mm"], b + 1)
                act.activation(kt_sb[:, QT * b:QT * (b + 1), :], bank(LAST[b][2]).rearrange("p (t d) -> p t d", t=QT),
                               ACT.Copy).then_inc(sm["kt_sb"], 1)

            def q_copy(b):
                act.wait_ge(sm["qT"], b + 1)
                act.activation(qT_sb[:, b, :], bank(LAST[b][0]), ACT.Copy).then_inc(sm["qT_sb"], 1)

            def h4(b):
                act.wait_ge(sm["xT4"], b + 1)
                act.activation(hT[:, b, :], bank(LAST[b][0]), ACT.Identity, scale=ga[:, 2, b:b + 1],
                               bias=ba[:, 2, b:b + 1]).then_inc(sm["h4"], 1)
                act.wait_ge(sm["h4"], b + 1)
                act.activation(t4[:, b, :], hT[:, b, :], ACT.Tanh, scale=0.5).then_inc(sm["h4_tanh"], 1)

            def o_copy(t):
                act.wait_ge(sm["oT"], t + 1)
                act.activation(oT_sb[:, t % QT], bank(5 + t % 2 * 2).rearrange("p (i c) -> p i c", i=4), ACT.Copy) \
                    .then_inc(sm["oT_sb"], 1)

            gate_exp(1)
            o_copy(4)
            o_copy(5)
            o_copy(6)
            o_copy(7)
            nx2(0)
            gate_exp(2)
            h_tanh(0, 0)
            h_tanh(0, 1)
            gate_exp(3)
            h_tanh(0, 2)
            h_tanh(0, 3)
            nx2(1)
            h_tanh(1, 0)
            h_tanh(1, 1)
            nx3(0)
            h_tanh(1, 2)
            h_tanh(1, 3)
            k_exp(0)
            k_copy(0)
            q_exp(0)
            q_copy(0)
            nx3(1)
            k_exp(1)
            k_copy(1)
            h4(0)
            q_exp(1)
            q_copy(1)
            h4(1)

        @block.vector
        def _(dve):
            link = chainer(dve, sm["dve_chain"])

            def normalise(k, t, dst, src):
                return dve.tensor_scalar(dst, src, mv[:, k, t, 0:1], rstd[:, k, t:t + 1], ALU.subtract, ALU.mult)

            dve.memset(parts_mem[:, 0, 0, 0, :], 0.0).then_inc(sm["warm_in"], 1)
            for b in range(B):
                dve.wait_ge(sm[f"x{b}_in"], 16)
                for t in range(QT * b, QT * (b + 1)):
                    ins = dve.bn_stats(bst[:, t, :], x_sb[:, t, :])
                link(ins)
                for t in range(QT * b, QT * (b + 1)):
                    ins = dve.bn_aggr(mv[:, 0, t, :], bst[:, t, :])
                ins.then_inc(sm["var1"], 1)
            dve.wait_ge(sm["tanh_c"], 1)
            link(dve.scalar_tensor_tensor(sil[:, 1, :], sil[:, 0, :], 1.0, pa[:, C_COND:C_COND + B], ALU.add, ALU.mult))
            dve.tensor_scalar(sil[:, 2, :], sil[:, 1, :], 0.5, None, ALU.mult).then_inc(sm["siluT"], 1)
            dve.wait_ge(sm["siluT"], 1)
            dve.tensor_copy(silb[:, :, :], sil[:, 2, :].unsqueeze(2).broadcast_to([P, B, P])).then_inc(sm["silb_ready"], 1)
            for b in range(B):
                dve.wait_ge(sm["var1"], b + 1)
                dve.wait_ge(sm["rstd1"], b + 1)
                for t in range(QT * b, QT * (b + 1)):
                    normalise(0, t, xh1[:, t, :], x_sb[:, t, :]).then_inc(sm["xh1_ready"], 1)
            dve.wait_ge(sm["ada_mm"], 1)
            link(dve.tensor_tensor(ada[:, :, :], bank(2)[:, 0:12].rearrange("p (j b) -> p j b", b=B),
                                   pa[:, C_ADA:C_ADA + 6].unsqueeze(2).broadcast_to([P, 6, B]), ALU.add))
            sc = ada[:, 0:3, :]
            dve.scalar_tensor_tensor(ga[:, :, :], sc, 1.0,
                                     pa[:, C_GAIN:C_GAIN + 3].unsqueeze(2).broadcast_to([P, 3, B]), ALU.add, ALU.mult)
            link(dve.scalar_tensor_tensor(ba[:, :, :], sc, 1.0,
                                          pa[:, C_BIAS:C_BIAS + 3].unsqueeze(2).broadcast_to([P, 3, B]), ALU.add, ALU.mult))
            dve.tensor_tensor(ba[:, :, :], ba[:, :, :], ada[:, 3:6, :], ALU.add).then_inc(sm["ga_ready"], 1)
            dve.wait_ge(sm["gr_mm"], 1)
            dve.wait_ge(sm["rw_in"], 16)
            link(dve.tensor_tensor(gr[:, :, :], bank(3).rearrange("p (b c) -> p b c", b=B),
                                   rw[:, R_G:R_G + 256].unsqueeze(1).broadcast_to([P, B, 256]), ALU.add))
            dve.tensor_scalar(gr[:, :, D:2 * D], gr[:, :, D:2 * D], 0.5, None, ALU.mult).then_inc(sm["gr_ready"], 1)
            for i in range(9):
                if i < 8:
                    b, n = i // 4, i % 4
                    dve.wait_ge(sm["part1"], i + 1)
                    if i >= 3:
                        dve.wait_ge(sm["part3"], i - 2)
                    dve.scalar_tensor_tensor(resid[i % 3], bank(4 + n), SCALE if n % 2 else 1.0, parts_mem[:, n, 0, b, :],
                                             ALU.mult, ALU.subtract).then_inc(sm["resid1"], 1)
                if i >= 1:
                    b, n = (i - 1) // 4, (i - 1) % 4
                    dve.wait_ge(sm["resid1"], i)
                    dve.wait_ge(sm["part2"], i)
                    dve.tensor_tensor(parts_mem[:, n, 2, b, :], resid[(i - 1) % 3], parts_mem[:, n, 1, b, :], ALU.subtract) \
                        .then_inc(sm["part3"], 1)

            def row_max(step, r, par):
                dve.wait_ge(sm["s_ready"], 16 * step + r + 1)
                dve.tensor_reduce(mneg[:, par, r:r + 1], bank(r % 2), AX.X, ALU.max, negate=True) \
                    .then_inc(sm["s_max"], 1)

            def split(step, par, k):
                m = mneg[:, par, :].rearrange("p (h q) -> p q h", h=G)
                r = mres[:, par, :].rearrange("p (h q) -> p q h", h=G)
                if k == 0:
                    dve.wait_ge(sm["s_max"], 16 * (step + 1))
                else:
                    dve.wait_ge(sm["split_step"], 4 * step + k)
                if k == 0:
                    dve.tensor_copy(mprt[:, par, :, 0, :], m).then_inc(sm["split_step"], 1)
                elif k == 1:
                    dve.tensor_tensor(r, m, mprt[:, par, :, 0, :], ALU.subtract).then_inc(sm["split_step"], 1)
                elif k == 2:
                    dve.tensor_copy(mprt[:, par, :, 1, :], r).then_inc(sm["split_step"], 1)
                elif k == 3:
                    dve.tensor_tensor(r, r, mprt[:, par, :, 1, :], ALU.subtract).then_inc(sm["split_step"], 1)
                else:
                    dve.tensor_copy(mprt[:, par, :, 2, :], r).then_inc(sm["m_split"], 1)

            def o_inv(n):
                t7 = bank(7).rearrange("p (n c) -> p n c", c=VW)
                dve.wait_ge(sm["ot_ready"], n + 2)
                dve.reciprocal(orec[:, :].unsqueeze(2), t7[:, :, DH:DH + 1]).then_inc(sm["o_rec"], 1)

            def o_norm(n, ty, slot):
                t4d = bank(7).rearrange("p (q h c) -> p q h c", q=QT, c=VW)
                dve.wait_ge(sm["o_rec"], n + 1)
                dst = o_sb[:, ty, :, bass.ds(slot, 1), :].rearrange("p q o (h d) -> p q (o h) d", d=DH)
                inv = orec[:, :].rearrange("p (q h) -> p q h", q=QT).unsqueeze(3).broadcast_to([P, QT, G, DH])
                dve.tensor_tensor(dst, t4d[:, :, :, 0:DH], inv, ALU.mult).then_inc(sm["o_norm"], 1)

            def fold(k):
                i, n, bk = ((0, 3, 6), (3, 1, 7))[k // 3]
                src = bank(bk)[:, 0:n * (D + 4)].rearrange("p (i c) -> p i c", i=n)
                b = k % 3
                if k == 0:
                    dve.wait_ge(sm["fold_mm"], 1)
                if b < B:
                    dve.tensor_tensor(wop[:, b, i:i + n, 0:D], src[:, :, 0:D],
                                      gr[:, b:b + 1, 0:D].broadcast_to([P, n, D]), ALU.mult)
                else:
                    ins = dve.tensor_copy(wop[:, :, i:i + n, D:D + 4],
                                          src[:, :, D:D + 4].unsqueeze(1).broadcast_to([P, B, n, 4]))
                if k == 5:
                    ins.then_inc(sm["fold_sb"], 1)
                    dve.wait_ge(sm["fold_sb"], 1)
                    dve.memset(bank(6), 1.0).then_inc(sm["primed"], 1)

            for step in range(2):
                for r in range(4 * G):
                    row_max(step, r, step)
                    if step == 1 and r < 5:
                        split(0, 0, r)
                    if step == 0 and 8 <= r < 14:
                        fold(r - 8)

            def steps(it, last):
                for u in range(4):
                    n = 4 * it + u
                    ahead = not (last and u >= 2)
                    for kt in range(QT):
                        for r in range(4 * kt, 4 * kt + 4):
                            if ahead:
                                row_max(n + 2, r, u % 2)
                            if r < 5 and not (last and u == 3):
                                split(n + 1, (u + 1) % 2, r)
                            if r == 4:
                                o_inv(n)
                            if r == 5:
                                o_norm(n, (u + 1) % 2, 2 * it + (u + 1) // 2)
                            if last and u == 2 and r in T_AT:
                                t = T_AT.index(r)
                                dve.wait_ge(sm["oT"], t + 1)
                                dve.tensor_copy(oT_sb[:, t], bank(t % 2).rearrange("p (i c) -> p i c", i=4)) \
                                    .then_inc(sm["oT_sb"], 1)
                            if last and (u, r) in ((0, 11), (0, 15), (1, 3), (1, 7)):
                                c = NT * H // 4 * (2 * u + (r % 8 == 7 or r == 15))
                                dve.wait_ge(sm["loc_sum"], 1)
                                dve.reciprocal(lsm[:, :, c:c + NT * H // 4], lsm[:, :, c:c + NT * H // 4]) \
                                    .then_inc(sm["loc_inv"], 1)

            def gate_logits(k):
                g, g3 = gate[:, k], gate_3[:, k]
                b0, _, b3 = OUT_BANKS[k]
                dve.wait_ge(sm["p_mm"], 2 * (k + 1))
                first3 = ps[:, b0:b0 + 2, 0:3 * OW].rearrange("p j (i c) -> p j c i", i=3)
                fourth = bank(b3)[:, 0:2 * OW].rearrange("p (j c) -> p j c", j=2)
                dve.tensor_reduce(g, first3[:, :, D:OW, :], AX.X, ALU.add)
                link(dve.tensor_tensor(g3, fourth[:, :, D:OW], rw[:, R_FB:R_FB + 4].unsqueeze(1).broadcast_to([P, 2, 4]),
                                       ALU.add))
                link(dve.tensor_tensor(g, g, g3, ALU.add))
                link(dve.tensor_reduce(gate_r[:, k, 0], g, AX.X, ALU.max))
                dve.tensor_tensor(g, g, gate_r[:, k, 0].unsqueeze(2).broadcast_to([P, 2, 4]), ALU.subtract) \
                    .then_inc(sm["logits"], 1)

            def x1_pair(k):
                g = gate[:, k]
                dve.wait_ge(sm["gate_exp"], k + 1)
                link(dve.tensor_reduce(gate_r[:, k, 1], g, AX.X, ALU.add))
                link(dve.reciprocal(gate_r[:, k, 1], gate_r[:, k, 1]))
                link(dve.tensor_tensor(g, g, gate_r[:, k, 1].unsqueeze(2).broadcast_to([P, 2, 4]), ALU.mult))
                for m in range(8):
                    j, i = m % 2, m // 2
                    t = 2 * k + j
                    if m >= 2:
                        dve.wait_ge(sm["x1_step"], 8 * k + m - 1)
                    src = bank(OUT_BANKS[k][j])[:, OW * i:OW * i + D] if i < 3 else \
                        bank(OUT_BANKS[k][2])[:, OW * j:OW * j + D]
                    dve.scalar_tensor_tensor(x_sb[:, t, :], src, g[:, j, i:i + 1], x_sb[:, t, :], ALU.mult, ALU.add) \
                        .then_inc(sm["x1_step"], 1)

            def norm_stats(k, b, src, ready, done=0):
                for t in range(done, QT):
                    ins = dve.bn_stats(bst[:, QT * b + t, :], src[:, t, :])
                link(ins)
                for t in range(QT):
                    ins = dve.bn_aggr(mv[:, k, QT * b + t, :], bst[:, QT * b + t, :])
                ins.then_inc(ready, 1)

            def xhat(k, b, src, var, inv, ready):
                dve.wait_ge(inv, b + 1)
                dve.wait_ge(var, b + 1)
                for t in range(QT):
                    normalise(k, QT * b + t, xh[:, QT * b + t, :], src[:, t, :]).then_inc(ready, 1)

            def tiles(b):
                return x_sb[:, QT * b:QT * (b + 1), :]

            def early_stats2(b):
                dve.wait_ge(sm["x1_step"], 16 * b + 8)
                for t in range(2):
                    dve.bn_stats(bst[:, QT * b + t, :], tiles(b)[:, t, :])

            def stats2(b):
                dve.wait_ge(sm["x1_step"], 16 * (b + 1))
                norm_stats(1, b, tiles(b), sm["var2"], done=2)

            def xh2(b):
                xhat(1, b, tiles(b), sm["var2"], sm["rstd2"], sm["xh2_ready"])

            with dve.Fori(0, LOOPED) as it:
                steps(it, False)
            l5 = ls[:, :].rearrange("p (n c) -> p n c", n=5)
            dve.wait_ge(sm["loc_scores"], 1)
            link(dve.tensor_tensor(lsm[:, :, :], l5[:, 0:4:3, :], l5[:, 1:5:3, :], ALU.max))
            dve.tensor_tensor(lsm[:, 0, :], lsm[:, 0, :], l5[:, 2, :], ALU.max).then_inc(sm["loc_max"], 1)
            steps(LOOPED, True)

            def ffn(b, f):
                n = FT * b + f
                dve.wait_ge(sm["h_tanh"], n + 1)
                dve.scalar_tensor_tensor(hv[:, n % 2], th[:, n % 2], 1.0, bank(2 + 2 * (n % 2)), ALU.add, ALU.mult) \
                    .then_inc(sm["h_v"], 1)
                dve.wait_ge(sm["h_v"], n + 1)
                dve.wait_ge(sm["h_mm"], 2 * n + 2)
                dve.tensor_tensor(u_sb[:, f, b, :], hv[:, n % 2], bank(3 + 2 * (n % 2)), ALU.mult).then_inc(sm["u_ready"], 1)

            def x2(b):
                dve.wait_ge(sm["y_mm"], b + 1)
                hb = xh[:, QT * b:QT * (b + 1), :]
                link(dve.tensor_tensor(hb, bank(6).rearrange("p (t d) -> p t d", t=QT),
                                       gr[:, b:b + 1, D:2 * D].broadcast_to([P, QT, D]), ALU.mult))
                dve.tensor_tensor(tiles(b), tiles(b), hb, ALU.add).then_inc(sm["x2_done"], 1)
                dve.wait_ge(sm["x2_done"], b + 1)
                norm_stats(2, b, tiles(b), sm["var3"])

            def xh3(b):
                xhat(2, b, tiles(b), sm["var3"], sm["rstd3"], sm["xh3_ready"])

            def k_max(b):
                k = ksm[:, b, :]
                dve.wait_ge(sm["k_mm"], b + 1)
                link(dve.tensor_reduce(k[:, 0:1], bank(LAST[b][2]), AX.X, ALU.max))
                link(dve.tensor_tensor(k[:, 1:2], k[:, 0:1], pa[:, C_BK:C_BK + 1], ALU.add))
                dve.tensor_tensor(k[:, 2:3], pa[:, C_BK:C_BK + 1], k[:, 1:2], ALU.subtract).then_inc(sm["k_max"], 1)

            def heads(b):
                return q_sb[:, QT * b:QT * (b + 1), :].rearrange("p t (h d) -> p (t h) d", d=DH)

            def q_max(b):
                dve.wait_ge(sm["qv_mm"], b + 1)
                x0 = LAST[b][0]
                qv = ps[:, x0:x0 + 2, :].rearrange("p n (t c) -> p (n t) c", t=2)
                link(dve.tensor_tensor(q_sb[:, QT * b:QT * (b + 1), :], qv[:, :, 0:D],
                                       rw[:, R_BQ:R_BQ + P].unsqueeze(1).broadcast_to([P, QT, D]), ALU.add))
                link(dve.tensor_reduce(qmx[:, b, :], heads(b), AX.X, ALU.max))
                dve.tensor_tensor(heads(b), heads(b), qmx[:, b, :].unsqueeze(2).broadcast_to([P, QT * H, DH]), ALU.subtract) \
                    .then_inc(sm["q_max"], 1)
                dve.tensor_tensor(v_sb[:, QT * b:QT * (b + 1), :], qv[:, :, D:2 * D],
                                  rw[:, R_BV:R_BV + P].unsqueeze(1).broadcast_to([P, QT, D]), ALU.add) \
                    .then_inc(sm["qv_ready"], 1)

            def q_sums(b):
                dve.wait_ge(sm["q_exp"], b + 1)
                link(dve.tensor_reduce(qsm[:, b, :], heads(b), AX.X, ALU.add))
                link(dve.reciprocal(qsm[:, b, :], qsm[:, b, :]))

            def context(b):
                dve.wait_ge(sm["k_exp"], b + 1)
                link(dve.reciprocal(ksm[:, b, 4:5], ksm[:, b, 3:4]))
                dve.wait_ge(sm["ctx_mm"], b + 1)
                dve.scalar_tensor_tensor(ctx_sb[:, b, :], bank(LAST[b][1])[:, 0:D], ksm[:, b, 4:5], hmask,
                                         ALU.mult, ALU.mult).then_inc(sm["ctx_sb"], 1)

            def stats4(b):
                dve.wait_ge(sm["yl_mm"], b + 1)
                yb = xh[:, QT * b:QT * (b + 1), :]
                link(dve.tensor_tensor(yb.rearrange("p t (h d) -> p (t h) d", d=DH),
                                       bank(LAST[b][2]).rearrange("p (g d) -> p g d", d=DH),
                                       qsm[:, b, :].unsqueeze(2).broadcast_to([P, QT * H, DH]), ALU.mult))
                norm_stats(3, b, yb, sm["var4"])

            def xh4(b):
                xhat(3, b, xh[:, QT * b:QT * (b + 1), :], sm["var4"], sm["rstd4"], sm["xh4_ready"])

            def silu4(b):
                dve.wait_ge(sm["h4_tanh"], b + 1)
                dve.scalar_tensor_tensor(t4[:, b, :], t4[:, b, :], 1.0, hT[:, b, :], ALU.add, ALU.mult) \
                    .then_inc(sm["u4"], 1)

            def result(b):
                dve.wait_ge(sm["gb_ready"], b + 1)
                for half in range(2):
                    t = slice(QT * b + 2 * half, QT * b + 2 * half + 2)
                    dve.wait_ge(sm["z_mm"], 2 * b + half + 1)
                    z = bank(LAST[b][1 - half])[:, 0:2 * D].rearrange("p (t d) -> p t d", t=2)
                    ins = dve.tensor_tensor(xh[:, t, :], z, cgh[:, b:b + 1, :].broadcast_to([P, 2, D]), ALU.mult)
                link(ins)
                for half in range(2):
                    t = slice(QT * b + 2 * half, QT * b + 2 * half + 2)
                    dve.tensor_tensor(x_sb[:, t, :], xh[:, t, :], xgb[:, t, :], ALU.add).then_inc(sm["o_ready"], 1)

            gate_logits(0)
            x1_pair(0)
            gate_logits(1)
            o_inv(STEPS)
            o_norm(STEPS, 1, B * NG)
            early_stats2(0)
            x1_pair(1)
            stats2(0)
            xh2(0)
            gate_logits(2)
            x1_pair(2)
            early_stats2(1)
            ffn(0, 0)
            ffn(0, 1)
            gate_logits(3)
            x1_pair(3)
            ffn(0, 2)
            stats2(1)
            ffn(0, 3)
            xh2(1)
            x2(0)
            ffn(1, 0)
            ffn(1, 1)
            xh3(0)
            ffn(1, 2)
            ffn(1, 3)
            k_max(0)
            q_max(0)
            x2(1)
            context(0)
            xh3(1)
            q_sums(0)
            stats4(0)
            k_max(1)
            xh4(0)
            q_max(1)
            silu4(0)
            context(1)
            q_sums(1)
            stats4(1)
            result(0)
            xh4(1)
            silu4(1)
            result(1)

        @block.tensor
        def _(pe):
            pe.sem_inc(sm["ot_ready"], 1)
            pe.sem_inc(sm["a_free"], 2)
            pe.wait_ge(sm["warm_in"], 1)
            for _ in range(WARM):
                ins = pe.matmul(bank(0), parts_mem[:, 0, 0, 0, 0:P], parts_mem[:, 0, 0, 0, :], start=True, stop=True)
            ins.then_inc(sm["warmed"], 1)
            pe.wait_ge(sm["pa_in"], 16)
            pe.wait_ge(sm["silb_ready"], 1)
            for j in range(6):
                ins = pe.matmul(bank(2)[:, 2 * j:2 * j + 2], pa[:, A_W + P * j:A_W + P * (j + 1)], sil[:, 2, :],
                                start=True, stop=True)
            ins.then_inc(sm["ada_mm"], 1)

            def transposes(bk, src, dst, ready, base):
                for t in range(QT):
                    pe.wait_ge(ready, base + t + 1)
                    ins = pe.transpose(bank(bk)[:, P * t:P * (t + 1)], src[:, base + t, :], ident)
                ins.then_inc(dst, 1)

            for b in range(B):
                transposes(b, xh1, sm["xT1"], sm["xh1_ready"], QT * b)
            for b in range(B):
                ins = pe.matmul(bank(3)[:, 256 * b:256 * (b + 1)], silb[:, b, :], pa[:, A_GW:A_GW + 256],
                                start=True, stop=True)
            ins.then_inc(sm["gr_mm"], 1)

            def qk_product(i):
                b, n = i // 4, i % 4
                pe.wait_ge(sm["nx_ready"], b + 1)
                if i >= 4:
                    pe.wait_ge(sm["resid1"], i - 3)
                pe.matmul(bank(4 + n), wb[:, P * n:P * (n + 1)], nxb[:, b, :], start=True, stop=True).then_inc(sm["qk_mm"], 1)

            def token_product(j, halves=(0, 1)):
                dst = bank(2 + j % 4)
                if halves[0] == 0:
                    if j == 0:
                        pe.wait_ge(sm["ga_ready"], 1)
                    elif j == 1:
                        pe.wait_ge(sm["gr_ready"], 1)
                    elif j < 4:
                        pe.wait_ge(sm["resid1"], 3 + j)
                    else:
                        done = j - 3
                        pe.wait_ge(sm["tok_act"], 2 * min(done, NT) + max(done - NT, 0))
                b, q = j % NT // QT, j % QT
                side, c = (nxb, 512 * (1 + j // NT)) if j < 2 * NT else (nxs, 1280)
                for half in halves:
                    ins = pe.matmul(dst[:, 256 * half:256 * (half + 1)], side[:, b, P * q:P * (q + 1)],
                                    wb[:, c + 256 * half:c + 256 * (half + 1)], start=True, stop=True)
                if halves[-1] == 1 or j >= 2 * NT:
                    ins.then_inc(sm["tok_mm"], 1)

            def token_unit(k):
                if k < 24:
                    token_product(4 + k // 2, (k % 2,))
                else:
                    token_product(k - 8, (0,))

            pe.wait_ge(sm["wqk_in"], 16)
            for i in range(6):
                qk_product(i)
            pe.wait_ge(sm["wb_in"], 16)
            for j in range(2):
                token_product(j)
                qk_product(6 + j)
            for j in range(2, 4):
                token_product(j)

            def wo_transposes():
                pe.wait_ge(sm["wo_in"], 16)
                for i in range(4):
                    ins = pe.transpose(bank(7)[:, P * i:P * (i + 1)], wc[:, W_WO + P * i:W_WO + P * (i + 1)], ident)
                ins.then_inc(sm["woT"], 1)

            def fold():
                pe.wait_ge(sm["woT_sb"], 1)
                for i in range(4):
                    dst = bank(6 + i // 3)[:, (D + 4) * (i % 3):(D + 4) * (i % 3 + 1)]
                    pe.matmul(dst[:, 0:D], woT_sb[:, i, :], wc[:, W_FWO:W_FWO + D], start=True, stop=True)
                    ins = pe.matmul(dst[:, D:D + 4], woT_sb[:, i, :], wc[:, W_FWG + 4 * i:W_FWG + 4 * (i + 1)],
                                    start=True, stop=True)
                ins.then_inc(sm["fold_mm"], 1)

            def score(u, r, step):
                h, q = r // QT, r % QT
                dst = bank(r % 2)
                if step is not None:
                    pe.wait_ge(sm["s_max"], 16 * step + r - 1)
                ins = pe.matmul(dst, stk[:, u, 1, h, P * q:P * (q + 1)], stk[:, u, 0, h, :], start=True, stop=u % 2 == 1)
                if u % 2 == 0:
                    ins = pe.matmul(dst[:, P * q:P * (q + 1)], ident_b, diag_b, start=False, stop=True)
                ins.then_inc(sm["s_ready"], 1)

            def score_t(u, kt, h, step):
                if h % 2 == 0:
                    pe.wait_ge(sm["st_free"], 8 * step + 2 * kt + h // 2 + 1)
                dst = bank(2 + h)
                ins = pe.matmul(dst, stk[:, u, 0, h, P * kt:P * (kt + 1)], stk[:, u, 1, h, :], start=True, stop=u % 2 == 1)
                if u % 2 == 0:
                    ins = pe.matmul(dst[:, P * kt:P * (kt + 1)], ident_b, diag_b, start=False, stop=True)
                if h % 2 == 1:
                    ins.then_inc(sm["st_ready"], 1)

            def weighted(u, kt, step, half):
                if half == 0:
                    pe.wait_ge(sm["st_free"], 2 + 8 * step + 2 * kt + 2)
                    if kt == 0:
                        pe.wait_ge(sm["o_evac"], step + 1)
                q = slice(S // 2 * half, S // 2 * (half + 1))
                for h in range(G):
                    ins = pe.matmul(bank(6)[VW * h:VW * (h + 1), q], vb[:, u, kt, h, :],
                                    a_buf[:, kt % 2, h, q], start=kt == 0 and half == 0, stop=kt == QT - 1 and half == 1)
                if half == 1:
                    ins.then_inc(sm["a_free"], 1)

            def o_back(n):
                pe.wait_ge(sm["mt_evac"], n + 1)
                pe.wait_ge(sm["o_evac"], n + 1)
                for q in range(QT):
                    ins = pe.transpose(bank(7)[:, P * q:P * (q + 1)], oev[:, P * q:P * (q + 1)], ident)
                ins.then_inc(sm["ot_ready"], 1)

            def max_t(step, par, normed):
                pe.wait_ge(sm["m_split"], step + 1)
                if normed is not None:
                    pe.wait_ge(sm["o_norm"], normed)
                for q in range(QT):
                    ins = pe.transpose(bank(7)[0:3 * G, P // 2 * q:P // 2 * (q + 1)].bitcast(BF16),
                                       mprt[:, par, q].rearrange("p c h -> p (c h)"), ident_b)
                ins.then_inc(sm["mt_ready"], 1)

            pe.wait_ge(sm["cst_in"], 48)
            pe.wait_ge(sm["nxs_ready"], 2)
            pe.wait_ge(sm["gr_ready"], 1)
            for step in range(2):
                pe.wait_ge(load_done[step], LOADS)
                for r in range(4 * G):
                    score(step, r, step if 16 * step + r >= 2 else None)
                    token_unit(16 * step + r)
                    if step == 0 and r == 3:
                        wo_transposes()
                    if step == 0 and r == 7:
                        fold()
                    if step == 1 and r == 8:
                        pe.wait_ge(sm["fold_sb"], 1)
                        max_t(0, 0, None)
            pe.wait_ge(m_done[0], 16)
            pe.wait_ge(sm["tok_act"], 4 * NT)
            for h in range(G):
                score_t(0, 0, h, 0)

            def out_t(t):
                b, q = t // QT, t % QT
                if t == 0:
                    pe.wait_ge(sm["loc_out"], 1)
                    pe.wait_ge(sm["s_max"], 16 * STEPS)
                elif t == QT:
                    pe.wait_ge(sm["o_norm"], STEPS + 1)
                elif t not in (1, QT + 1):
                    pe.wait_ge(sm["oT_sb"], t - 1)

                def tile(ty):
                    first = b * NG + 1
                    return o_sb[:, ty, q, first:first + NG, :].rearrange("p g c -> p (g c)")
                srcs = [tile(0), o_loc[:, 0, t, :], o_loc[:, 1, t, :], tile(1)]
                for i, src in enumerate(srcs):
                    ins = pe.transpose(bank((t % 2, 5 + t % 2 * 2)[b])[:, P * i:P * (i + 1)], src, ident)
                ins.then_inc(sm["oT"], 1)

            def out_product(t):
                k, j = t // 2, t % 2
                pe.wait_ge(sm["oT_sb"], (QT, QT, NT, NT)[k])
                if k == 0:
                    pe.wait_ge(sm["o_norm"], STEPS)
                elif k >= 2:
                    pe.wait_ge(sm["x1_step"], 8 if k == 2 else 24)
                    pe.wait_ge(sm["o_evac"], STEPS + 1)
                for i in range(4):
                    bk, c = (OUT_BANKS[k][j], OW * i) if i < 3 else (OUT_BANKS[k][2], OW * j)
                    ins = pe.matmul(bank(bk)[:, c:c + OW], oT_sb[:, t % QT, i, :], wop[:, t // QT, i, :],
                                    start=True, stop=True)
                ins.then_inc(sm["p_mm"], 1)

            def steps(it, last):
                for u in range(4):
                    n = 4 * it + u
                    ahead = not (last and u >= 2)
                    w = (u + 2) % 4
                    for kt in range(QT):
                        if kt == 0 and ahead:
                            pe.wait_ge(load_done[w], LOADS * (it + 1 + (u >= 2)))
                        more = not (last and u == 3 and kt == 3)
                        if kt == 3 and more:
                            pe.wait_ge(m_done[(u + 1) % 4], 16 * (it + 1 + (u == 3)))

                        def st(h):
                            if more and kt < 3:
                                score_t(u, kt + 1, h, n)
                            elif more:
                                score_t((u + 1) % 4, 0, h, n + 1)

                        def s(i):
                            if ahead:
                                score(w, 4 * kt + i, n + 2)
                            elif u == 2 and 4 * kt + i in T_AT:
                                out_t(T_AT.index(4 * kt + i))
                            elif u == 3 and 4 * kt + i in O_AT:
                                out_product(O_AT.index(4 * kt + i))

                        s(0)
                        st(0)
                        st(1)
                        s(1)
                        if kt == 0:
                            pe.wait_ge(v_done[u], it + 1)
                        weighted(u, kt, n, 0)
                        s(2)
                        st(2)
                        st(3)
                        s(3)
                        if kt == 1 and not (last and u == 3):
                            max_t(n + 1, (u + 1) % 2, n + 1)
                        weighted(u, kt, n, 1)
                        if kt == 0:
                            o_back(n)

            with pe.Fori(0, LOOPED) as it:
                steps(it, False)
            steps(LOOPED, True)

            def h_products(b, f):
                n = FT * b + f
                pe.wait_ge(sm["nx2"], b + 1)
                if n >= 2:
                    pe.wait_ge(sm["u_ready"], n - 1)
                for k, w in enumerate((W_W1, W_W3)):
                    pe.matmul(bank(2 + 2 * (n % 2) + k), wc[:, w + P * f:w + P * (f + 1)], nT[:, b, :],
                              start=True, stop=True).then_inc(sm["h_mm"], 1)

            def ffn_out(b, f):
                pe.wait_ge(sm["u_ready"], FT * b + f + 1)
                if b > 0 and f == 0:
                    pe.wait_ge(sm["x2_done"], b)
                for t in range(QT):
                    ins = pe.matmul(bank(6)[:, P * t:P * (t + 1)], u_sb[:, f, b, P * t:P * (t + 1)],
                                    wc[:, W_W2 + P * f:W_W2 + P * (f + 1)], start=f == 0 and t == 0,
                                    stop=f == FT - 1 and t == QT - 1)
                if f == FT - 1:
                    ins.then_inc(sm["y_mm"], 1)

            def kqv(b):
                x0, x1, x2 = LAST[b]
                pe.wait_ge(sm["nx3"], b + 1)
                pe.wait_ge(sm["nx2"], B)
                pe.matmul(bank(x2), wc[:, W_K:W_K + D], nT[:, b, :], start=True, stop=True).then_inc(sm["k_mm"], 1)
                for t in range(QT):
                    ins = pe.matmul(ps[:, x0 + t // 2, 256 * (t % 2):256 * (t % 2 + 1)], nT[:, b, P * t:P * (t + 1)],
                                    wc[:, W_QV:W_QV + 256], start=True, stop=True)
                ins.then_inc(sm["qv_mm"], 1)

            def k_back(b):
                pe.wait_ge(sm["k_exp"], b + 1)
                for t in range(QT):
                    ins = pe.transpose(bank(LAST[b][2])[:, P * t:P * (t + 1)], kx[:, b, P * t:P * (t + 1)], ident)
                ins.then_inc(sm["kt_mm"], 1)

            def q_back(b):
                pe.wait_ge(sm["q_exp"], b + 1)
                pe.wait_ge(sm["qv_ready"], b + 1)
                for t in range(QT):
                    ins = pe.transpose(bank(LAST[b][0])[:, P * t:P * (t + 1)], q_sb[:, QT * b + t, :], ident)
                ins.then_inc(sm["qT"], 1)

            def context(b):
                pe.wait_ge(sm["kt_sb"], b + 1)
                pe.wait_ge(sm["qv_ready"], b + 1)
                for t in range(QT):
                    ins = pe.matmul(bank(LAST[b][1])[:, 0:D], kt_sb[:, QT * b + t, :], v_sb[:, QT * b + t, :],
                                    start=t == 0, stop=t == QT - 1)
                ins.then_inc(sm["ctx_mm"], 1)

            def linear_out(b):
                pe.wait_ge(sm["ctx_sb"], b + 1)
                pe.wait_ge(sm["qT_sb"], b + 1)
                for t in range(QT):
                    ins = pe.matmul(bank(LAST[b][2])[:, P * t:P * (t + 1)], qT_sb[:, b, P * t:P * (t + 1)], ctx_sb[:, b, :],
                                    start=True, stop=True)
                ins.then_inc(sm["yl_mm"], 1)

            def last_product(b):
                pe.wait_ge(sm["u4"], b + 1)
                for half in range(2):
                    for j in range(2):
                        t = 2 * half + j
                        ins = pe.matmul(bank(LAST[b][1 - half])[:, P * j:P * (j + 1)], t4[:, b, P * t:P * (t + 1)],
                                        wc[:, W_OUT:W_OUT + D], start=True, stop=True)
                    ins.then_inc(sm["z_mm"], 1)

            def xT2(b):
                pe.wait_ge(sm["oT_sb"], NT)
                transposes((5, 0)[b], xh, sm["xT2"], sm["xh2_ready"], QT * b)

            def xT3(b):
                transposes(LAST[b][0], xh, sm["xT3"], sm["xh3_ready"], QT * b)

            def xT4(b):
                transposes(LAST[b][0], xh, sm["xT4"], sm["xh4_ready"], QT * b)

            def keep_warm(bk, n):
                for _ in range(n):
                    pe.matmul(bank(bk)[:, 0:2 * P], ident_b, cb[:, :], start=True, stop=True)

            pe.wait_ge(sm["wc_in"], 16)
            for t in range(2, QT):
                out_product(t)
            pe.wait_ge(sm["x1_step"], 8)
            pe.wait_ge(sm["o_evac"], STEPS + 1)
            for q in range(QT):
                ins = pe.transpose(bank(7)[:, P * q:P * (q + 1)], oev[:, P * q:P * (q + 1)], ident)
            ins.then_inc(sm["ot_ready"], 1)
            for t in range(QT, NT):
                out_t(t)
            pe.wait_ge(sm["oT_sb"], NT)
            keep_warm(5, 8)
            out_product(4)
            out_product(5)
            keep_warm(5, 4)
            xT2(0)
            keep_warm(7, 8)
            h_products(0, 0)
            h_products(0, 1)
            out_product(6)
            out_product(7)
            h_products(0, 2)
            ffn_out(0, 0)
            h_products(0, 3)
            ffn_out(0, 1)
            ffn_out(0, 2)
            keep_warm(7, 8)
            ffn_out(0, 3)
            xT2(1)
            keep_warm(7, 8)
            h_products(1, 0)
            h_products(1, 1)
            keep_warm(7, 4)
            ffn_out(1, 0)
            xT3(0)
            h_products(1, 2)
            h_products(1, 3)
            kqv(0)
            ffn_out(1, 1)
            k_back(0)
            ffn_out(1, 2)
            ffn_out(1, 3)
            q_back(0)
            context(0)
            keep_warm(5, 8)
            linear_out(0)
            xT3(1)
            keep_warm(5, 6)
            kqv(1)
            k_back(1)
            xT4(0)
            keep_warm(5, 16)
            context(1)
            q_back(1)
            last_product(0)
            linear_out(1)
            keep_warm(5, 32)
            xT4(1)
            keep_warm(5, 18)
            last_product(1)


def _constants():
    import numpy as np
    bf = mybir.dt.np(BF16)
    tok = np.arange(S)
    tile, at = tok // P, tok % P
    kside = np.zeros((MROW - DATA, S), np.float32)
    qside = np.zeros((MROW - DATA, S), np.float32)
    for t in range(QT):
        s = np.sign(tile - t).astype(np.float32)
        kside[3 * t] = -s * P * (tile - t)
        kside[3 * t + 1] = -s * at
        kside[3 * t + 2] = s
        qside[3 * t] = tile == t
        qside[3 * t + 1] = tile == t
        qside[3 * t + 2] = (tile == t) * at
    stk_c = np.zeros((MROW - DATA, 4, 2, G, S), np.float32)
    for u in (0, 2):
        stk_c[:, u, 0] = kside[:, None, :]
        stk_c[:, u, 1] = qside[:, None, :]
    stk_o = np.zeros((3, G, 4, 2, G, S), np.float32)
    for h in range(G):
        stk_o[:, h, :, 0, h] = 1.0
    i = np.arange(P)
    diag = -np.abs(i[:, None] - i[None, :]).astype(np.float32)
    cst_bf = np.concatenate([np.eye(P, dtype=np.float32), diag], 1)
    hmask = (i[:, None] // DH == i[None, :] // DH).astype(np.float32)
    lmask = np.zeros((P, 3, NT), np.float32)
    for t in range(NT):
        if t % QT == 0:
            lmask[0, 0, t] = -1e9
        if t % QT == QT - 1:
            lmask[P - 1, 2, t] = -1e9
    return (np.eye(P, dtype=np.float32), hmask, lmask.reshape(P, 3 * NT), cst_bf.astype(bf),
            stk_c.reshape(MROW - DATA, -1).astype(bf), stk_o.reshape(3 * G, -1).astype(bf))


def kernel(**inputs):
    import numpy as np
    import concourse.bacc as bacc
    from concourse.bass_utils import run_bass_kernel_spmd as run

    a = {k: np.asarray(v) for k, v in inputs.items()}
    l0 = {k[8:]: v for k, v in a.items() if k.startswith("L0_cond_")}
    l1 = {k[8:]: v for k, v in a.items() if k.startswith("L1_cond_")}
    eye, hmask, lmask, cst_bf, stk_c, stk_o = _constants()

    def block(w, j):
        return w[..., P * j:P * (j + 1)]

    aw, ab, ew, eb = l0["ada_w"], l0["ada_b"], l1["emb_W"], l1["emb_b"]
    cond = a["cond_1024"]
    cols = np.stack([l0["ln1_g"], l0["ln2_g"], l1["sn_g"], l0["ln1_b"], l0["ln2_b"], l1["sn_b"], l1["norm_g"], l1["norm_b"],
                     l1["bk"], cond[0], cond[1], block(ab, 1), block(ab, 4), block(eb, 0), block(ab, 0), block(ab, 3),
                     block(eb, 1)], 1)
    pk_a = np.concatenate([cols, block(aw, 1), block(aw, 4), block(ew, 0), block(aw, 0), block(aw, 3), block(ew, 1),
                           block(aw, 2), block(aw, 5), eye, hmask, lmask], 1)
    pk_b = np.concatenate([l0["grid_wk"], l0["grid_wq"], l0["sem_wk"], l0["sem_wq"],
                           l0["reg_wq"], l0["ent_wq"], l0["grid_wv"], l0["sem_wv"],
                           l0["reg_wk"], l0["reg_wv"], l0["ent_wk"], l0["ent_wv"]], 1)
    fwg = l0["fus_wg"].reshape(4, P, 4).transpose(1, 0, 2).reshape(P, 16)
    w2 = l0["ffn_w2"].reshape(FT, P, D).transpose(1, 0, 2).reshape(P, FT * D)
    pk_c = np.concatenate([l0["grid_wo"], l0["reg_wo"], l0["ent_wo"], l0["sem_wo"], l0["fus_wo"], fwg,
                           l0["ffn_w1"], l0["ffn_w3"], w2, l1["Wq"], l1["Wv"], l1["Wk"], l1["out_W"]], 1)
    row = np.concatenate([block(ab, 2), block(ab, 5), l1["bq"], l1["bv"], l1["out_b"], cond[0], cond[1], l0["fus_bg"]])
    arrays = {"x": a["x"], "pk_a": pk_a, "pk_b": pk_b, "pk_c": pk_c, "rows": np.broadcast_to(row, (P, R_END)),
              "cst_bf": cst_bf, "stk_c": stk_c, "stk_o": stk_o}
    arrays = {k: np.ascontiguousarray(v) for k, v in arrays.items()}
    nc = bacc.Bacc("TRN2", target_bir_lowering=False, num_devices=1)
    args = [nc.dram_tensor(k, v.shape, mybir.dt.from_np(v.dtype), kind="ExternalInput").ap() for k, v in arrays.items()]
    args.append(nc.dram_tensor("out", (B, S, D), F32, kind="ExternalOutput").ap())
    program(nc, *args)
    r = run(nc, [arrays], core_ids=[0])
    return r.results[0]["out"]
```
